# Optimizing a Trainium2 kernel written in Bass

```python
import numpy as np
import jax
import jax.numpy as jnp

def _softmax(x, axis=-1):
    return jax.nn.softmax(x, axis=axis)

def _gelu(x):
    return jax.nn.gelu(x, approximate=True)

def _silu(x):
    return jax.nn.silu(x)

def _sigmoid(x):
    return jax.nn.sigmoid(x)

def _layernorm(x, axis=-1, eps=1e-05):
    m = jnp.mean(x, axis=axis, keepdims=True)
    v = jnp.var(x, axis=axis, keepdims=True)
    return (x - m) / jnp.sqrt(v + eps)

def _scatter_add(tgt, idx, src, axis=0):
    return tgt.at[idx].add(src)

def _segment_sum(src, seg, n):
    return jax.ops.segment_sum(src, seg, n)
kernel_name = 'mk_adj_ffn_d4_adj_r2_f04b1a'

def setup_inputs(seed: int=0):
    np.random.seed(seed)
    _w = jnp.asarray

    def _rec_inputs():
        import jax
        import jax.numpy as jnp
        _gk = jax.random.key(seed)
        x = -0.000929 + 1 * jax.random.normal(jax.random.fold_in(_gk, 1), (16, 512, 128), jnp.float32)
        _a = jax.random.bernoulli(jax.random.fold_in(_gk, 2), 0.0078125, (16, 512, 512))
        _a = jnp.logical_or(_a, jnp.swapaxes(_a, -1, -2))
        _a = jnp.logical_or(_a, jnp.eye(512, dtype=bool))
        adj = _a.astype(jnp.int32)
        return (x, adj)
    x, adj = _rec_inputs()

    def _L0_gnn_setup():
        import math
        import jax, jax.numpy as jnp
        import numpy as np
        B, N, E, H = (1, 2048, 128, 8)
        D = E // H
        key = jax.random.key(seed)
        ks = jax.random.split(key, 10)
        s = 1.0 / math.sqrt(E)
        return {'x': jax.random.normal(ks[0], (B, N, E), dtype=jnp.float32), 'adjacency': jax.random.randint(ks[1], (B, N, N), 0, 2, dtype=jnp.int32), 'Wq': jax.random.normal(ks[2], (E, E), dtype=jnp.float32) * s, 'bq': jnp.zeros((E,), dtype=jnp.float32), 'Wk': jax.random.normal(ks[3], (E, E), dtype=jnp.float32) * s, 'bk': jnp.zeros((E,), dtype=jnp.float32), 'Wv': jax.random.normal(ks[4], (E, E), dtype=jnp.float32) * s, 'bv': jnp.zeros((E,), dtype=jnp.float32), 'Wo': jax.random.normal(ks[5], (E, E), dtype=jnp.float32) * s, 'bo': jnp.zeros((E,), dtype=jnp.float32)}
    _L0_gnn_all = _L0_gnn_setup()
    _L0_gnn_in = {k: v for k, v in _L0_gnn_all.items() if k in ('Wq', 'bq', 'Wk', 'bk', 'Wv', 'bv', 'Wo', 'bo')}
    del _L0_gnn_all

    def _L0_ffn_setup():
        import jax, jax.numpy as jnp
        import numpy as np
        B, T, D, H, L = (16, 2048, 128, 128, 2)

        def _lstm(x, W_ih, W_hh, b_ih, b_hh):
            x_proj = jnp.einsum('btd,gd->btg', x, W_ih) + b_ih + b_hh
            h0 = jnp.zeros((x.shape[0], W_hh.shape[1]), x.dtype)
            c0 = jnp.zeros_like(h0)

            def step(carry, xp):
                h, c = carry
                gates = xp + h @ W_hh.T
                i, f, g, o = jnp.split(gates, 4, axis=-1)
                c = jax.nn.sigmoid(f) * c + jax.nn.sigmoid(i) * jnp.tanh(g)
                h = jax.nn.sigmoid(o) * jnp.tanh(c)
                return ((h, c), h)
            _, hs = jax.lax.scan(step, (h0, c0), jnp.swapaxes(x_proj, 0, 1))
            return jnp.swapaxes(hs, 0, 1)
        key = jax.random.key(seed)
        ks = jax.random.split(key, 9)
        s = 1.0 / np.sqrt(H)
        u = lambda k, shape: jax.random.uniform(k, shape, jnp.float32, -s, s)
        return {'x': jax.random.normal(ks[0], (B, T, D), jnp.float32), 'W_ih': u(ks[1], (4 * H, D)), 'W_hh': u(ks[2], (4 * H, H)), 'b_ih': u(ks[3], (4 * H,)), 'b_hh': u(ks[4], (4 * H,)), 'W_lin': u(ks[5], (L, H)), 'b_lin': u(ks[6], (L,)), 'fw_att': jnp.full((1, H), 0.001, jnp.float32), 'bw_att': jnp.full((1, H), 0.001, jnp.float32)}
    _L0_ffn_all = _L0_ffn_setup()
    _L0_ffn_in = {k: v for k, v in _L0_ffn_all.items() if k in ('W_ih', 'W_hh', 'b_ih', 'b_hh', 'W_lin', 'b_lin', 'fw_att', 'bw_att')}
    del _L0_ffn_all

    def _L1_gnn_setup():
        import jax, jax.numpy as jnp
        import numpy as np
        DIM = 128
        HEADS = 8
        HEAD_DIM = DIM // HEADS
        DFF = 4 * DIM
        EPS = 1e-05

        def _layernorm(x, g, b):
            m = jnp.mean(x, axis=-1, keepdims=True)
            v = jnp.mean(jnp.square(x - m), axis=-1, keepdims=True)
            return (x - m) * jax.lax.rsqrt(v + EPS) * g + b
        key = jax.random.key(seed)
        ks = jax.random.split(key, 12)
        B, N = (8, 512)
        s = 1.0 / np.sqrt(DIM)
        x = jax.random.normal(ks[0], (B, N, DIM), dtype=jnp.float32)
        adj = jax.random.randint(ks[1], (B, N, N), 0, 2, dtype=jnp.int32)
        return {'x': x, 'adj': adj, 'Wqkv': jax.random.normal(ks[2], (3 * DIM, DIM), jnp.float32) * s, 'bqkv': jnp.zeros((3 * DIM,), jnp.float32), 'Wo': jax.random.normal(ks[3], (DIM, DIM), jnp.float32) * s, 'bo': jnp.zeros((DIM,), jnp.float32), 'ln1_g': jnp.ones((DIM,), jnp.float32), 'ln1_b': jnp.zeros((DIM,), jnp.float32), 'W1': jax.random.normal(ks[4], (DFF, DIM), jnp.float32) * s, 'b1': jnp.zeros((DFF,), jnp.float32), 'W2': jax.random.normal(ks[5], (DIM, DFF), jnp.float32) * (1.0 / np.sqrt(DFF)), 'b2': jnp.zeros((DIM,), jnp.float32), 'ln2_g': jnp.ones((DIM,), jnp.float32), 'ln2_b': jnp.zeros((DIM,), jnp.float32)}
    _L1_gnn_all = _L1_gnn_setup()
    _L1_gnn_in = {k: v for k, v in _L1_gnn_all.items() if k in ('Wqkv', 'bqkv', 'Wo', 'bo', 'ln1_g', 'ln1_b', 'W1', 'b1', 'W2', 'b2', 'ln2_g', 'ln2_b')}
    del _L1_gnn_all

    def _L1_ffn_setup():
        import jax, jax.numpy as jnp
        import numpy as np
        B, S, D = (8, 2048, 128)
        H = 4 * D
        CAPACITY = 0.5
        key = jax.random.key(seed)
        ks = jax.random.split(key, 6)
        x = jax.random.normal(ks[0], (B, S, D), dtype=jnp.float32)
        attention_mask = jnp.zeros((B, 1, 1, S), dtype=jnp.float32)
        wr = jax.random.normal(ks[1], (D, 1), dtype=jnp.float32) * 0.02
        br = jnp.zeros((1,), dtype=jnp.float32)
        w1 = jax.random.normal(ks[2], (D, H), dtype=jnp.float32) * 0.02
        b1 = jnp.zeros((H,), dtype=jnp.float32)
        w2 = jax.random.normal(ks[3], (H, D), dtype=jnp.float32) * 0.02
        b2 = jnp.zeros((D,), dtype=jnp.float32)
        return {'x': x, 'attention_mask': attention_mask, 'wr': wr, 'br': br, 'w1': w1, 'b1': b1, 'w2': w2, 'b2': b2}
    _L1_ffn_all = _L1_ffn_setup()
    _L1_ffn_in = {k: v for k, v in _L1_ffn_all.items() if k in ('attention_mask', 'wr', 'br', 'w1', 'b1', 'w2', 'b2')}
    del _L1_ffn_all

    def _L2_gnn_setup():
        import jax, jax.numpy as jnp
        import numpy as np
        NEG_SLOPE = 0.2
        key = jax.random.key(seed)
        k1, k2, k3, k4 = jax.random.split(key, 4)
        B, N, Fin, Fout = (8, 1024, 128, 128)
        x = jax.random.normal(k1, (B, N, Fin), dtype=jnp.float32)
        A = jax.random.randint(k2, (B, N, N), 0, 2, dtype=jnp.int32)
        W = jax.random.normal(k3, (Fin, Fout), dtype=jnp.float32) * (1.0 / np.sqrt(Fin))
        a = jax.random.normal(k4, (2 * Fout,), dtype=jnp.float32)
        return {'x': x, 'A': A, 'W': W, 'a': a}
    _L2_gnn_all = _L2_gnn_setup()
    _L2_gnn_in = {k: v for k, v in _L2_gnn_all.items() if k in ('W', 'a')}
    del _L2_gnn_all

    def _L2_ffn_setup():
        import jax, jax.numpy as jnp
        import numpy as np
        TOP_K = 2
        LN_EPS = 1e-05
        key = jax.random.key(seed)
        ks = jax.random.split(key, 8)
        B, S, D, E, H = (16, 512, 128, 8, 512)
        x = jax.random.normal(ks[0], (B, S, D), dtype=jnp.float32)
        Wr = jax.random.normal(ks[1], (D, E), dtype=jnp.float32) * 0.1
        br = jnp.zeros((E,), dtype=jnp.float32)
        ln_g = jnp.ones((E, D), dtype=jnp.float32)
        ln_b = jnp.zeros((E, D), dtype=jnp.float32)
        W1 = jax.random.normal(ks[2], (E, D, H), dtype=jnp.float32) * (1.0 / np.sqrt(D))
        b1 = jnp.zeros((E, H), dtype=jnp.float32)
        W2 = jax.random.normal(ks[3], (E, H, D), dtype=jnp.float32) * (1.0 / np.sqrt(H))
        b2 = jnp.zeros((E, D), dtype=jnp.float32)
        return {'x': x, 'Wr': Wr, 'br': br, 'ln_g': ln_g, 'ln_b': ln_b, 'W1': W1, 'b1': b1, 'W2': W2, 'b2': b2}
    _L2_ffn_all = _L2_ffn_setup()
    _L2_ffn_in = {k: v for k, v in _L2_ffn_all.items() if k in ('Wr', 'br', 'ln_g', 'ln_b', 'W1', 'b1', 'W2', 'b2')}
    del _L2_ffn_all

    def _L3_gnn_setup():
        import jax, jax.numpy as jnp
        import numpy as np
        NEG_INF = -1000000000.0
        LEAKY_SLOPE = 0.2
        key = jax.random.key(seed)
        k1, k2, k3, k4 = jax.random.split(key, 4)
        B, N, D_in, D_out = (8, 1024, 128, 128)
        x = jax.random.normal(k1, (B, N, D_in), dtype=jnp.float32)
        adj_matrix = jax.random.randint(k2, (B, N, N), 0, 2, dtype=jnp.int32)
        W = jax.random.normal(k3, (D_out, D_in), dtype=jnp.float32) / np.sqrt(D_in)
        a = jax.random.normal(k4, (1, 2 * D_out), dtype=jnp.float32) / np.sqrt(2 * D_out)
        return {'x': x, 'adj_matrix': adj_matrix, 'W': W, 'a': a}
    _L3_gnn_all = _L3_gnn_setup()
    _L3_gnn_in = {k: v for k, v in _L3_gnn_all.items() if k in ('W', 'a')}
    del _L3_gnn_all

    def _L3_ffn_setup():
        import jax, jax.numpy as jnp
        import numpy as np
        B, T, C = (64, 192, 128)
        NH, NKV = (4, 2)
        HD = C // NH
        NREP = NH // NKV
        NE, TOPK = (8, 2)
        HID = int(8 / 3 * C)
        EPS_RMS = 1e-06

        def _rope_tables(t_len):
            inv_freq = 1.0 / 10000.0 ** (np.arange(0, HD, 2, dtype=np.float32) / HD)
            t = np.arange(t_len, dtype=np.float32)
            freqs = np.outer(t, inv_freq)
            emb = np.concatenate([freqs, freqs], axis=-1)
            return (jnp.asarray(np.cos(emb)), jnp.asarray(np.sin(emb)))

        def _rotate_half(x):
            h = x.shape[-1] // 2
            return jnp.concatenate([-x[..., h:], x[..., :h]], axis=-1)

        def _rmsnorm(v, w):
            return v * jax.lax.rsqrt(jnp.mean(v * v, axis=-1, keepdims=True) + EPS_RMS) * w
        key = jax.random.key(seed)
        ks = jax.random.split(key, 10)
        s = lambda k, shape: jax.random.normal(k, shape, jnp.float32) * 0.02
        return {'x': jax.random.normal(ks[0], (B, T, C), jnp.float32), 'ln1_w': jnp.ones((C,), jnp.float32), 'ln2_w': jnp.ones((C,), jnp.float32), 'wq': s(ks[1], (NH * HD, C)), 'wk': s(ks[2], (NKV * HD, C)), 'wv': s(ks[3], (NKV * HD, C)), 'wo': s(ks[4], (C, C)), 'router_w': s(ks[5], (NE, C)), 'w1': s(ks[6], (NE, HID, C)), 'w2': s(ks[7], (NE, C, HID)), 'w3': s(ks[8], (NE, HID, C))}
    _L3_ffn_all = _L3_ffn_setup()
    _L3_ffn_in = {k: v for k, v in _L3_ffn_all.items() if k in ('ln1_w', 'ln2_w', 'wq', 'wk', 'wv', 'wo', 'router_w', 'w1', 'w2', 'w3')}
    del _L3_ffn_all
    return {'x': x, 'adj': adj, 'L0_gnn_Wq': _L0_gnn_in['Wq'], 'L0_gnn_bq': _L0_gnn_in['bq'], 'L0_gnn_Wk': _L0_gnn_in['Wk'], 'L0_gnn_bk': _L0_gnn_in['bk'], 'L0_gnn_Wv': _L0_gnn_in['Wv'], 'L0_gnn_bv': _L0_gnn_in['bv'], 'L0_gnn_Wo': _L0_gnn_in['Wo'], 'L0_gnn_bo': _L0_gnn_in['bo'], 'L0_ffn_W_ih': _L0_ffn_in['W_ih'], 'L0_ffn_W_hh': _L0_ffn_in['W_hh'], 'L0_ffn_b_ih': _L0_ffn_in['b_ih'], 'L0_ffn_b_hh': _L0_ffn_in['b_hh'], 'L0_ffn_W_lin': _L0_ffn_in['W_lin'], 'L0_ffn_b_lin': _L0_ffn_in['b_lin'], 'L0_ffn_fw_att': _L0_ffn_in['fw_att'], 'L0_ffn_bw_att': _L0_ffn_in['bw_att'], 'L1_gnn_Wqkv': _L1_gnn_in['Wqkv'], 'L1_gnn_bqkv': _L1_gnn_in['bqkv'], 'L1_gnn_Wo': _L1_gnn_in['Wo'], 'L1_gnn_bo': _L1_gnn_in['bo'], 'L1_gnn_ln1_g': _L1_gnn_in['ln1_g'], 'L1_gnn_ln1_b': _L1_gnn_in['ln1_b'], 'L1_gnn_W1': _L1_gnn_in['W1'], 'L1_gnn_b1': _L1_gnn_in['b1'], 'L1_gnn_W2': _L1_gnn_in['W2'], 'L1_gnn_b2': _L1_gnn_in['b2'], 'L1_gnn_ln2_g': _L1_gnn_in['ln2_g'], 'L1_gnn_ln2_b': _L1_gnn_in['ln2_b'], 'L1_ffn_attention_mask': _L1_ffn_in['attention_mask'], 'L1_ffn_wr': _L1_ffn_in['wr'], 'L1_ffn_br': _L1_ffn_in['br'], 'L1_ffn_w1': _L1_ffn_in['w1'], 'L1_ffn_b1': _L1_ffn_in['b1'], 'L1_ffn_w2': _L1_ffn_in['w2'], 'L1_ffn_b2': _L1_ffn_in['b2'], 'L2_gnn_W': _L2_gnn_in['W'], 'L2_gnn_a': _L2_gnn_in['a'], 'L2_ffn_Wr': _L2_ffn_in['Wr'], 'L2_ffn_br': _L2_ffn_in['br'], 'L2_ffn_ln_g': _L2_ffn_in['ln_g'], 'L2_ffn_ln_b': _L2_ffn_in['ln_b'], 'L2_ffn_W1': _L2_ffn_in['W1'], 'L2_ffn_b1': _L2_ffn_in['b1'], 'L2_ffn_W2': _L2_ffn_in['W2'], 'L2_ffn_b2': _L2_ffn_in['b2'], 'L3_gnn_W': _L3_gnn_in['W'], 'L3_gnn_a': _L3_gnn_in['a'], 'L3_ffn_ln1_w': _L3_ffn_in['ln1_w'], 'L3_ffn_ln2_w': _L3_ffn_in['ln2_w'], 'L3_ffn_wq': _L3_ffn_in['wq'], 'L3_ffn_wk': _L3_ffn_in['wk'], 'L3_ffn_wv': _L3_ffn_in['wv'], 'L3_ffn_wo': _L3_ffn_in['wo'], 'L3_ffn_router_w': _L3_ffn_in['router_w'], 'L3_ffn_w1': _L3_ffn_in['w1'], 'L3_ffn_w2': _L3_ffn_in['w2'], 'L3_ffn_w3': _L3_ffn_in['w3']}

def reference(x, adj, L0_gnn_Wq, L0_gnn_bq, L0_gnn_Wk, L0_gnn_bk, L0_gnn_Wv, L0_gnn_bv, L0_gnn_Wo, L0_gnn_bo, L0_ffn_W_ih, L0_ffn_W_hh, L0_ffn_b_ih, L0_ffn_b_hh, L0_ffn_W_lin, L0_ffn_b_lin, L0_ffn_fw_att, L0_ffn_bw_att, L1_gnn_Wqkv, L1_gnn_bqkv, L1_gnn_Wo, L1_gnn_bo, L1_gnn_ln1_g, L1_gnn_ln1_b, L1_gnn_W1, L1_gnn_b1, L1_gnn_W2, L1_gnn_b2, L1_gnn_ln2_g, L1_gnn_ln2_b, L1_ffn_attention_mask, L1_ffn_wr, L1_ffn_br, L1_ffn_w1, L1_ffn_b1, L1_ffn_w2, L1_ffn_b2, L2_gnn_W, L2_gnn_a, L2_ffn_Wr, L2_ffn_br, L2_ffn_ln_g, L2_ffn_ln_b, L2_ffn_W1, L2_ffn_b1, L2_ffn_W2, L2_ffn_b2, L3_gnn_W, L3_gnn_a, L3_ffn_ln1_w, L3_ffn_ln2_w, L3_ffn_wq, L3_ffn_wk, L3_ffn_wv, L3_ffn_wo, L3_ffn_router_w, L3_ffn_w1, L3_ffn_w2, L3_ffn_w3):
    import jax
    import jax.numpy as jnp

    def _L0_gnn_ref(x, adjacency, Wq, bq, Wk, bk, Wv, bv, Wo, bo):
        import math
        import jax, jax.numpy as jnp
        import numpy as np
        B, N, E, H = (1, 2048, 128, 8)
        D = E // H
        b, n, e = x.shape

        def heads(y):
            return y.reshape(b, n, H, D).transpose(0, 2, 1, 3)
        q = heads(x @ Wq.T + bq)
        k = heads(x @ Wk.T + bk)
        v = heads(x @ Wv.T + bv)
        scores = jnp.einsum('bhnd,bhmd->bhnm', q, k) / math.sqrt(D)
        mask = adjacency[:, None, :, :] == 0
        scores = jnp.where(mask, -jnp.inf, scores)
        w = jax.nn.softmax(scores, axis=-1)
        out = jnp.einsum('bhnm,bhmd->bhnd', w, v)
        out = out.transpose(0, 2, 1, 3).reshape(b, n, e)
        return out @ Wo.T + bo

    def _L0_ffn_ref(x, W_ih, W_hh, b_ih, b_hh, W_lin, b_lin, fw_att, bw_att):
        import jax, jax.numpy as jnp
        import numpy as np
        B, T, D, H, L = (16, 2048, 128, 128, 2)

        def _lstm(x, W_ih, W_hh, b_ih, b_hh):
            x_proj = jnp.einsum('btd,gd->btg', x, W_ih) + b_ih + b_hh
            h0 = jnp.zeros((x.shape[0], W_hh.shape[1]), x.dtype)
            c0 = jnp.zeros_like(h0)

            def step(carry, xp):
                h, c = carry
                gates = xp + h @ W_hh.T
                i, f, g, o = jnp.split(gates, 4, axis=-1)
                c = jax.nn.sigmoid(f) * c + jax.nn.sigmoid(i) * jnp.tanh(g)
                h = jax.nn.sigmoid(o) * jnp.tanh(c)
                return ((h, c), h)
            _, hs = jax.lax.scan(step, (h0, c0), jnp.swapaxes(x_proj, 0, 1))
            return jnp.swapaxes(hs, 0, 1)
        lstm_out = _lstm(x, W_ih, W_hh, b_ih, b_hh)
        logits = jnp.einsum('bth,lh->btl', lstm_out, W_lin) + b_lin
        g = jax.lax.stop_gradient(jnp.argmax(logits, axis=-1).astype(lstm_out.dtype))[..., None]
        w = g * lstm_out
        inc = jnp.cumsum(w, axis=1)
        prefix = inc - w
        suffix = inc[:, -1:, :] - inc
        return 2.0 * lstm_out + prefix * fw_att + suffix * bw_att

    def _L1_gnn_ref(x, adj, Wqkv, bqkv, Wo, bo, ln1_g, ln1_b, W1, b1, W2, b2, ln2_g, ln2_b):
        import jax, jax.numpy as jnp
        import numpy as np
        DIM = 128
        HEADS = 8
        HEAD_DIM = DIM // HEADS
        DFF = 4 * DIM
        EPS = 1e-05

        def _layernorm(x, g, b):
            m = jnp.mean(x, axis=-1, keepdims=True)
            v = jnp.mean(jnp.square(x - m), axis=-1, keepdims=True)
            return (x - m) * jax.lax.rsqrt(v + EPS) * g + b
        B, N, _ = x.shape
        eye = jnp.eye(N, dtype=bool)[None]
        allowed = (adj > 0) | (jnp.swapaxes(adj, 1, 2) > 0) | eye
        qkv = x @ Wqkv.T + bqkv
        q, k, v = jnp.split(qkv, 3, axis=-1)

        def heads(t):
            return t.reshape(B, N, HEADS, HEAD_DIM).transpose(0, 2, 1, 3)
        q, k, v = (heads(q), heads(k), heads(v))
        scale = 1.0 / np.sqrt(HEAD_DIM)
        scores = jnp.einsum('bhqd,bhkd->bhqk', q * scale, k)
        scores = jnp.where(allowed[:, None], scores, -jnp.inf)
        attn = jax.nn.softmax(scores, axis=-1)
        ctx = jnp.einsum('bhqk,bhkd->bhqd', attn, v)
        ctx = ctx.transpose(0, 2, 1, 3).reshape(B, N, DIM)
        attn_out = ctx @ Wo.T + bo
        x = _layernorm(x + attn_out, ln1_g, ln1_b)
        ff = jax.nn.relu(x @ W1.T + b1) @ W2.T + b2
        x = _layernorm(x + ff, ln2_g, ln2_b)
        return x

    def _L1_ffn_ref(x, attention_mask, wr, br, w1, b1, w2, b2):
        import jax, jax.numpy as jnp
        import numpy as np
        B, S, D = (8, 2048, 128)
        H = 4 * D
        CAPACITY = 0.5
        b, s, d = x.shape
        weights = (jnp.einsum('bsd,do->bso', x, wr) + br)[..., 0]
        k = max(1, int(CAPACITY * s))
        kk = k - 1 if k > 1 else 1
        _, idx = jax.lax.top_k(weights, k)
        sel_idx = idx[:, :kk]
        sel = jnp.take_along_axis(x, sel_idx[:, :, None], axis=1)
        h = jax.nn.gelu(jnp.einsum('bkd,dh->bkh', sel, w1) + b1)
        y = jnp.einsum('bkh,hd->bkd', h, w2) + b2
        w_sel = jnp.take_along_axis(weights, sel_idx, axis=1)
        y = y * w_sel[..., None]
        batch_idx = jnp.arange(b)[:, None]
        processed = jnp.zeros_like(x).at[batch_idx, sel_idx].set(y)
        return processed + x

    def _L2_gnn_ref(x, A, W, a):
        import jax, jax.numpy as jnp
        import numpy as np
        NEG_SLOPE = 0.2
        h = jnp.einsum('bnf,fd->bnd', x, W)
        d = h.shape[-1]
        s_src = h @ a[:d]
        s_dst = h @ a[d:]
        e = s_src[:, :, None] + s_dst[:, None, :]
        e = jnp.where(e >= 0, e, NEG_SLOPE * e)
        e = jnp.where(A <= 0, -jnp.inf, e)
        alpha = jax.nn.softmax(e, axis=-1)
        y = jnp.einsum('bij,bjd->bid', alpha, h)
        return y

    def _L2_ffn_ref(x, Wr, br, ln_g, ln_b, W1, b1, W2, b2):
        import jax, jax.numpy as jnp
        import numpy as np
        TOP_K = 2
        LN_EPS = 1e-05
        B, S, D = x.shape
        N = B * S
        xt = x.reshape(N, D)
        logits = xt @ Wr + br
        probs = jax.nn.softmax(logits, axis=-1)
        top_p, top_idx = jax.lax.top_k(probs, TOP_K)
        weights = top_p / top_p.sum(axis=-1, keepdims=True)
        mu = xt.mean(axis=-1, keepdims=True)
        var = ((xt - mu) ** 2).mean(axis=-1, keepdims=True)
        xn = (xt - mu) * jax.lax.rsqrt(var + LN_EPS)
        xe = xn[None, :, :] * ln_g[:, None, :] + ln_b[:, None, :]
        h = jax.nn.gelu(jnp.einsum('end,edh->enh', xe, W1) + b1[:, None, :], approximate=False)
        y = jnp.einsum('enh,ehd->end', h, W2) + b2[:, None, :]
        y_tok = jnp.transpose(y, (1, 0, 2))
        sel = jnp.take_along_axis(y_tok, top_idx[:, :, None], axis=1)
        out = (weights[:, :, None] * sel).sum(axis=1)
        return out.reshape(B, S, D)

    def _L3_gnn_ref(x, adj_matrix, W, a):
        import jax, jax.numpy as jnp
        import numpy as np
        NEG_INF = -1000000000.0
        LEAKY_SLOPE = 0.2
        h = jnp.einsum('bnd,od->bno', x, W)
        D = h.shape[-1]
        a_left, a_right = (a[0, :D], a[0, D:])
        e = (h @ a_left)[:, :, None] + (h @ a_right)[:, None, :]
        e = jnp.where(e > 0, e, LEAKY_SLOPE * e)
        e = jnp.where(adj_matrix == 0, NEG_INF, e)
        alpha = jax.nn.softmax(e, axis=-1)
        return jnp.einsum('bij,bjd->bid', alpha, h)

    def _L3_ffn_ref(x, ln1_w, ln2_w, wq, wk, wv, wo, router_w, w1, w2, w3):
        import jax, jax.numpy as jnp
        import numpy as np
        B, T, C = (64, 192, 128)
        NH, NKV = (4, 2)
        HD = C // NH
        NREP = NH // NKV
        NE, TOPK = (8, 2)
        HID = int(8 / 3 * C)
        EPS_RMS = 1e-06

        def _rope_tables(t_len):
            inv_freq = 1.0 / 10000.0 ** (np.arange(0, HD, 2, dtype=np.float32) / HD)
            t = np.arange(t_len, dtype=np.float32)
            freqs = np.outer(t, inv_freq)
            emb = np.concatenate([freqs, freqs], axis=-1)
            return (jnp.asarray(np.cos(emb)), jnp.asarray(np.sin(emb)))

        def _rotate_half(x):
            h = x.shape[-1] // 2
            return jnp.concatenate([-x[..., h:], x[..., :h]], axis=-1)

        def _rmsnorm(v, w):
            return v * jax.lax.rsqrt(jnp.mean(v * v, axis=-1, keepdims=True) + EPS_RMS) * w
        Bx, Tx, Cx = x.shape
        h = _rmsnorm(x, ln1_w)
        q = (h @ wq.T).reshape(Bx, Tx, NH, HD).transpose(0, 2, 1, 3)
        k = (h @ wk.T).reshape(Bx, Tx, NKV, HD).transpose(0, 2, 1, 3)
        v = (h @ wv.T).reshape(Bx, Tx, NKV, HD).transpose(0, 2, 1, 3)
        cos, sin = _rope_tables(Tx)
        cos, sin = (cos[None, None], sin[None, None])
        q = q * cos + _rotate_half(q) * sin
        k = k * cos + _rotate_half(k) * sin
        k = jnp.repeat(k, NREP, axis=1)
        v = jnp.repeat(v, NREP, axis=1)
        scores = jnp.einsum('bhtd,bhsd->bhts', q, k) / jnp.sqrt(jnp.float32(HD))
        causal = jnp.tril(jnp.ones((Tx, Tx), dtype=bool))
        scores = jnp.where(causal[None, None], scores, jnp.float32(-1e+30))
        att = jax.nn.softmax(scores, axis=-1)
        y = jnp.einsum('bhts,bhsd->bhtd', att, v).transpose(0, 2, 1, 3).reshape(Bx, Tx, Cx)
        x = x + y @ wo.T
        flat = _rmsnorm(x, ln2_w).reshape(-1, Cx)
        probs = jax.nn.softmax(flat @ router_w.T, axis=-1)
        tp, ti = jax.lax.top_k(probs, TOPK)
        tp = tp / (jnp.sum(tp, axis=-1, keepdims=True) + 1e-09)
        weights = jnp.sum(tp[..., None] * jax.nn.one_hot(ti, NE, dtype=flat.dtype), axis=1)
        out = jnp.zeros_like(flat)
        for e in range(NE):
            hh = jax.nn.silu(flat @ w1[e].T) * (flat @ w3[e].T)
            out = out + weights[:, e:e + 1] * (hh @ w2[e].T)
        return x + out.reshape(Bx, Tx, Cx)
    x = x + _L0_gnn_ref(_layernorm(x, axis=-1), adj, L0_gnn_Wq, L0_gnn_bq, L0_gnn_Wk, L0_gnn_bk, L0_gnn_Wv, L0_gnn_bv, L0_gnn_Wo, L0_gnn_bo)
    x = x + _L0_ffn_ref(_layernorm(x, axis=-1), L0_ffn_W_ih, L0_ffn_W_hh, L0_ffn_b_ih, L0_ffn_b_hh, L0_ffn_W_lin, L0_ffn_b_lin, L0_ffn_fw_att, L0_ffn_bw_att)
    x = x + _L1_gnn_ref(_layernorm(x, axis=-1), adj, L1_gnn_Wqkv, L1_gnn_bqkv, L1_gnn_Wo, L1_gnn_bo, L1_gnn_ln1_g, L1_gnn_ln1_b, L1_gnn_W1, L1_gnn_b1, L1_gnn_W2, L1_gnn_b2, L1_gnn_ln2_g, L1_gnn_ln2_b)
    x = x + _L1_ffn_ref(_layernorm(x, axis=-1), L1_ffn_attention_mask, L1_ffn_wr, L1_ffn_br, L1_ffn_w1, L1_ffn_b1, L1_ffn_w2, L1_ffn_b2)
    x = x + _L2_gnn_ref(_layernorm(x, axis=-1), adj, L2_gnn_W, L2_gnn_a)
    x = x + _L2_ffn_ref(_layernorm(x, axis=-1), L2_ffn_Wr, L2_ffn_br, L2_ffn_ln_g, L2_ffn_ln_b, L2_ffn_W1, L2_ffn_b1, L2_ffn_W2, L2_ffn_b2)
    x = x + _L3_gnn_ref(_layernorm(x, axis=-1), adj, L3_gnn_W, L3_gnn_a)
    x = x + _L3_ffn_ref(_layernorm(x, axis=-1), L3_ffn_ln1_w, L3_ffn_ln2_w, L3_ffn_wq, L3_ffn_wk, L3_ffn_wv, L3_ffn_wo, L3_ffn_router_w, L3_ffn_w1, L3_ffn_w2, L3_ffn_w3)
    return x

_drawn_inputs = setup_inputs


def setup_inputs(seed=0):
    import zlib

    import numpy as np

    out = dict(_drawn_inputs(seed))
    spreads = {'L0_gnn_bq': (0.0, 0.1),
     'L0_gnn_bk': (0.0, 0.8),
     'L0_gnn_bv': (0.0, 0.1),
     'L0_gnn_bo': (0.0, 0.1),
     'L0_ffn_fw_att': (0.0010000000474974513, 0.6),
     'L0_ffn_bw_att': (0.0010000000474974513, 0.6),
     'L1_gnn_bqkv': (0.0, 0.1),
     'L1_gnn_bo': (0.0, 0.1),
     'L1_gnn_ln1_g': (1.0, 0.2),
     'L1_gnn_ln1_b': (0.0, 0.1),
     'L1_gnn_b1': (0.0, 0.1),
     'L1_gnn_b2': (0.0, 0.1),
     'L1_gnn_ln2_g': (1.0, 0.2),
     'L1_gnn_ln2_b': (0.0, 0.1),
     'L1_ffn_b1': (0.0, 0.8),
     'L1_ffn_b2': (0.0, 0.8),
     'L2_ffn_br': (0.0, 0.1),
     'L2_ffn_ln_g': (1.0, 0.2),
     'L2_ffn_ln_b': (0.0, 0.496),
     'L2_ffn_b1': (0.0, 0.508),
     'L2_ffn_b2': (0.0, 0.334),
     'L3_ffn_ln1_w': (1.0, 0.6),
     'L3_ffn_ln2_w': (1.0, 0.6)}
    factors = {'L0_ffn_W_lin': 8.0,
     'L0_ffn_b_lin': 3.071,
     'L1_ffn_wr': 6.477,
     'L1_ffn_w1': 8.0,
     'L1_ffn_w2': 8.0,
     'L3_ffn_wq': 8.0,
     'L3_ffn_wk': 8.0,
     'L3_ffn_wv': 8.0,
     'L3_ffn_wo': 8.0,
     'L3_ffn_router_w': 8.0,
     'L3_ffn_w1': 8.0,
     'L3_ffn_w2': 8.0,
     'L3_ffn_w3': 8.0}
    for name, (base, spread) in spreads.items():
        noise = np.random.default_rng([zlib.crc32(name.encode()), seed]).standard_normal(out[name].shape)
        drawn = base * np.exp(spread * noise) if base else spread * noise
        out[name] = jnp.asarray(drawn.astype(out[name].dtype))
    for name, factor in factors.items():
        out[name] = (out[name] * factor).astype(out[name].dtype)
    return out
```

```python
from contextlib import ExitStack

import numpy as np

import concourse.bass as bass
from concourse import mybir

F32 = mybir.dt.float32
BF16 = mybir.dt.bfloat16
I32 = mybir.dt.int32
ALU = mybir.AluOpType
ACT = mybir.ActivationFunctionType
AX = mybir.AxisListType

P = 128
B = 16
N = 512
D = 128
T = N // P
BIG = 1e30
LN_EPS = 1e-5


class Mem:

    def __init__(self, nc, ctx, tag):
        self.nc, self.ctx, self.tag, self.sems = nc, ctx, tag, []
        ctx.callback(self.clear)

    def sb(self, name, shape, dt=F32):
        return self.ctx.enter_context(self.nc.sbuf_tensor(f"{self.tag}_{name}", shape, dt))

    def ps(self, name, shape=(P, 512), dt=F32):
        return self.ctx.enter_context(self.nc.psum_tensor(f"{self.tag}_{name}", list(shape), dt))

    def sem(self, name):
        self.sems.append(self.ctx.enter_context(self.nc.semaphore(f"{self.tag}_{name}")))
        return self.sems[-1]

    def clear(self):
        numbers = sorted(sem.num for sem in self.sems)
        first = min(numbers, default=0)
        for n, after in zip(numbers, numbers[1:] + [None]):
            if after != n + 1:
                self.nc.gpsimd.sem_clear(range(first, n + 1))
                first = after
        self.nc.all_engine_barrier()


class Chain:

    def __init__(self, engine, sem, base=0):
        self.engine, self.sem, self.base, self.n = engine, sem, base, 0

    def step(self, ins):
        ins.then_inc(self.sem, 1)
        self.n += 1

    def settle(self):
        self.engine.wait_ge(self.sem, self.base + self.n)


class Core:

    def __init__(self, nc, ctx, dram):
        m = Mem(nc, ctx, "core")
        self.nc, self.dram = nc, dram
        self.x_res = m.sb("x_res", [P, B, T, D])
        self.mid = m.sb("mid", [P, B, T, D])
        self.x_stat = m.sb("x_stat", [P, B, T, 2])
        self.stat2 = m.sb("stat2", [P, B, T, 2])
        self.gate = m.sb("gate", [P, B, T, 8])
        self.ident = m.sb("ident", [P, P])
        self.ident_bf = m.sb("ident_bf", [P, P], BF16)
        self.passed = {nc.vector.engine: m.sem("passed_dve"), nc.gpsimd.engine: m.sem("passed_pool")}
        self.params = [m.sb(f"params{i}", [P, w]) for i, w in enumerate(REGION)]
        self.params_in = [m.sem(f"params_in{k}") for k in range(len(STAGES))]

    def load_params(self, sp, k):
        if k == len(SPAN):
            return
        lo, hi = SPAN[k]
        sp.dma_start(self.params[k % 2][:, 0:hi - lo], self.dram["weights"][:, lo:hi]).then_inc(self.params_in[k], 16)

    def param(self, k, name):
        lo, n = PLACE[name]
        return self.params[k % 2][:, lo - SPAN[k][0]:lo - SPAN[k][0] + n]


def apart(engine, core):
    engine.sem_inc(core.passed[engine.engine], 1)


class Spare:

    def __init__(self, core, k):
        self.region, self.at = core.params[k % 2], SPAN[k][1] - SPAN[k][0]

    def sb(self, shape, dt=F32):
        words = int(np.prod(shape[1:])) * (2 if dt == BF16 else 4) // 4
        flat_ap = self.region[:, self.at:self.at + words]
        self.at += words
        assert self.at <= self.region.shape[1]
        if dt != F32:
            flat_ap = flat_ap.bitcast(dt)
        if len(shape) == 2:
            return flat_ap
        return flat_ap.rearrange("p (a b) -> p a b", a=shape[1])


def layout():
    return [
        ("mha0", [("wq0", 256), ("wk0", 256), ("wv0", 128), ("wo0", 128), ("bq0", 2), ("bk0", 2), ("bv0", 128), ("bo0", 128)]),
        ("lstm", [("w_ih", 512), ("w_hh", 512), ("b_ih", 4), ("b_hh", 4), ("w_lin", 256), ("b_lin", 2), ("fw", 1), ("bw", 1)]),
        ("mha1", [("wq1", 256), ("wk1", 256), ("wv1", 128), ("wo1", 128), ("bq1", 2), ("bk1", 2), ("bv1", 128), ("bo1", 128)]),
        ("ffn1", [("f1w1", 512), ("f1w2", 512), ("f1b1", 4), ("f1b2", 128), ("g1", 128), ("be1", 128), ("g2", 128), ("be2", 128)]),
        ("mod", [("mw1", 512), ("mw2", 512), ("mb1", 4), ("mb2", 128), ("mwr", 1), ("mbr", 1)]),
        ("gat2", [("gw2", 128), ("gwt2", 128), ("ga2", 2)]),
        ("moe2", [("ew1", 4096), ("ew2", 4096), ("eb1", 32), ("eb2", 128), ("eg", 8), ("ebt", 8), ("er", 8), ("ebr", 8)]),
        ("gat3", [("gw3", 128), ("gwt3", 128), ("ga3", 2)]),
        ("mha3", [("wq3", 128), ("wqr3", 128), ("wk3", 128), ("wkr3", 128), ("wv3", 128), ("wo3", 128), ("ln1w", 1), ("cos", 512), ("sin", 512)]),
        ("moe3", [("hw1", 8 * 341), ("hw3", 8 * 341), ("hw2", 8 * 3 * 128), ("hr", 8), ("ln2w", 1)]),
    ]


def spans():
    place, span, at = {}, [], 0
    for _, parts in layout():
        start = at
        for name, n in parts:
            place[name] = (at, n)
            at += n
        span.append((start, at))
    return place, span, at


PLACE, SPAN, COLUMNS = spans()
STAGES = [name for name, _ in layout()]
REGION = [max(hi - lo for lo, hi in SPAN[i::2]) for i in range(2)]


def row_stats(dve, chain, core, six, two, tile):
    for t in range(T):
        chain.step(dve.bn_stats(six[:, t, :], tile[:, t, :]))
    chain.settle()
    apart(dve, core)
    for t in range(T):
        chain.step(dve.bn_aggr(two[:, t, :], six[:, t, :]))


WRITE_STEPS = 2 * T + 3


def write_x(dve, chain, core, b, change, base, upd, six, two):
    chain.step(dve.tensor_tensor(upd[:, :, :], change, base, ALU.add))
    chain.settle()
    apart(dve, core)
    chain.step(dve.tensor_copy(core.x_res[:, b], upd[:, :, :]))
    row_stats(dve, chain, core, six, two, upd)
    chain.settle()
    apart(dve, core)
    chain.step(dve.tensor_copy(core.x_stat[:, b], two[:, :, :]))
    chain.settle()


def rsqrt_stats(pool, done, rstd, shift, stat, scratch, half, eps, rms=False):
    pool.memset(half, -0.5).then_inc(done, 1)
    if rms:
        pool.tensor_tensor(shift, stat[:, :, :, 0], stat[:, :, :, 0], ALU.mult).then_inc(done, 1)
        pool.wait_ge(done, 2)
        pool.tensor_tensor(scratch, shift, stat[:, :, :, 1], ALU.add).then_inc(done, 1)
        pool.wait_ge(done, 3)
        pool.tensor_scalar(scratch, scratch, eps, None, ALU.add).then_inc(done, 1)
        pool.wait_ge(done, 4)
        pool.tensor_tensor(rstd, scratch, half, ALU.pow).then_inc(done, 1)
        pool.wait_ge(done, 5)
        return
    pool.tensor_scalar(scratch, stat[:, :, :, 1], eps, None, ALU.add).then_inc(done, 1)
    pool.wait_ge(done, 2)
    pool.tensor_tensor(rstd, scratch, half, ALU.pow).then_inc(done, 1)
    pool.wait_ge(done, 3)
    pool.tensor_tensor(shift, stat[:, :, :, 0], rstd, ALU.mult).then_inc(done, 1)
    pool.wait_ge(done, 4)
    pool.tensor_scalar(shift, shift, -1.0, None, ALU.mult).then_inc(done, 1)
    pool.wait_ge(done, 5)


def over_features(ap):
    return ap.unsqueeze(2).broadcast_to([P, T, D])


def flat(ap):
    return ap.rearrange("p a b -> p (a b)")


def load_stage(core):
    nc = core.nc
    with ExitStack() as ctx:
        m = Mem(nc, ctx, "load")
        six = m.sb("six", [P, T, 6])
        two = m.sb("two", [P, T, 2])
        x_in = [m.sem(f"x_in{b}") for b in range(B)]
        ones_set, ident_set, bf_set, chain_sem = m.sem("ones_set"), m.sem("ident_set"), m.sem("bf_set"), m.sem("chain")
        block = ctx.enter_context(nc.Block())

        @block.sync
        def _(sp):
            for b in range(B):
                sp.dma_start(core.x_res[:, b], core.dram["x"][b].rearrange("(t p) d -> p t d", p=P)).then_inc(x_in[b], 16)
                if b == 0:
                    core.load_params(sp, 0)

        @block.gpsimd
        def _(pool):
            pool.memset(core.ident[:, :], 0.0).then_inc(ones_set, 1)
            pool.wait_ge(ones_set, 1)
            pool.affine_select(out=core.ident[:, :], in_=core.ident[:, :], compare_op=ALU.not_equal, fill=1.0,
                               base=0, pattern=[[-1, P]], channel_multiplier=1).then_inc(ident_set, 1)
            pool.wait_ge(ident_set, 1)
            pool.tensor_copy(core.ident_bf[:, :], core.ident[:, :]).then_inc(bf_set, 1)

        @block.vector
        def _(dve):
            chain = Chain(dve, chain_sem)
            for b in range(B):
                dve.wait_ge(x_in[b], 16)
                row_stats(dve, chain, core, six, two, core.x_res[:, b])
                chain.settle()
                apart(dve, core)
                chain.step(dve.tensor_copy(core.x_stat[:, b], two[:, :, :]))


def mha_stage(core, k, tag, heads, head_dim, groups, scale, out_res, sym=False, rope=False, from_xn=False):
    nc = core.nc
    with ExitStack() as ctx:
        m = Mem(nc, ctx, tag)
        items = 4 * T * groups
        rstd, shift = m.sb("rstd", [P, B, T]), m.sb("shift", [P, B, T])
        scratch, half = m.sb("scratch", [P, B, T]), m.sb("half", [P, B, T])
        spare = Spare(core, k)
        adj_raw = None if rope else spare.sb([P, T, N], I32)
        mask = [m.sb(f"mask{s}", [P, T, N], BF16) for s in range(1 if rope else 2)]
        either = spare.sb([P, T, N], BF16) if sym else None
        xn = [spare.sb([P, T, D]) for s in range(2)]
        xT = spare.sb([P, N])
        neg_bq = m.sb("neg_bq", [P, 2])
        qT = [[m.sb(f"qT{g}{j}", [P, N]) for j in range(4)] for g in range(groups)]
        kT = [m.sb(f"kT{g}", [P, N]) for g in range(groups)]
        v32 = m.sb("v32", [P, T, heads, 32])
        PR = 4
        LAG = 3
        prob = m.sb("prob", [P, PR, N])
        bias = m.sb("bias", [P, PR])
        ncos, nsin, part = (m.sb("ncos", [P, N]), m.sb("nsin", [P, N]), m.sb("part", [P, 4, N])) if rope else (None,) * 3
        total = m.sb("total", [P, T, 4])
        projections = 4 if rope else 2 * groups
        keys = lambda t: t + 1 if rope else T
        probT = m.sb("probT", [P, 4, T, N]) if rope or from_xn else core.mid[:, :, :, :].rearrange("p (j u) t d -> p j u (t d)", j=4)
        oT = [spare.sb([P, N]) for g in range(groups)]
        rinv = m.sb("rinv", [P, T, 4])
        ctx_tok = spare.sb([P, T, D])
        ctxT = spare.sb([P, N])
        upd = spare.sb([P, T, D])
        six, two = m.sb("six", [P, T, 6]), m.sb("two", [P, T, 2])
        misc = [m.ps(f"misc{i}") for i in range(2)]
        score = [m.ps(f"score{i}") for i in range(2)]
        tpose = [m.ps(f"tpose{i}") for i in range(2)]
        o_ps = [m.ps(f"o{g}") for g in range(2)]

        names = ["stat_done", "half_mean", "adj_in", "mask_ready", "xn_ready", "batch_free", "xt_in_psum", "xT_ready",
                 "proj_done", "qk_ready", "v_ready", "score_done", "score_taken", "prob_ready", "prob_free",
                 "probT_act", "probT_dve", "pv_done", "oT_ready", "back_done", "ctx_ready", "ctxt_in_psum",
                 "ctxT_ready", "attn_done", "chain", "const_set", "sym_raw", "sym_done", "sym_taken", "adj_free", "rot_ready",
                 "zeros_set"]
        S = {n: m.sem(n) for n in names}
        wq, wk, wv, wo = (core.param(k, w + tag[-1]) for w in ("wq", "wk", "wv", "wo"))
        if rope:
            wqr, wkr = core.param(k, "wqr3"), core.param(k, "wkr3")
            cos, sin, ln1w = core.param(k, "cos"), core.param(k, "sin"), core.param(k, "ln1w")
        else:
            bq, bk, bv, bo = (core.param(k, w + tag[-1]) for w in ("bq", "bk", "bv", "bo"))
        block = ctx.enter_context(nc.Block())

        @block.sync
        def _(sp):
            core.load_params(sp, k + 1)
            if rope:
                return
            adj = core.dram["adj"].rearrange("b (t p) n -> b p t n", p=P)
            sp.dma_start(adj_raw[:, :, :], adj[0]).then_inc(S["adj_in"], 16)
            with sp.Fori(1, B) as b:
                sp.wait_ge(S["adj_free"], b)
                sp.dma_start(adj_raw[:, :, :], adj[b]).then_inc(S["adj_in"], 16)

        @block.gpsimd
        def _(pool):
            rsqrt_stats(pool, S["stat_done"], rstd[:, :, :], shift[:, :, :], core.stat2 if rope else core.x_stat,
                        scratch[:, :, :], half[:, :, :], 1e-6 if rope else LN_EPS, rms=rope)
            if rope:
                pool.memset(mask[0][:, :, :], 0.0).then_inc(S["sym_raw"], 1)
                pool.wait_ge(S["sym_raw"], 1)
                pool.affine_select(out=mask[0][:, :, :], in_=mask[0][:, :, :], compare_op=ALU.is_ge, fill=BIG, base=0,
                                   pattern=[[P, T], [-1, N]], channel_multiplier=1).then_inc(S["adj_free"], 1)

            def graph(b, s):
                pool.wait_ge(S["batch_free"], b + 1)
                if rope:
                    pool.tensor_tensor(xn[s][:, :, :], core.mid[:, b], over_features(rstd[:, b]), ALU.mult)\
                        .then_inc(S["xn_ready"], 1)
                    return
                pool.tensor_tensor(xn[s][:, :, :], core.x_res[:, b], over_features(rstd[:, b]), ALU.mult)\
                    .then_inc(S["half_mean"], 1)
                pool.wait_ge(S["half_mean"], b + 1)
                pool.tensor_tensor(xn[s][:, :, :], xn[s][:, :, :], over_features(shift[:, b]), ALU.add)\
                    .then_inc(S["xn_ready"], 1)
                pool.wait_ge(S["adj_in"], 16 * (b + 1))
                apart(pool, core)
                if sym:
                    pool.tensor_scalar(mask[s][:, :, :], adj_raw[:, :, :], 0.0, None, ALU.is_gt)\
                        .then_inc(S["adj_free"], 1)
                else:
                    pool.tensor_scalar(mask[s][:, :, :], adj_raw[:, :, :], 0.0, BIG, ALU.is_equal, ALU.mult)\
                        .then_inc(S["adj_free"], 1)

            with pool.Fori(0, B // 2) as j:
                for s in range(2):
                    graph(j * 2 + s, s)

        @block.tensor
        def _(pe):
            pe.sem_inc(S["prob_free"], PR)
            pe.sem_inc(S["pv_done"], 1)
            pe.wait_ge(core.params_in[k], 16)

            def front(b, s):
                pe.wait_ge(S["xn_ready"], b + 1)
                for t in range(T):
                    last = pe.transpose(misc[0][:, t * P:(t + 1) * P], xn[s][:, t, :], core.ident[:, :])
                last.then_inc(S["xt_in_psum"], 1)
                pe.wait_ge(S["xT_ready"], b + 1)
                uses = [wq, wqr, wk, wkr] if rope else [wq[:, g * P:(g + 1) * P] for g in range(groups)] + [wk[:, g * P:(g + 1) * P] for g in range(groups)]
                for n, w in enumerate(uses):
                    if n == 0:
                        pe.wait_ge(S["batch_free"], b + 2)
                    if n >= 2:
                        pe.wait_ge(S["qk_ready"], projections * b + n - 1)
                    pe.matmul(misc[(n + 1) % 2][:, :], w, xT[:, :], start=True, stop=True).then_inc(S["proj_done"], 1)
                n = len(uses)
                pe.wait_ge(S["qk_ready"], projections * b + n - 1)
                for t in range(T):
                    last = pe.matmul(misc[(n + 1) % 2][:, t * D:(t + 1) * D], xT[:, t * P:(t + 1) * P], wv,
                                     start=True, stop=True)
                last.then_inc(S["proj_done"], 1)
                if sym:
                    pe.wait_ge(S["adj_free"], b + 1)
                    for t in range(T):
                        pe.wait_ge(S["sym_taken"], T * b + t + 1)
                        bank = o_ps[0][:, 0:N // 2].bitcast(BF16)
                        for u in range(T):
                            last = pe.transpose(bank[:, u * P:(u + 1) * P], mask[s][:, u, t * P:(t + 1) * P],
                                                core.ident_bf[:, :])
                        last.then_inc(S["sym_done"], 1)

            def scores(b, n):
                g, t, j = n // (4 * T), n // 4 % T, n % 4
                if n == 0:
                    pe.wait_ge(S["qk_ready"], projections * (b + 1))
                if n == 0 and rope:
                    pe.wait_ge(S["rot_ready"], 2 * b + 4)
                pe.wait_ge(S["score_taken"], items * b + n + 1)
                width = keys(t) * P
                pe.matmul(score[n % 2][:, 0:width], qT[g][j][:, t * P:(t + 1) * P], kT[g][:, 0:width], start=True, stop=True)\
                    .then_inc(S["score_done"], 1)

            def transposes(b, n):
                pe.wait_ge(S["prob_ready"], items * b + n + 1)
                half_n = (items * b) // 2 if isinstance(b, int) else b * (items // 2)
                pe.wait_ge(S["probT_act"] if n % 2 == 0 else S["probT_dve"], half_n + n // 2 + 1)
                for u in range(keys(n // 4 % T)):
                    last = pe.transpose(tpose[n % 2][:, u * P:(u + 1) * P], prob[:, n % PR, u * P:(u + 1) * P],
                                        core.ident[:, :])
                last.then_inc(S["prob_free"], 1)

            def values(b, g):
                done = b * (items // 2) + 2 * T * (g + 1) + 1
                if g == 0:
                    pe.wait_ge(S["v_ready"], b + 1)
                pe.wait_ge(S["oT_ready"], groups * b + g + 1)
                pe.wait_ge(S["probT_act"], done)
                pe.wait_ge(S["probT_dve"], done)
                for u in range(T):
                    for j in range(4):
                        first = u * P if rope else 0
                        last = pe.matmul(o_ps[g][32 * j:32 * j + 32, first:], v32[:, u, 4 * g + j, :], probT[:, j, u, first:],
                                         start=(u == 0), stop=(u == T - 1))
                last.then_inc(S["pv_done"], 1)

            def back(b):
                for g in range(groups):
                    pe.wait_ge(S["oT_ready"], groups * (b + 1) + g + 1)
                    if g == 0:
                        pe.wait_ge(S["v_ready"], b + 1)
                    for t in range(T):
                        last = pe.transpose(misc[g][:, t * P:(t + 1) * P], oT[g][:, t * P:(t + 1) * P], core.ident[:, :])
                    last.then_inc(S["back_done"], 1)
                pe.wait_ge(S["ctx_ready"], groups * (b + 1))
                for t in range(T):
                    last = pe.transpose(misc[0][:, t * P:(t + 1) * P], ctx_tok[:, t, :], core.ident[:, :])
                last.then_inc(S["ctxt_in_psum"], 1)
                pe.wait_ge(S["ctxT_ready"], b + 1)
                for t in range(T):
                    last = pe.matmul(misc[1][:, t * D:(t + 1) * D], ctxT[:, t * P:(t + 1) * P], wo, start=True, stop=True)
                last.then_inc(S["attn_done"], 1)

            def graph(b, s):
                front(b, s)
                for n in range(items + LAG):
                    if n < items:
                        scores(b, n)
                    if n >= LAG:
                        if (n - LAG) % (4 * T) == 0 and n > LAG:
                            values(b, (n - LAG) // (4 * T) - 1)
                        transposes(b, n - LAG)
                values(b, groups - 1)
                back(b)

            with pe.Fori(0, B // 2) as j:
                for s in range(2):
                    graph(j * 2 + s, s)

        @block.scalar
        def _(act):
            act.sem_inc(S["probT_act"], 1)
            act.wait_ge(core.params_in[k], 16)
            if rope:
                act.mul(ncos[:, :], cos, -scale).then_inc(S["const_set"], 1)
                act.mul(nsin[:, :], sin, -scale).then_inc(S["const_set"], 1)
            else:
                act.mul(neg_bq[:, 0:groups], bq, -scale).then_inc(S["const_set"], 1)
                act.wait_ge(S["const_set"], 1)
                act.wait_ge(S["zeros_set"], 4 * groups)

            def copy_probT(b, n):
                act.wait_ge(S["prob_free"], items * b + n + 1 + PR)
                if n % (4 * T) == 0:
                    act.wait_ge(S["pv_done"], groups * b + n // (4 * T) + 1)
                t, j = n // 4 % T, n % 4
                act.copy(probT[:, j, 0:keys(t), t * P:(t + 1) * P],
                         tpose[0][:, 0:keys(t) * P].rearrange("p (u q) -> p u q", u=keys(t)))\
                    .then_inc(S["probT_act"], 1)

            def graph(b, s):
                for n in range(0 if rope else 2 * groups):
                    act.wait_ge(S["proj_done"], (2 * groups + 1) * b + n + 1)
                    g, is_k = n % groups, n >= groups
                    if is_k:
                        ins = act.activation(kT[g][:, :], misc[(n + 1) % 2][:, :], ACT.Identity, bias=bk[:, g:g + 1])
                    else:
                        for j in range(4):
                            rows = slice(32 * j, 32 * j + 32)
                            ins = act.activation(qT[g][j][rows, :], misc[(n + 1) % 2][rows, :], ACT.Identity,
                                                 bias=neg_bq[rows, g:g + 1], scale=-scale)
                    ins.then_inc(S["qk_ready"], 1)
                for n in range(items + LAG):
                    if n < items:
                        act.wait_ge(S["score_taken"], items * b + n + 1 + 2)
                        tile = prob[:, n % PR, 0:keys(n // 4 % T) * P]
                        sums = {"accum_out": total[:, n // 4, n % 4:n % 4 + 1]} if rope else {}
                        act.activation(tile, tile, ACT.Exp, bias=bias[:, n % PR:n % PR + 1], scale=-1.0, **sums)\
                            .then_inc(S["prob_ready"], 1)
                    if n >= LAG and (n - LAG) % 2 == 0:
                        copy_probT(b, n - LAG)
                for g in range(groups):
                    act.wait_ge(S["pv_done"], groups * b + g + 1 + 1)
                    act.copy(oT[g][:, :], o_ps[g][:, :]).then_inc(S["oT_ready"], 1)
                act.wait_ge(S["ctxt_in_psum"], b + 1)
                act.copy(ctxT[:, :], misc[0][:, :]).then_inc(S["ctxT_ready"], 1)

            act.sem_inc(S["oT_ready"], groups)
            with act.Fori(0, B // 2) as j:
                for s in range(2):
                    graph(j * 2 + s, s)

        @block.vector
        def _(dve):
            dve.sem_inc(S["batch_free"], 2)
            dve.sem_inc(S["score_taken"], 2)
            dve.sem_inc(S["probT_dve"], 1)
            if sym:
                dve.sem_inc(S["sym_taken"], 1)
            dve.wait_ge(core.params_in[k], 16)
            for q in qT:
                for j in range(4):
                    dve.memset(q[j][:, :], 0.0).then_inc(S["zeros_set"], 1)
            dve.memset(v32[:, :, :, :], 0.0).then_inc(S["rot_ready"], 1)
            dve.wait_ge(S["rot_ready"], 1)
            if rope:
                dve.sem_inc(S["rot_ready"], 1)
                dve.wait_ge(S["zeros_set"], 4 * groups)
                dve.wait_ge(S["const_set"], 2)
                dve.wait_ge(S["adj_free"], 1)
            else:
                dve.memset(v32[:, :, :, head_dim:head_dim + 1], 1.0).then_inc(S["rot_ready"], 1)

            def copy_probT(b, n):
                dve.wait_ge(S["prob_free"], items * b + n + 1 + PR)
                if n % (4 * T) == 1:
                    dve.wait_ge(S["pv_done"], groups * b + n // (4 * T) + 1)
                t, j = n // 4 % T, n % 4
                dve.tensor_copy(probT[:, j, 0:keys(t), t * P:(t + 1) * P],
                                tpose[1][:, 0:keys(t) * P].rearrange("p (u q) -> p u q", u=keys(t)))\
                    .then_inc(S["probT_dve"], 1)

            def graph(b, s):
                chain = Chain(dve, S["chain"], b * CHAIN)
                dve.wait_ge(S["xt_in_psum"], b + 1)
                if rope:
                    dve.tensor_scalar(xT[:, :], misc[0][:, :], ln1w, None, ALU.mult).then_inc(S["xT_ready"], 1)
                    for n, table in enumerate((ncos[:, :], nsin[:, :], cos, sin)):
                        dve.wait_ge(S["proj_done"], 5 * b + n + 1)
                        dve.tensor_tensor(part[:, n, :], misc[(n + 1) % 2][:, :], table, ALU.mult).then_inc(S["qk_ready"], 1)
                    dve.wait_ge(S["qk_ready"], 4 * (b + 1))
                    dve.tensor_tensor(kT[0][:, :], part[:, 2, :], part[:, 3, :], ALU.add).then_inc(S["rot_ready"], 1)
                    for j in range(4):
                        rows = slice(32 * j, 32 * j + 32)
                        ins = dve.tensor_tensor(qT[0][j][rows, :], part[rows, 0, :], part[rows, 1, :], ALU.add)
                    ins.then_inc(S["rot_ready"], 1)
                else:
                    dve.tensor_copy(xT[:, :], misc[0][:, :]).then_inc(S["xT_ready"], 1)
                dve.wait_ge(S["proj_done"], (projections + 1) * (b + 1))
                if rope:
                    dve.tensor_copy(v32[:, :, :, :], misc[1][:, :].rearrange("p (t h d) -> p t h d", t=T, h=heads))\
                        .then_inc(S["v_ready"], 1)
                else:
                    dve.tensor_tensor(v32[:, :, :, 0:head_dim],
                                      misc[1][:, :].rearrange("p (t h d) -> p t h d", t=T, h=heads),
                                      bv.rearrange("p (h d) -> p h d", h=heads).unsqueeze(1).broadcast_to([P, T, heads, head_dim]),
                                      ALU.add).then_inc(S["v_ready"], 1)
                if sym:
                    for t in range(T):
                        dve.wait_ge(S["sym_done"], T * b + t + 1)
                        dve.tensor_tensor(either[:, t, :], mask[s][:, t, :], o_ps[0][:, 0:N // 2].bitcast(BF16), ALU.add)\
                            .then_inc(S["sym_taken"], 1)
                    dve.wait_ge(S["sym_taken"], T * (b + 1) + 1)
                    for t in range(T):
                        own = either[:, t, t * P:(t + 1) * P]
                        chain.step(dve.tensor_tensor(own, own, core.ident_bf[:, :], ALU.add))
                    chain.settle()
                    chain.step(dve.tensor_scalar(either[:, :, :], either[:, :, :], 0.0, BIG, ALU.is_equal, ALU.mult))
                    chain.settle()
                    apart(dve, core)
                else:
                    dve.wait_ge(S["adj_free"], 1 if rope else b + 1)
                    apart(dve, core)
                for n in range(items + LAG):
                    if n < items:
                        t = n // 4 % T
                        dve.wait_ge(S["score_done"], items * b + n + 1)
                        dve.wait_ge(S["prob_free"], items * b + n + 1)
                        apart(dve, core)
                        allowed = either if sym else mask[0] if rope else mask[s]
                        width = keys(t) * P
                        dve.tensor_tensor_reduce(prob[:, n % PR, 0:width], score[n % 2][:, 0:width], allowed[:, t, 0:width], 1.0, 3e38,
                                                 ALU.add, ALU.min, bias[:, n % PR:n % PR + 1])\
                            .then_inc(S["score_taken"], 1)
                    if n >= LAG and (n - LAG) % 2 == 1:
                        copy_probT(b, n - LAG)
                for g in range(groups):
                    dve.wait_ge(S["back_done"], groups * b + g + 1)
                    o = misc[g][:, :].rearrange("p (t j c) -> p t j c", t=T, j=4)
                    chain.step(dve.reciprocal(rinv[:, :, :], total[:, :, :] if rope else o[:, :, :, head_dim]))
                    chain.settle()
                    dve.tensor_tensor(ctx_tok[:, :, 4 * g * head_dim:4 * (g + 1) * head_dim].rearrange("p t (j c) -> p t j c", j=4),
                                      o[:, :, :, 0:head_dim], rinv[:, :, :].unsqueeze(3).broadcast_to([P, T, 4, head_dim]),
                                      ALU.mult).then_inc(S["ctx_ready"], 1)
                    dve.wait_ge(S["ctx_ready"], groups * b + g + 1)
                dve.wait_ge(S["attn_done"], b + 1)
                base = core.mid[:, b] if rope else xn[s][:, :, :] if from_xn else core.x_res[:, b]
                chain.step(dve.tensor_tensor(upd[:, :, :], misc[1][:, :].rearrange("p (t d) -> p t d", t=T), base, ALU.add))
                chain.settle()
                if not rope:
                    chain.step(dve.tensor_tensor(upd[:, :, :], upd[:, :, :], bo.unsqueeze(1).broadcast_to([P, T, D]), ALU.add))
                    chain.settle()
                row_stats(dve, chain, core, six, two, upd)
                chain.step(dve.tensor_copy(out_res[:, b], upd[:, :, :]))
                chain.settle()
                apart(dve, core)
                dve.tensor_copy(core.x_stat[:, b], two[:, :, :]).then_inc(S["batch_free"], 1)
                assert chain.n == CHAIN, chain.n

            CHAIN = groups + (1 if rope else 2) + 2 * T + 1 + (T + 1 if sym else 0)
            with dve.Fori(0, B // 2) as j:
                for s in range(2):
                    graph(j * 2 + s, s)


def lstm_stage(core, k):
    nc = core.nc
    C = 16
    CB = C * B
    CHUNKS = N // C
    GATE = [0, 1, 3, 2]
    with ExitStack() as ctx:
        m = Mem(nc, ctx, "lstm")
        rstd, shift = m.sb("rstd", [P, B, T]), m.sb("shift", [P, B, T])
        scratch, half = m.sb("scratch", [P, B, T]), m.sb("half", [P, B, T])
        xn = [m.sb(f"xn{s}", [P, T, D]) for s in range(2)]
        xT = m.sb("xT", [P, N * B])
        hT = core.mid[:, :, :, :].rearrange("p b t d -> p b (t d)")
        w_part = [m.sb(f"w_part{i}", [P, 4 * P], BF16) for i in range(3)]
        w_rest = m.sb("w_rest", [P, 4 * P])
        gate_bias = m.sb("gate_bias", [P, 4])
        xg = [m.sb(f"xg{s}", [P, C, 4, B]) for s in range(2)]
        h_part = m.sb("h_part", [P, 3, B], BF16)
        h_rest = m.sb("h_rest", [P, B])
        hist = [m.sb(f"hist{s}", [P, C, B]) for s in range(2)]
        sig = m.sb("sig", [P, 3, B])
        gc = m.sb("gc", [P, 2, B])
        prod = m.sb("prod", [P, 2, B])
        tanh_c = m.sb("tanh_c", [P, B])
        w_lin = m.sb("w_lin", [P, 2, P])
        ones = m.sb("ones", [P, N])
        logit0, gated, sums, before, after = (m.sb(n, [P, N]) for n in ("logit0", "gated", "sums", "before", "after"))
        upd = m.sb("upd", [P, T, D])
        six, two = m.sb("six", [P, T, 6]), m.sb("two", [P, T, 2])
        gates = [m.ps(f"gates{i}") for i in range(2)]
        xproj = [m.ps(f"xproj{i}") for i in range(2)]
        logit = [m.ps(f"logit_ps{i}") for i in range(2)]
        tpose = [m.ps(f"tpose{i}") for i in range(2)]
        names = ["stat_done", "half_mean", "xn_ready", "xt_in_psum", "xT_act", "xT_dve", "w_parts", "w_chain", "xproj_done",
                 "xg_ready", "hi_ready", "mid_ready", "lo_ready", "h_full", "gates_done", "sig_ready", "tg_ready",
                 "prod_done", "c_ready", "tc_ready", "hist_saved", "hist_free", "logits_done", "logits_free",
                 "scan_chain", "out_ready", "out_in_psum", "chain", "bias_set", "rest"]
        S = {n: m.sem(n) for n in names}
        par = lambda name: core.param(k, name)
        block = ctx.enter_context(nc.Block())

        @block.sync
        def _(sp):
            core.load_params(sp, k + 1)

        @block.gpsimd
        def _(pool):
            rsqrt_stats(pool, S["stat_done"], rstd[:, :, :], shift[:, :, :], core.x_stat, scratch[:, :, :],
                        half[:, :, :], LN_EPS)

            def normalise(b, s):
                pool.wait_ge(S["xt_in_psum"], b + 1)
                pool.tensor_tensor(xn[s][:, :, :], core.x_res[:, b], over_features(rstd[:, b]), ALU.mult)\
                    .then_inc(S["half_mean"], 1)
                pool.wait_ge(S["half_mean"], b + 1)
                pool.tensor_tensor(xn[s][:, :, :], xn[s][:, :, :], over_features(shift[:, b]), ALU.add)\
                    .then_inc(S["xn_ready"], 1)

            with pool.Fori(0, B // 2) as j:
                for s in range(2):
                    normalise(j * 2 + s, s)

            def save(c, s):
                pool.wait_ge(S["h_full"], C * (c + 1) + 1)
                pool.tensor_copy(hT[:, :, bass.ds(c * C, C)], hist[s][:, :, :].rearrange("p t b -> p b t"))\
                    .then_inc(S["hist_saved"], 1)

            pool.sem_inc(S["hist_saved"], 2)
            with pool.Fori(0, CHUNKS // 2) as it:
                for s in range(2):
                    save(it * 2 + s, s)

        @block.tensor
        def _(pe):
            pe.sem_inc(S["xt_in_psum"], 2)
            pe.wait_ge(core.params_in[k], 16)

            def turn(b, s):
                pe.wait_ge(S["xn_ready"], b + 1)
                pe.wait_ge(S["xT_act" if s == 0 else "xT_dve"], j + 1)
                for t in range(T):
                    last = pe.transpose(tpose[s][:, t * P:(t + 1) * P], xn[s][:, t, :], core.ident[:, :])
                last.then_inc(S["xt_in_psum"], 1)

            with pe.Fori(0, B // 2) as j:
                for s in range(2):
                    turn(j * 2 + s, s)
            pe.wait_ge(S["xT_act"], B // 2 + 1)
            pe.wait_ge(S["xT_dve"], B // 2 + 1)

            def project(c, n):
                pe.wait_ge(S["xg_ready"], 4 * c + n + 1)
                g = GATE[n]
                pe.matmul(xproj[n % 2][:, 0:CB], par("w_ih")[:, g * P:(g + 1) * P], xT[:, bass.ds(c * CB, CB)],
                          start=True, stop=True).then_inc(S["xproj_done"], 1)

            def seed(step, c, s, t):
                if t == 0:
                    pe.wait_ge(S["xg_ready"], 4 * c + 4 + 2)
                pe.matmul(gates[t % 2][:, 0:4 * B], core.ident[:, :], xg[s][:, t, :, :].rearrange("p g b -> p (g b)"),
                          start=True, stop=False)

            def recur(step, t):
                for part, sem in enumerate(("hi_ready", "mid_ready", "lo_ready")):
                    pe.wait_ge(S[sem], step + 1)
                    for w in range(3 - part):
                        for n in range(4):
                            g = GATE[n]
                            last = pe.matmul(gates[t % 2][:, n * B:(n + 1) * B], w_part[w][:, g * P:(g + 1) * P],
                                             h_part[:, part, :], start=False, stop=(part == 2 and w == 0 and n == 3))
                last.then_inc(S["gates_done"], 1)

            def chunk(c, s, last):
                for t in range(C):
                    recur(c * C + t, t)
                    if t < C - 1:
                        seed(c * C + t + 1, c, s, t + 1)
                    elif not last:
                        seed(c * C + t + 1, c + 1, 1 - s, 0)
                    if not last and 1 <= t <= 4:
                        project(c + 1, t - 1)

            for n in range(4):
                project(0, n)
            pe.wait_ge(S["w_parts"], 3)
            seed(0, 0, 0, 0)
            with pe.Fori(0, CHUNKS // 2 - 1) as it:
                for s in range(2):
                    chunk(it * 2 + s, s, False)
            chunk(CHUNKS - 2, 0, False)
            chunk(CHUNKS - 1, 1, True)

            def label(b):
                pe.wait_ge(S["logits_free"], b + 1)
                for i in range(2):
                    last = pe.matmul(logit[i][:, :], w_lin[:, i, :], hT[:, b, :], start=True, stop=True)
                last.then_inc(S["logits_done"], 1)

            def back(b):
                pe.wait_ge(S["out_ready"], b + 1)
                for t in range(T):
                    last = pe.transpose(tpose[0][:, t * P:(t + 1) * P], before[:, t * P:(t + 1) * P], core.ident[:, :])
                last.then_inc(S["out_in_psum"], 1)

            pe.wait_ge(S["hist_saved"], CHUNKS + 2)
            with pe.Fori(0, B) as b:
                label(b)
                back(b)

        @block.scalar
        def _(act):
            act.sem_inc(S["xT_act"], 1)
            act.sem_inc(S["xg_ready"], 2)
            act.wait_ge(core.params_in[k], 16)
            with act.Fori(0, B // 2) as j:
                act.wait_ge(S["xt_in_psum"], j * 2 + 1 + 2)
                act.copy(xT[:, :].rearrange("p (t b) -> p b t", b=B)[:, j * 2, :], tpose[0][:, :]).then_inc(S["xT_act"], 1)
            act.wait_ge(S["bias_set"], 1)

            def bring(c, s, n):
                act.wait_ge(S["xproj_done"], 4 * c + n + 1)
                act.activation(xg[s][:, :, n, :], xproj[n % 2][:, 0:CB].rearrange("p (t b) -> p t b", b=B),
                               ACT.Identity, bias=gate_bias[:, GATE[n]:GATE[n] + 1]).then_inc(S["xg_ready"], 1)

            def step(g, t):
                act.wait_ge(S["gates_done"], g + 1)
                bank = gates[t % 2]
                act.activation(sig[:, :, :], bank[:, 0:3 * B].rearrange("p (g b) -> p g b", b=B), ACT.Sigmoid)\
                    .then_inc(S["sig_ready"], 1)
                act.activation(gc[:, 0, :], bank[:, 3 * B:4 * B], ACT.Tanh).then_inc(S["tg_ready"], 1)
                act.wait_ge(S["c_ready"], g + 1)
                act.activation(tanh_c[:, :], gc[:, 1, :], ACT.Tanh).then_inc(S["tc_ready"], 1)

            def chunk(c, s, last):
                for t in range(C):
                    step(c * C + t, t)
                    if not last and 1 <= t <= 4:
                        bring(c + 1, 1 - s, t - 1)

            for n in range(4):
                bring(0, 0, n)
            with act.Fori(0, CHUNKS // 2 - 1) as it:
                for s in range(2):
                    chunk(it * 2 + s, s, False)
            chunk(CHUNKS - 2, 0, False)
            chunk(CHUNKS - 1, 1, True)

        @block.vector
        def _(dve):
            dve.sem_inc(S["xT_dve"], 1)
            dve.wait_ge(core.params_in[k], 16)
            dve.tensor_tensor(gate_bias[:, :], par("b_ih"), par("b_hh"), ALU.add).then_inc(S["bias_set"], 1)
            dve.tensor_copy(w_part[0][:, :], par("w_hh")).then_inc(S["w_parts"], 1)
            dve.wait_ge(S["w_parts"], 1)
            dve.tensor_tensor(w_rest[:, :], par("w_hh"), w_part[0][:, :], ALU.subtract).then_inc(S["w_chain"], 1)
            dve.wait_ge(S["w_chain"], 1)
            dve.tensor_copy(w_part[1][:, :], w_rest[:, :]).then_inc(S["w_parts"], 1)
            dve.wait_ge(S["w_parts"], 2)
            dve.tensor_tensor(w_part[2][:, :], w_rest[:, :], w_part[1][:, :], ALU.subtract).then_inc(S["w_parts"], 1)
            dve.memset(ones[:, :], 1.0).then_inc(S["w_chain"], 1)
            for i in range(2):
                dve.tensor_copy(w_lin[:, i, :], par("w_lin")[:, i * P:(i + 1) * P]).then_inc(S["w_chain"], 1)
            dve.memset(gc[:, :, :], 0.0).then_inc(S["h_full"], 1)
            for part, sem in enumerate(("hi_ready", "mid_ready", "lo_ready")):
                dve.memset(h_part[:, part, :], 0.0).then_inc(S[sem], 1)
            with dve.Fori(0, B // 2) as j:
                dve.wait_ge(S["xt_in_psum"], j * 2 + 2 + 2)
                dve.tensor_copy(xT[:, :].rearrange("p (t b) -> p b t", b=B)[:, j * 2 + 1, :], tpose[1][:, :])\
                    .then_inc(S["xT_dve"], 1)

            def step(g, s, t):
                dve.wait_ge(S["sig_ready"], g + 1)
                dve.wait_ge(S["tg_ready"], g + 1)
                dve.tensor_tensor(prod[:, :, :], sig[:, 0:2, :], gc[:, :, :], ALU.mult).then_inc(S["prod_done"], 1)
                dve.wait_ge(S["prod_done"], g + 1)
                dve.tensor_tensor(gc[:, 1, :], prod[:, 0, :], prod[:, 1, :], ALU.add).then_inc(S["c_ready"], 1)
                dve.wait_ge(S["tc_ready"], g + 1)
                dve.tensor_tensor(h_part[:, 0, :], sig[:, 2, :], tanh_c[:, :], ALU.mult).then_inc(S["hi_ready"], 1)
                dve.tensor_tensor(hist[s][:, t, :], sig[:, 2, :], tanh_c[:, :], ALU.mult).then_inc(S["h_full"], 1)
                dve.wait_ge(S["hi_ready"], g + 2)
                dve.wait_ge(S["h_full"], g + 2)
                dve.tensor_tensor(h_part[:, 1, :], hist[s][:, t, :], h_part[:, 0, :], ALU.subtract)\
                    .then_inc(S["mid_ready"], 1)
                dve.tensor_tensor(h_rest[:, :], hist[s][:, t, :], h_part[:, 0, :], ALU.subtract).then_inc(S["rest"], 1)
                dve.wait_ge(S["mid_ready"], g + 2)
                dve.wait_ge(S["rest"], g + 1)
                dve.tensor_tensor(h_part[:, 2, :], h_rest[:, :], h_part[:, 1, :], ALU.subtract)\
                    .then_inc(S["lo_ready"], 1)

            def chunk(c, s):
                dve.wait_ge(S["hist_saved"], c + 1)
                for t in range(C):
                    step(c * C + t, s, t)

            with dve.Fori(0, CHUNKS // 2) as it:
                for s in range(2):
                    chunk(it * 2 + s, s)

            dve.sem_inc(S["logits_free"], 1)
            dve.wait_ge(S["hist_saved"], CHUNKS + 2)
            with dve.Fori(0, B) as b:
                steps = 8 + 2 * T + 2
                chain = Chain(dve, S["chain"], b * steps)
                h = hT[:, b, :]
                dve.wait_ge(S["logits_done"], b + 1)
                chain.step(dve.tensor_scalar(logit0[:, :], logit[0][:, :], par("b_lin")[:, 0:1], None, ALU.add))
                chain.settle()
                dve.scalar_tensor_tensor(gated[:, :], logit[1][:, :], par("b_lin")[:, 1:2], logit0[:, :], ALU.add,
                                         ALU.is_gt).then_inc(S["logits_free"], 1)
                dve.wait_ge(S["logits_free"], b + 2)
                chain.step(dve.tensor_tensor(gated[:, :], gated[:, :], h, ALU.mult))
                chain.settle()
                chain.step(dve.tensor_tensor_scan(sums[:, :], ones[:, :], gated[:, :], 0.0, ALU.mult, ALU.add))
                chain.settle()
                chain.step(dve.tensor_tensor(before[:, :], sums[:, :], gated[:, :], ALU.subtract))
                chain.step(dve.tensor_scalar(after[:, :], sums[:, :], -1.0, sums[:, N - 1:N], ALU.mult, ALU.add))
                chain.settle()
                chain.step(dve.scalar_tensor_tensor(before[:, :], before[:, :], par("fw"), h, ALU.mult, ALU.add))
                chain.step(dve.scalar_tensor_tensor(after[:, :], after[:, :], par("bw"), h, ALU.mult, ALU.add))
                chain.settle()
                dve.tensor_tensor(before[:, :], before[:, :], after[:, :], ALU.add).then_inc(S["out_ready"], 1)
                dve.wait_ge(S["out_in_psum"], b + 1)
                chain.step(dve.tensor_tensor(upd[:, :, :], tpose[0][:, :].rearrange("p (t d) -> p t d", t=T),
                                             core.x_res[:, b], ALU.add))
                chain.settle()
                row_stats(dve, chain, core, six, two, upd)
                chain.step(dve.tensor_copy(core.x_res[:, b], upd[:, :, :]))
                chain.settle()
                apart(dve, core)
                chain.step(dve.tensor_copy(core.x_stat[:, b], two[:, :, :]))
                chain.settle()
                assert chain.n == steps + 0, chain.n


def ffn_tiles(pe, hid_ps, hid_done, hid_free, w1, xT, base, tiles):
    for n in range(tiles):
        pe.wait_ge(hid_free, base + n + 1)
        pe.matmul(hid_ps[n % len(hid_ps)][:, :], w1[:, n * P:(n + 1) * P], xT, start=True, stop=True)\
            .then_inc(hid_done, 1)


def ffn1_stage(core, k):
    nc = core.nc
    H = 4
    with ExitStack() as ctx:
        m = Mem(nc, ctx, "ffn1")
        rstd, shift = m.sb("rstd", [P, B, T]), m.sb("shift", [P, B, T])
        scratch, half = m.sb("scratch", [P, B, T]), m.sb("half", [P, B, T])
        y = [m.sb(f"y{s}", [P, T, D]) for s in range(2)]
        yT = [m.sb(f"yT{s}", [P, N]) for s in range(2)]
        hid = [m.sb(f"hid{s}", [P, H, N]) for s in range(2)]
        r = [m.sb(f"r{s}", [P, T, D]) for s in range(2)]
        upd = m.sb("upd", [P, T, D])
        six, two = m.sb("six", [P, T, 6]), m.sb("two", [P, T, 2])
        rstat = [m.sb(f"rstat{s}", [P, T, 2]) for s in range(2)]
        rv, rr, rs = m.sb("rv", [P, T]), [m.sb(f"rr{s}", [P, T]) for s in range(2)], [m.sb(f"rs{s}", [P, T]) for s in range(2)]
        tp = [m.ps(f"tp{s}") for s in range(2)]
        hid_ps = [m.ps(f"hid_ps{i}") for i in range(2)]
        out_ps = [m.ps(f"out_ps{s}") for s in range(2)]
        names = ["stat_done", "y_chain", "y_ready", "y_free", "y_in_psum", "yT_ready", "hid_done", "hid_free",
                 "out_done", "r_chain", "r_ready", "norm_ready", "chain", "x_chain"]
        S = {n: m.sem(n) for n in names}
        par = lambda name: core.param(k, name)
        block = ctx.enter_context(nc.Block())

        @block.sync
        def _(sp):
            core.load_params(sp, k + 1)

        @block.gpsimd
        def _(pool):
            rsqrt_stats(pool, S["stat_done"], rstd[:, :, :], shift[:, :, :], core.x_stat, scratch[:, :, :],
                        half[:, :, :], LN_EPS)
            pool.wait_ge(core.params_in[k], 16)
            row = lambda name: par(name).unsqueeze(1).broadcast_to([P, T, D])

            def first(b, s):
                chain = Chain(pool, S["y_chain"], b * 3)
                pool.wait_ge(S["y_free"], b + 1)
                chain.step(pool.tensor_tensor(y[s][:, :, :], core.mid[:, b], over_features(rstd[:, b]), ALU.mult))
                chain.settle()
                chain.step(pool.tensor_tensor(y[s][:, :, :], y[s][:, :, :], over_features(shift[:, b]), ALU.add))
                chain.settle()
                chain.step(pool.tensor_tensor(y[s][:, :, :], y[s][:, :, :], row("g1"), ALU.mult))
                chain.settle()
                pool.tensor_tensor(y[s][:, :, :], y[s][:, :, :], row("be1"), ALU.add).then_inc(S["y_ready"], 1)

            def second(b, s):
                chain = Chain(pool, S["r_chain"], b * 2)
                pool.wait_ge(S["r_ready"], b + 1)
                apart(pool, core)
                chain.step(pool.tensor_scalar(rv[:, :], rstat[s][:, :, 1], LN_EPS, None, ALU.add))
                chain.settle()
                chain.step(pool.tensor_tensor(rr[s][:, :], rv[:, :], half[:, 0, :], ALU.pow))
                chain.settle()
                pool.tensor_tensor(rs[s][:, :], rstat[s][:, :, 0], rr[s][:, :], ALU.mult).then_inc(S["norm_ready"], 1)

            first(0, 0)
            with pool.Fori(0, B // 2 - 1) as j:
                first(j * 2 + 1, 1)
                second(j * 2, 0)
                first(j * 2 + 2, 0)
                second(j * 2 + 1, 1)
            first(B - 1, 1)
            second(B - 2, 0)
            second(B - 1, 1)

        @block.tensor
        def _(pe):
            pe.wait_ge(core.params_in[k], 16)

            def graph(b, s):
                pe.wait_ge(S["y_ready"], b + 1)
                for t in range(T):
                    last = pe.transpose(tp[s][:, t * P:(t + 1) * P], y[s][:, t, :], core.ident[:, :])
                last.then_inc(S["y_in_psum"], 1)
                pe.wait_ge(S["yT_ready"], b + 1)
                ffn_tiles(pe, hid_ps, S["hid_done"], S["hid_free"], par("f1w1"), yT[s][:, :], H * b, H)
                pe.wait_ge(S["hid_free"], H * (b + 1) + 2)
                for t in range(T):
                    for n in range(H):
                        last = pe.matmul(out_ps[s][:, t * D:(t + 1) * D], hid[s][:, n, t * P:(t + 1) * P],
                                         par("f1w2")[:, n * D:(n + 1) * D], start=(n == 0), stop=(n == H - 1))
                last.then_inc(S["out_done"], 1)

            with pe.Fori(0, B // 2) as j:
                for s in range(2):
                    graph(j * 2 + s, s)

        @block.scalar
        def _(act):
            act.sem_inc(S["hid_free"], 2)
            act.wait_ge(core.params_in[k], 16)

            def graph(b, s):
                act.wait_ge(S["y_in_psum"], b + 1)
                act.copy(yT[s][:, :], tp[s][:, :]).then_inc(S["yT_ready"], 1)
                for n in range(H):
                    act.wait_ge(S["hid_done"], H * b + n + 1)
                    act.activation(hid[s][:, n, :], hid_ps[n % 2][:, :], ACT.Relu, bias=par("f1b1")[:, n:n + 1])\
                        .then_inc(S["hid_free"], 1)

            with act.Fori(0, B // 2) as j:
                for s in range(2):
                    graph(j * 2 + s, s)

        @block.vector
        def _(dve):
            dve.sem_inc(S["y_free"], 2)
            dve.wait_ge(core.params_in[k], 16)
            row = lambda name: par(name).unsqueeze(1).broadcast_to([P, T, D])

            def graph(b, s):
                chain = Chain(dve, S["chain"], b * STEPS)
                dve.wait_ge(S["out_done"], b + 1)
                o = out_ps[s][:, :].rearrange("p (t d) -> p t d", t=T)
                chain.step(dve.tensor_tensor(r[s][:, :, :], o, row("f1b2"), ALU.add))
                chain.settle()
                dve.tensor_tensor(r[s][:, :, :], r[s][:, :, :], y[s][:, :, :], ALU.add).then_inc(S["y_free"], 1)
                dve.wait_ge(S["y_free"], b + 1 + 2)
                for t in range(T):
                    chain.step(dve.bn_stats(six[:, t, :], r[s][:, t, :]))
                chain.settle()
                apart(dve, core)
                for t in range(T):
                    ins = dve.bn_aggr(rstat[s][:, t, :], six[:, t, :])
                ins.then_inc(S["r_ready"], 1)
                dve.wait_ge(S["norm_ready"], b + 1)
                for t in range(T):
                    chain.step(dve.tensor_scalar(r[s][:, t, :], r[s][:, t, :], rr[s][:, t:t + 1], rs[s][:, t:t + 1],
                                                 ALU.mult, ALU.subtract))
                chain.settle()
                chain.step(dve.tensor_tensor(r[s][:, :, :], r[s][:, :, :], row("g2"), ALU.mult))
                chain.settle()
                chain.step(dve.tensor_tensor(r[s][:, :, :], r[s][:, :, :], row("be2"), ALU.add))
                chain.settle()
                write_x(dve, chain, core, b, r[s][:, :, :], core.x_res[:, b], upd, six, two)
                assert chain.n == STEPS, chain.n

            STEPS = 3 + 2 * T + WRITE_STEPS
            with dve.Fori(0, B // 2) as j:
                for s in range(2):
                    graph(j * 2 + s, s)


class Rows:

    def __init__(self, m, core, S, source, shifted=True):
        self.core, self.S, self.source, self.shifted = core, S, source, shifted
        self.rstd, self.shift = m.sb("rstd", [P, B, T]), m.sb("shift", [P, B, T])
        self.scratch, self.half = m.sb("scratch", [P, B, T]), m.sb("half", [P, B, T])
        self.xn = [m.sb(f"xn{s}", [P, T, D]) for s in range(2)]

    def scales(self, pool, stat, eps):
        rsqrt_stats(pool, self.S["stat_done"], self.rstd[:, :, :], self.shift[:, :, :], stat,
                    self.scratch[:, :, :], self.half[:, :, :], eps, rms=not self.shifted)

    def normalise(self, pool, b, s):
        S, xn = self.S, self.xn[s][:, :, :]
        pool.wait_ge(S["xn_free"], b + 1)
        if not self.shifted:
            pool.tensor_tensor(xn, self.source[:, b], over_features(self.rstd[:, b]), ALU.mult).then_inc(S["xn_ready"], 1)
            return
        pool.tensor_tensor(xn, self.source[:, b], over_features(self.rstd[:, b]), ALU.mult).then_inc(S["half_mean"], 1)
        pool.wait_ge(S["half_mean"], b + 1)
        pool.tensor_tensor(xn, xn, over_features(self.shift[:, b]), ALU.add).then_inc(S["xn_ready"], 1)

    NAMES = ["stat_done", "xn_free", "half_mean", "xn_ready"]


def pairs(engine, graph, first=0, last=B):
    with engine.Fori(first // 2, last // 2) as j:
        for s in range(2):
            graph(j * 2 + s, s)


def turn(pe, core, bank, tile):
    for t in range(T):
        last = pe.transpose(bank[:, t * P:(t + 1) * P], tile[:, t, :], core.ident[:, :])
    return last


def mod_stage(core, k):
    nc = core.nc
    H = 4
    KEPT = max(1, N // 2) - 1
    with ExitStack() as ctx:
        m = Mem(nc, ctx, "mod")
        names = Rows.NAMES + ["xt_done", "xT_ready", "w_done", "wcol_ready", "wide_ready", "wrow_done", "ranked",
                              "hid_done", "hid_free", "out_done", "out_taken", "tri_set", "tri_chain", "chain"]
        S = {n: m.sem(n) for n in names}
        rows_ = Rows(m, core, S, core.x_res)
        xT = [m.sb(f"xT{s}", [P, N]) for s in range(2)]
        wcol = [m.sb(f"wcol{s}", [P, T]) for s in range(2)]
        wide = m.sb("wide", [P, T, P])
        earlier, later = m.sb("earlier", [P, T, N], BF16), m.sb("later", [P, T, N], BF16)
        hits = m.sb("hits", [P, 2 * T, N], BF16)
        count = m.sb("count", [P, 2, T])
        rank, coef = m.sb("rank", [P, T]), m.sb("coef", [P, T])
        hid = [m.sb(f"hid{s}", [P, H, N]) for s in range(2)]
        y = m.sb("y", [P, T, D])
        upd = m.sb("upd", [P, T, D])
        six, two = m.sb("six", [P, T, 6]), m.sb("two", [P, T, 2])
        tp = m.ps("tp")
        w_ps = m.ps("w_ps")
        wrow = m.ps("wrow")
        hid_ps = [m.ps(f"hid_ps{i}") for i in range(2)]
        out_ps = [m.ps(f"out_ps{s}") for s in range(2)]
        par = lambda name: core.param(k, name)
        block = ctx.enter_context(nc.Block())

        @block.sync
        def _(sp):
            core.load_params(sp, k + 1)

        @block.gpsimd
        def _(pool):
            rows_.scales(pool, core.x_stat, LN_EPS)
            for n, (tri, op, sign) in enumerate(((earlier, ALU.is_gt, 1), (later, ALU.is_ge, -1))):
                pool.memset(tri[:, :, :], 1.0).then_inc(S["tri_chain"], 1)
                pool.wait_ge(S["tri_chain"], n + 1)
                pool.affine_select(out=tri[:, :, :], in_=tri[:, :, :], compare_op=op, fill=0.0, base=0,
                                   pattern=[[sign * P, T], [-sign, N]], channel_multiplier=sign).then_inc(S["tri_set"], 1)
            pairs(pool, lambda b, s: rows_.normalise(pool, b, s))

        @block.tensor
        def _(pe):
            pe.wait_ge(core.params_in[k], 16)

            def graph(b, s):
                pe.wait_ge(S["xn_ready"], b + 1)
                turn(pe, core, tp, rows_.xn[s]).then_inc(S["xt_done"], 1)
                pe.wait_ge(S["xT_ready"], b + 1)
                for t in range(T):
                    last = pe.matmul(w_ps[:, t:t + 1], xT[s][:, t * P:(t + 1) * P], par("mwr"), start=True, stop=True)
                last.then_inc(S["w_done"], 1)
                ffn_tiles(pe, hid_ps, S["hid_done"], S["hid_free"], par("mw1"), xT[s][:, :], H * b, H)
                pe.wait_ge(S["wide_ready"], b + 1)
                turn(pe, core, wrow, wide).then_inc(S["wrow_done"], 1)
                pe.wait_ge(S["hid_free"], H * (b + 1) + 2)
                for t in range(T):
                    for n in range(H):
                        last = pe.matmul(out_ps[s][:, t * D:(t + 1) * D], hid[s][:, n, t * P:(t + 1) * P],
                                         par("mw2")[:, n * D:(n + 1) * D], start=(n == 0), stop=(n == H - 1))
                last.then_inc(S["out_done"], 1)

            pairs(pe, graph)

        @block.scalar
        def _(act):
            act.sem_inc(S["hid_free"], 2)
            act.wait_ge(core.params_in[k], 16)

            def graph(b, s):
                act.wait_ge(S["xt_done"], b + 1)
                act.copy(xT[s][:, :], tp[:, :]).then_inc(S["xT_ready"], 1)
                for n in range(H):
                    act.wait_ge(S["hid_done"], H * b + n + 1)
                    act.activation(hid[s][:, n, :], hid_ps[n % 2][:, :], ACT.Gelu_apprx_tanh,
                                   bias=par("mb1")[:, n:n + 1]).then_inc(S["hid_free"], 1)

            pairs(act, graph)

        @block.vector
        def _(dve):
            dve.sem_inc(S["xn_free"], 2)
            dve.wait_ge(core.params_in[k], 16)
            dve.wait_ge(S["tri_set"], 2)
            STEPS = 2 * T + 2 + 1 + T - 1 + WRITE_STEPS

            def graph(b, s):
                chain = Chain(dve, S["chain"], b * STEPS)
                dve.wait_ge(S["w_done"], b + 1)
                dve.tensor_scalar(wcol[s][:, :], w_ps[:, 0:T], par("mbr"), None, ALU.add).then_inc(S["wcol_ready"], 1)
                dve.wait_ge(S["wcol_ready"], b + 1)
                dve.tensor_copy(wide[:, :, :], wcol[s][:, :].unsqueeze(2).broadcast_to([P, T, P])).then_inc(S["wide_ready"], 1)
                dve.wait_ge(S["wrow_done"], b + 1)
                for t in range(T):
                    for i, (tri, op) in enumerate(((earlier, ALU.is_ge), (later, ALU.is_gt))):
                        chain.step(dve.scalar_tensor_tensor(hits[:, 2 * t + i, :], wrow[:, :], wcol[s][:, t:t + 1],
                                                            tri[:, t, :], op, ALU.mult, accum_out=count[:, i, t:t + 1]))
                chain.settle()
                chain.step(dve.tensor_tensor(rank[:, :], count[:, 0, :], count[:, 1, :], ALU.add))
                chain.settle()
                chain.step(dve.scalar_tensor_tensor(coef[:, :], rank[:, :], float(KEPT), wcol[s][:, :], ALU.is_lt, ALU.mult))
                dve.wait_ge(S["out_done"], b + 1)
                chain.step(dve.tensor_tensor(y[:, :, :], out_ps[s][:, :].rearrange("p (t d) -> p t d", t=T),
                                             par("mb2").unsqueeze(1).broadcast_to([P, T, D]), ALU.add))
                chain.settle()
                for t in range(T):
                    ins = dve.scalar_tensor_tensor(y[:, t, :], y[:, t, :], coef[:, t:t + 1], rows_.xn[s][:, t, :],
                                                   ALU.mult, ALU.add)
                    if t < T - 1:
                        chain.step(ins)
                ins.then_inc(S["xn_free"], 1)
                chain.settle()
                dve.wait_ge(S["xn_free"], b + 1 + 2)
                write_x(dve, chain, core, b, y[:, :, :], core.x_res[:, b], upd, six, two)
                assert chain.n == STEPS, (chain.n, STEPS)

            pairs(dve, graph)


def gat_stage(core, k, i):
    nc = core.nc
    with ExitStack() as ctx:
        m = Mem(nc, ctx, f"gat{i}")
        names = Rows.NAMES + ["adj_in", "adj_free", "xt_done", "xT_ready", "wa_done", "wa_ready", "h_done", "h_ready",
                              "t_done", "s_ready", "masked", "low_ready", "nmax_ready", "prob_ready", "prob_turned",
                              "probT_act", "probT_dve", "pv_done", "x_done", "chain", "wide_set", "s_low", "prep", "leaky"]
        S = {n: m.sem(n) for n in names}
        rows_ = Rows(m, core, S, core.x_res)
        adj_raw = m.sb("adj_raw", [P, T, N], I32)
        mask = [m.sb(f"mask{s}", [P, T, N], BF16) for s in range(2)]
        xT = m.sb("xT", [P, N])
        a_wide = m.sb("a_wide", [P, P])
        wa = m.sb("wa", [P, P + 1])
        h = m.sb("h", [P, T, D])
        s_col, s_low = m.sb("s_col", [P, T]), m.sb("s_low", [P, T])
        tmax, zmax, low, nmax = (m.sb(n, [P, T]) for n in ("tmax", "zmax", "low", "nmax"))
        z = m.sb("z", [P, T, N])
        zlow = m.sb("zlow", [P, T, N])
        total, rinv = m.sb("total", [P, T]), m.sb("rinv", [P, T])
        probT = m.sb("probT", [P, T, T, P])
        y = m.sb("y", [P, T, D])
        upd = m.sb("upd", [P, T, D])
        six, two = m.sb("six", [P, T, 6]), m.sb("two", [P, T, 2])
        tp, h_ps, s_ps, t_ps, o_ps = (m.ps(n) for n in ("tp", "h_ps", "s_ps", "t_ps", "o_ps"))
        tpose = [m.ps(f"tpose{n}") for n in range(2)]
        par = lambda name: core.param(k, name)
        w, wt, a = par(f"gw{i}"), par(f"gwt{i}"), par(f"ga{i}")
        SLOPE = 0.2
        block = ctx.enter_context(nc.Block())

        @block.sync
        def _(sp):
            core.load_params(sp, k + 1)
            adj = core.dram["adj"].rearrange("b (t p) n -> b p t n", p=P)
            sp.dma_start(adj_raw[:, :, :], adj[0]).then_inc(S["adj_in"], 16)
            with sp.Fori(1, B) as b:
                sp.wait_ge(S["adj_free"], b)
                sp.dma_start(adj_raw[:, :, :], adj[b]).then_inc(S["adj_in"], 16)

        @block.gpsimd
        def _(pool):
            rows_.scales(pool, core.x_stat, LN_EPS)

            def graph(b, s):
                rows_.normalise(pool, b, s)
                pool.wait_ge(S["adj_in"], 16 * (b + 1))
                pool.wait_ge(S["x_done"], b + 1)
                apart(pool, core)
                pool.tensor_scalar(mask[s][:, :, :], adj_raw[:, :, :], 0.0, -BIG, ALU.is_le if i == 2 else ALU.is_equal,
                                   ALU.mult).then_inc(S["adj_free"], 1)

            pairs(pool, graph)

        @block.tensor
        def _(pe):
            pe.sem_inc(S["xn_free"], 2)
            pe.sem_inc(S["pv_done"], 1)
            pe.wait_ge(core.params_in[k], 16)
            pe.wait_ge(S["wide_set"], 1)
            pe.matmul(s_ps[:, 0:P], wt, a_wide[:, :], start=True, stop=True).then_inc(S["wa_done"], 1)
            pe.matmul(t_ps[:, 0:1], wt, a[:, 0:1], start=True, stop=True).then_inc(S["wa_done"], 1)
            pe.wait_ge(S["wa_ready"], 2)

            def graph(b, s):
                pe.wait_ge(S["xn_ready"], b + 1)
                turn(pe, core, tp, rows_.xn[s]).then_inc(S["xn_free"], 1)
                pe.wait_ge(S["xT_ready"], b + 1)
                pe.matmul(t_ps[:, :], wa[:, 0:P], xT[:, :], start=True, stop=True).then_inc(S["t_done"], 1)
                for t in range(T):
                    last = pe.matmul(s_ps[:, t:t + 1], xT[:, t * P:(t + 1) * P], wa[:, P:P + 1], start=True, stop=True)
                last.then_inc(S["t_done"], 1)
                for t in range(T):
                    last = pe.matmul(h_ps[:, t * D:(t + 1) * D], xT[:, t * P:(t + 1) * P], w, start=True, stop=True)
                last.then_inc(S["h_done"], 1)
                for t in range(T):
                    pe.wait_ge(S["prob_ready"], T * b + t + 1)
                    pe.wait_ge(S["probT_act"] if t % 2 == 0 else S["probT_dve"], 2 * b + t // 2 + 1)
                    for u in range(T):
                        last = pe.transpose(tpose[t % 2][:, u * P:(u + 1) * P], zlow[:, t, u * P:(u + 1) * P],
                                            core.ident[:, :])
                    last.then_inc(S["prob_turned"], 1)
                    if t >= 1:
                        values(b, t - 1)
                values(b, T - 1)

            def values(b, t):
                if t == 0:
                    pe.wait_ge(S["h_ready"], b + 1)
                pe.wait_ge(S["probT_act"] if t % 2 == 0 else S["probT_dve"], 2 * b + t // 2 + 2)
                for u in range(T):
                    last = pe.matmul(o_ps[:, t * D:(t + 1) * D], probT[:, t, u, :], h[:, u, :],
                                     start=(u == 0), stop=(u == T - 1))
                if t == T - 1:
                    last.then_inc(S["pv_done"], 1)

            pairs(pe, graph)

        @block.scalar
        def _(act):
            act.sem_inc(S["probT_act"], 1)
            act.wait_ge(S["wa_done"], 2)
            act.copy(wa[:, 0:P], s_ps[:, 0:P]).then_inc(S["wa_ready"], 1)
            act.copy(wa[:, P:P + 1], t_ps[:, 0:1]).then_inc(S["wa_ready"], 1)

            def graph(b, s):
                act.wait_ge(S["xn_free"], b + 1 + 2)
                act.copy(xT[:, :], tp[:, :]).then_inc(S["xT_ready"], 1)
                act.wait_ge(S["t_done"], 2 * (b + 1))
                act.copy(s_col[:, :], s_ps[:, 0:T]).then_inc(S["s_ready"], 1)
                act.mul(s_low[:, :], s_ps[:, 0:T], SLOPE).then_inc(S["s_low"], 1)
                act.wait_ge(S["h_done"], b + 1)
                act.copy(flat(h[:, :, :]), h_ps[:, :]).then_inc(S["h_ready"], 1)
                act.wait_ge(S["s_low"], b + 1)
                for t in range(T):
                    act.wait_ge(S["masked"], T * b + t + 1)
                    act.activation(zlow[:, t, :], z[:, t, :], ACT.Identity, bias=s_low[:, t:t + 1], scale=SLOPE)\
                        .then_inc(S["low_ready"], 1)
                for t in range(T):
                    act.wait_ge(S["leaky"], T * b + t + 1)
                    act.activation(zlow[:, t, :], z[:, t, :], ACT.Exp, bias=nmax[:, t:t + 1],
                                   accum_out=total[:, t:t + 1]).then_inc(S["prob_ready"], 1)
                    if t % 2 == 1:
                        copy_probT(b, t - 1)

            def copy_probT(b, t):
                act.wait_ge(S["prob_turned"], T * b + t + 1)
                if t == 0:
                    act.wait_ge(S["pv_done"], b + 1)
                act.copy(probT[:, t, :, :].rearrange("p u q -> p (u q)"), tpose[t % 2][:, :]).then_inc(S["probT_act"], 1)

            pairs(act, graph)

        @block.vector
        def _(dve):
            dve.sem_inc(S["probT_dve"], 1)
            dve.sem_inc(S["x_done"], 2)
            dve.wait_ge(core.params_in[k], 16)
            dve.tensor_copy(a_wide[:, :], a[:, 1:2].broadcast_to([P, P])).then_inc(S["wide_set"], 1)
            STEPS = 3 + 1 + T + 2 * T + 1

            def graph(b, s):
                chain = Chain(dve, S["chain"], b * STEPS)
                dve.wait_ge(S["t_done"], 2 * b + 1)
                dve.wait_ge(S["adj_free"], b + 1)
                apart(dve, core)
                for t in range(T):
                    dve.tensor_tensor_reduce(z[:, t, :], t_ps[:, :], mask[s][:, t, :], 1.0, -3e38, ALU.add, ALU.max,
                                             tmax[:, t:t + 1]).then_inc(S["masked"], 1)
                dve.wait_ge(S["s_ready"], b + 1)
                dve.wait_ge(S["masked"], T * (b + 1))
                chain.step(dve.tensor_tensor(zmax[:, :], tmax[:, :], s_col[:, :], ALU.add))
                chain.settle()
                chain.step(dve.scalar_tensor_tensor(low[:, :], zmax[:, :], SLOPE, zmax[:, :], ALU.mult, ALU.max))
                chain.settle()
                chain.step(dve.tensor_scalar(nmax[:, :], low[:, :], -1.0, None, ALU.mult))
                chain.settle()
                for t in range(T):
                    dve.wait_ge(S["low_ready"], T * b + t + 1)
                    dve.scalar_tensor_tensor(z[:, t, :], z[:, t, :], s_col[:, t:t + 1], zlow[:, t, :], ALU.add, ALU.max)\
                        .then_inc(S["leaky"], 1)
                for t in (1, 3):
                    dve.wait_ge(S["prob_turned"], T * b + t + 1)
                    if t == 1:
                        dve.wait_ge(S["pv_done"], b + 1)
                    dve.tensor_copy(probT[:, t, :, :].rearrange("p u q -> p (u q)"), tpose[1][:, :])\
                        .then_inc(S["probT_dve"], 1)
                dve.wait_ge(S["prob_ready"], T * (b + 1))
                chain.step(dve.reciprocal(rinv[:, :], total[:, :]))
                chain.settle()
                dve.wait_ge(S["pv_done"], b + 1 + 1)
                for t in range(T):
                    chain.step(dve.scalar_tensor_tensor(upd[:, t, :], o_ps[:, t * D:(t + 1) * D], rinv[:, t:t + 1],
                                                        core.x_res[:, b, t, :], ALU.mult, ALU.add))
                chain.settle()
                apart(dve, core)
                chain.step(dve.tensor_copy(core.x_res[:, b], upd[:, :, :]))
                row_stats(dve, chain, core, six, two, upd)
                chain.settle()
                apart(dve, core)
                dve.tensor_copy(core.x_stat[:, b], two[:, :, :]).then_inc(S["x_done"], 1)
                assert chain.n == STEPS, (chain.n, STEPS)

            pairs(dve, graph)


E_ = 8
TOP = 2


def prep_stage(core, k, kind):
    nc = core.nc
    renorm, router = "renorm" in kind, "router" in kind
    tag = f"prep{k}"
    R = B * T
    with ExitStack() as ctx:
        m = Mem(nc, ctx, tag)
        names = Rows.NAMES + ["saved", "xt_done", "xT_ready", "logit_done", "logit_taken", "chain", "gate_chain",
                              "low_ready", "exp_ready", "tri_zero", "tri_set"]
        S = {n: m.sem(n) for n in names}
        rows_ = Rows(m, core, S, core.x_res if renorm else core.mid, shifted=renorm)
        xT = [m.sb(f"xT{s}", [P, N]) for s in range(2)]
        six, two = m.sb("six", [P, T, 6]), m.sb("two", [P, T, 2])
        tp = [m.ps(f"tp{s}") for s in range(2)]
        lg = [m.ps(f"lg{s}") for s in range(2)]
        if router:
            logits = m.sb("logits", [P, R, E_])
            prob = m.sb("prob", [P, R, E_])
            above, ties = m.sb("above", [P, R, E_, E_], BF16), m.sb("ties", [P, R, E_, E_], BF16)
            order = m.sb("order", [P, E_, E_], BF16)
            rank = m.sb("rank", [P, R, E_])
            row = [m.sb(f"row{i}", [P, R]) for i in range(5)]
            w_router = core.param(k, "er" if renorm else "hr")
        block = ctx.enter_context(nc.Block())

        @block.gpsimd
        def _(pool):
            rows_.scales(pool, core.x_stat, LN_EPS if renorm else 1e-6)
            if router:
                pool.memset(order[:, :, :], 1.0).then_inc(S["tri_zero"], 1)
                pool.wait_ge(S["tri_zero"], 1)
                pool.affine_select(out=order[:, :, :], in_=order[:, :, :], compare_op=ALU.is_gt, fill=0.0, base=0,
                                   pattern=[[1, E_], [-1, E_]], channel_multiplier=0).then_inc(S["tri_set"], 1)
            pairs(pool, lambda b, s: rows_.normalise(pool, b, s))

        @block.tensor
        def _(pe):
            if not router:
                return
            pe.wait_ge(core.params_in[k], 16)

            def graph(b, s):
                pe.wait_ge(S["xn_ready"], b + 1)
                turn(pe, core, tp[s], rows_.xn[s]).then_inc(S["xt_done"], 1)
                pe.wait_ge(S["xT_ready"], b + 1)
                pe.wait_ge(S["logit_taken"], b + 1)
                for t in range(T):
                    last = pe.matmul(lg[s][:, t * E_:(t + 1) * E_], xT[s][:, t * P:(t + 1) * P], w_router,
                                     start=True, stop=True)
                last.then_inc(S["logit_done"], 1)

            pairs(pe, graph)

        @block.scalar
        def _(act):
            act.sem_inc(S["saved"], 2)
            if router:
                act.wait_ge(core.params_in[k], 16)

            def graph(b, s):
                if renorm:
                    act.wait_ge(S["xn_ready"], b + 1)
                    act.copy(core.mid[:, b], rows_.xn[s][:, :, :]).then_inc(S["saved"], 1)
                if router:
                    act.wait_ge(S["xt_done"], b + 1)
                    if renorm:
                        ins = act.copy(xT[s][:, :], tp[s][:, :])
                    else:
                        ins = act.activation(xT[s][:, :], tp[s][:, :], ACT.Identity, scale=core.param(k, "ln2w"))
                    ins.then_inc(S["xT_ready"], 1)

            pairs(act, graph)
            if router:
                act.wait_ge(S["low_ready"], 1)
                act.activation(logits[:, :, :], logits[:, :, :], ACT.Exp).then_inc(S["exp_ready"], 1)

        @block.vector
        def _(dve):
            dve.sem_inc(S["xn_free"], 2)
            dve.sem_inc(S["logit_taken"], 2)
            if router:
                dve.wait_ge(core.params_in[k], 16)
                dve.wait_ge(S["tri_set"], 1)

            def graph(b, s):
                chain = Chain(dve, S["chain"], b * STEPS)
                if renorm:
                    dve.wait_ge(S["xn_ready"], b + 1)
                    row_stats(dve, chain, core, six, two, rows_.xn[s])
                    chain.settle()
                    apart(dve, core)
                    chain.step(dve.tensor_copy(core.stat2[:, b], two[:, :, :]))
                    dve.wait_ge(S["saved"], b + 1 + 2)
                if router:
                    dve.wait_ge(S["logit_done"], b + 1)
                    apart(dve, core)
                    out = logits[:, bass.ds(b * T, T), :]
                    got = lg[s][:, 0:T * E_].rearrange("p (t e) -> p t e", t=T)
                    if renorm:
                        ins = dve.tensor_tensor(out, got, core.param(k, "ebr").unsqueeze(1).broadcast_to([P, T, E_]), ALU.add)
                    else:
                        ins = dve.tensor_copy(out, got)
                    ins.then_inc(S["logit_taken"], 1)
                chain.settle() if chain.n else None
                dve.sem_inc(S["xn_free"], 1)

            STEPS = 2 * T + 1 if renorm else 0
            pairs(dve, graph)
            if not router:
                return
            g = Chain(dve, S["gate_chain"])
            dve.wait_ge(S["logit_taken"], B + 2)
            top, total, inv, kept, inv2 = (r[:, :] for r in row)
            wide = lambda ap: ap.unsqueeze(2).broadcast_to([P, R, E_])
            g.step(dve.tensor_reduce(top, logits[:, :, :], AX.X, ALU.max))
            g.settle()
            dve.tensor_tensor(logits[:, :, :], logits[:, :, :], wide(top), ALU.subtract).then_inc(S["low_ready"], 1)
            dve.wait_ge(S["exp_ready"], 1)
            g.step(dve.tensor_reduce(total, logits[:, :, :], AX.X, ALU.add))
            g.settle()
            g.step(dve.reciprocal(inv, total))
            g.settle()
            g.step(dve.tensor_tensor(prob[:, :, :], logits[:, :, :], wide(inv), ALU.mult))
            g.settle()
            other = prob[:, :, :].unsqueeze(2).broadcast_to([P, R, E_, E_])
            own = prob[:, :, :].unsqueeze(3).broadcast_to([P, R, E_, E_])
            g.step(dve.tensor_tensor(above[:, :, :, :], other, own, ALU.is_gt))
            g.step(dve.tensor_tensor(ties[:, :, :, :], other, own, ALU.is_ge))
            g.settle()
            g.step(dve.tensor_tensor(ties[:, :, :, :], ties[:, :, :, :],
                                     order[:, :, :].unsqueeze(1).broadcast_to([P, R, E_, E_]), ALU.mult))
            g.settle()
            g.step(dve.tensor_tensor(above[:, :, :, :], above[:, :, :, :], ties[:, :, :, :], ALU.max))
            g.settle()
            g.step(dve.tensor_reduce(rank[:, :, :], above[:, :, :, :], AX.X, ALU.add))
            g.settle()
            g.step(dve.scalar_tensor_tensor(prob[:, :, :], rank[:, :, :], float(TOP), prob[:, :, :], ALU.is_lt, ALU.mult))
            g.settle()
            g.step(dve.tensor_reduce(kept, prob[:, :, :], AX.X, ALU.add))
            g.settle()
            if not renorm:
                g.step(dve.tensor_scalar(kept, kept, 1e-9, None, ALU.add))
                g.settle()
            g.step(dve.reciprocal(inv2, kept))
            g.settle()
            g.step(dve.tensor_tensor(core.gate[:, :, :, :].rearrange("p b t e -> p (b t) e"), prob[:, :, :], wide(inv2), ALU.mult))
            g.settle()


def moe_stage(core, k, swiglu, store=False):
    nc = core.nc
    if swiglu:
        FULL = 341
        WID = [P, P, FULL - 2 * P]
    else:
        FULL = 512
        WID = [P] * 4
    HT = len(WID)
    with ExitStack() as ctx:
        m = Mem(nc, ctx, f"moe{k}")
        names = Rows.NAMES + ["xT_ready", "hid_done", "hid_read", "out_done", "combined", "gate_ready", "b1_done",
                              "w1_ready", "b1_ready", "gT_done", "gT_ready", "bias_done", "chain", "x_chain", "silu_ready",
                              "acc_init", "stored"]
        S = {n: m.sem(n) for n in names}
        rows_ = Rows(m, core, S, core.mid, shifted=not swiglu)
        xT = [m.sb(f"xT{s}", [P, N]) for s in range(2)]
        hid = [m.sb(f"hid{s}", [P, HT, N]) for s in range(2)]
        gate = m.sb("gate", [P, T, E_])
        acc = m.sb("acc", [P, T, D])
        upd = m.sb("upd", [P, T, D])
        six, two = m.sb("six", [P, T, 6]), m.sb("two", [P, T, 2])
        tp, gb = m.ps("tp"), m.ps("gb")
        hid_ps = [m.ps(f"hid_ps{i}") for i in range(4)]
        out_ps = [m.ps(f"out_ps{s}") for s in range(2)]
        par = lambda name: core.param(k, name)
        if swiglu:
            silu = [m.sb(f"silu{i}", [P, N]) for i in range(2)]
        else:
            b1 = m.sb("b1", [P, E_ * HT])
            gT = m.sb("gT", [E_, N])
        PAIRS = 2 if swiglu else 4
        block = ctx.enter_context(nc.Block())

        @block.sync
        def _(sp):
            core.load_params(sp, k + 1)
            if store:
                with sp.Fori(0, B) as b:
                    sp.wait_ge(S["x_chain"], b + 1)
                    sp.dma_start(core.dram["out"][b].rearrange("(t p) d -> p t d", p=P), core.x_res[:, b])\
                        .then_inc(S["stored"], 16)
                sp.wait_ge(S["stored"], 16 * B)

        @block.gpsimd
        def _(pool):
            rows_.scales(pool, core.x_stat if swiglu else core.stat2, 1e-6 if swiglu else LN_EPS)
            pairs(pool, lambda b, s: rows_.normalise(pool, b, s))

        @block.tensor
        def _(pe):
            pe.sem_inc(S["xn_free"], 2)
            pe.wait_ge(core.params_in[k], 16)
            if not swiglu:
                for e in range(E_):
                    for n in range(HT):
                        last = pe.matmul(gb[:, e * HT + n:e * HT + n + 1], par("ew1")[:, e * FULL + n * P:e * FULL + (n + 1) * P],
                                         par("ebt")[:, e:e + 1], start=True, stop=True)
                last.then_inc(S["b1_done"], 1)

            def front(b, s):
                pe.wait_ge(S["xn_ready"], b + 1)
                turn(pe, core, tp, rows_.xn[s]).then_inc(S["xn_free"], 1)

            def hidden(b, s, e):
                if e == 0:
                    pe.wait_ge(S["xT_ready"], b + 1)
                for n, wid in enumerate(WID):
                    i = e * HT + n
                    pe.wait_ge(S["hid_read"], E_ * HT * b + i + 1)
                    col = e * FULL + n * P
                    if swiglu:
                        pe.matmul(hid_ps[2 * (i % 2)][0:wid, :], par("hw1")[:, col:col + wid], xT[s][:, :], start=True, stop=True)\
                            .then_inc(S["hid_done"], 1)
                        pe.matmul(hid_ps[2 * (i % 2) + 1][0:wid, :], par("hw3")[:, col:col + wid], xT[s][:, :], start=True, stop=True)\
                            .then_inc(S["hid_done"], 1)
                    else:
                        pe.matmul(hid_ps[i % 4][:, :], par("ew1")[:, col:col + wid], xT[s][:, :], start=True, stop=True)\
                            .then_inc(S["hid_done"], 1)

            def output(b, e):
                pe.wait_ge(S["combined"], E_ * b + e + 1)
                pe.wait_ge(S["hid_read"], HT * (E_ * b + e + 1) + PAIRS)
                w2 = par("hw2" if swiglu else "ew2")
                for t in range(T):
                    for n, wid in enumerate(WID):
                        last = pe.matmul(out_ps[e % 2][:, t * D:(t + 1) * D], hid[e % 2][0:wid, n, t * P:(t + 1) * P],
                                         w2[0:wid, (e * HT + n) * D:(e * HT + n + 1) * D], start=(n == 0), stop=(n == HT - 1))
                last.then_inc(S["out_done"], 1)

            def graph(b, s, last=False):
                for e in range(E_):
                    if e == 0 and not swiglu:
                        pe.wait_ge(S["gate_ready"], b + 1)
                        for t in range(T):
                            ins = pe.transpose(tp[0:E_, t * P:(t + 1) * P], gate[:, t, :], core.ident[:, :])
                        ins.then_inc(S["gT_done"], 1)
                    if e < E_ - 1:
                        hidden(b, s, e + 1)
                    elif not last:
                        hidden(b + 1, 1 - s, 0)
                    if e == 0 and not swiglu:
                        pe.wait_ge(S["gT_ready"], b + 1)
                        for t in range(T):
                            ins = pe.matmul(gb[:, t * D:(t + 1) * D], gT[:, t * P:(t + 1) * P], par("eb2")[0:E_, :],
                                            start=True, stop=True)
                        ins.then_inc(S["bias_done"], 1)
                    if e == 3 and not last:
                        front(b + 1, 1 - s)
                    output(b, e)

            front(0, 0)
            if not swiglu:
                pe.wait_ge(S["w1_ready"], E_)
            hidden(0, 0, 0)
            pairs(pe, graph, 0, B - 2)
            graph(B - 2, 0)
            graph(B - 1, 1, last=True)

        @block.scalar
        def _(act):
            act.wait_ge(core.params_in[k], 16)
            if not swiglu:
                act.sem_inc(S["hid_read"], PAIRS)
                act.wait_ge(S["b1_ready"], 1)

            def front(b, s):
                act.wait_ge(S["xn_free"], b + 1 + 2)
                if swiglu:
                    ins = act.activation(xT[s][:, :], tp[:, :], ACT.Identity, scale=par("ln2w"))
                else:
                    ins = act.copy(xT[s][:, :], tp[:, :])
                ins.then_inc(S["xT_ready"], 1)

            def hidden(b, e):
                for n, wid in enumerate(WID):
                    i = e * HT + n
                    if swiglu:
                        act.wait_ge(S["hid_done"], 2 * (E_ * HT * b + i) + 1)
                        act.activation(silu[i % 2][0:wid, :], hid_ps[2 * (i % 2)][0:wid, :], ACT.Silu).then_inc(S["silu_ready"], 1)
                    else:
                        act.wait_ge(S["hid_done"], E_ * HT * b + i + 1)
                        act.activation(hid[e % 2][:, n, :], hid_ps[i % 4][:, :], ACT.Gelu, bias=b1[:, i:i + 1])\
                            .then_inc(S["hid_read"], 1)

            def graph(b, s, last=False):
                for e in range(E_):
                    if e == 0 and not swiglu:
                        act.wait_ge(S["gT_done"], b + 1)
                        act.copy(gT[:, :], tp[0:E_, :]).then_inc(S["gT_ready"], 1)
                    if e < E_ - 1:
                        hidden(b, e + 1)
                    elif not last:
                        hidden(b + 1, 0)
                    if e == 3 and not last:
                        front(b + 1, 1 - s)

            front(0, 0)
            hidden(0, 0)
            pairs(act, graph, 0, B - 2)
            graph(B - 2, 0)
            graph(B - 1, 1, last=True)

        @block.vector
        def _(dve):
            dve.sem_inc(S["combined"], 2)
            dve.wait_ge(core.params_in[k], 16)
            if swiglu:
                dve.sem_inc(S["hid_read"], PAIRS)
            else:
                dve.wait_ge(S["b1_done"], 1)
                dve.tensor_tensor(b1[:, :], gb[:, 0:E_ * HT], par("eb1"), ALU.add).then_inc(S["b1_ready"], 1)
                for e in range(E_):
                    w1 = par("ew1")[:, e * FULL:(e + 1) * FULL]
                    dve.tensor_scalar(w1, w1, par("eg")[:, e:e + 1], None, ALU.mult).then_inc(S["w1_ready"], 1)

            def product(b, e):
                for n, wid in enumerate(WID):
                    i = e * HT + n
                    dve.wait_ge(S["silu_ready"], E_ * HT * b + i + 1)
                    dve.wait_ge(S["hid_done"], 2 * (E_ * HT * b + i) + 2)
                    dve.tensor_tensor(hid[e % 2][0:wid, n, :], hid_ps[2 * (i % 2) + 1][0:wid, :], silu[i % 2][0:wid, :],
                                      ALU.mult).then_inc(S["hid_read"], 1)

            def graph(b, s, last=False):
                chain = Chain(dve, S["chain"], b * STEPS)
                dve.tensor_copy(gate[:, :, :], core.gate[:, b]).then_inc(S["gate_ready"], 1)
                if not swiglu:
                    dve.wait_ge(S["bias_done"], b + 1)
                    dve.tensor_copy(flat(acc[:, :, :]), gb[:, :]).then_inc(S["acc_init"], 1)
                    dve.wait_ge(S["acc_init"], b + 1)
                dve.wait_ge(S["gate_ready"], b + 1)
                for e in range(E_):
                    if swiglu:
                        if e < E_ - 1:
                            product(b, e + 1)
                        elif not last:
                            product(b + 1, 0)
                    dve.wait_ge(S["out_done"], E_ * b + e + 1)
                    for t in range(T):
                        before = core.mid[:, b, t, :] if e == 0 and swiglu else acc[:, t, :]
                        ins = dve.scalar_tensor_tensor(acc[:, t, :], out_ps[e % 2][:, t * D:(t + 1) * D], gate[:, t, e:e + 1],
                                                       before, ALU.mult, ALU.add)
                        if t < T - 1:
                            chain.step(ins)
                    ins.then_inc(S["combined"], 1)
                    chain.settle()
                    dve.wait_ge(S["combined"], E_ * b + e + 1 + 2)
                if store:
                    dve.tensor_tensor(core.x_res[:, b], acc[:, :, :], core.x_res[:, b], ALU.add).then_inc(S["x_chain"], 1)
                    dve.wait_ge(S["x_chain"], b + 1)
                else:
                    write_x(dve, chain, core, b, acc[:, :, :], core.x_res[:, b], upd, six, two)
                assert chain.n == STEPS, (chain.n, STEPS)

            STEPS = E_ * (T - 1) + (0 if store else WRITE_STEPS)
            if swiglu:
                product(0, 0)
            pairs(dve, graph, 0, B - 2)
            graph(B - 2, 0)
            graph(B - 1, 1, last=True)


def program(core):
    load_stage(core)
    mha_stage(core, 0, "mha0", 8, 16, 2, 0.25, core.x_res)
    lstm_stage(core, 1)
    mha_stage(core, 2, "mha1", 8, 16, 2, 0.25, core.mid, sym=True, from_xn=True)
    ffn1_stage(core, 3)
    mod_stage(core, 4)
    gat_stage(core, 5, 2)
    prep_stage(core, 6, "renorm+router")
    moe_stage(core, 6, False)
    gat_stage(core, 7, 3)
    prep_stage(core, 8, "renorm")
    mha_stage(core, 8, "mha3", 4, 32, 1, 32 ** -0.5, core.mid, rope=True)
    prep_stage(core, 9, "router")
    moe_stage(core, 9, True, store=True)


def columns(a):
    out = np.zeros((P, a.shape[1]), np.float32)
    out[:a.shape[0]] = a
    return out


def rows(v):
    return np.broadcast_to(v.reshape(1, -1), (P, v.size))


def head_columns(w, heads, dim, groups):
    out = np.zeros((P, groups, 4, 32), np.float32)
    out[..., :dim] = w.T.reshape(P, groups, 4, dim)
    return out.reshape(P, groups * P)


def head_bias(v, dim, groups):
    out = np.zeros((4, 32, groups), np.float32)
    out[:, :dim] = v.reshape(groups, 4, dim).transpose(1, 2, 0)
    return out.reshape(P, groups)


def hidden_rows(w):
    return w.reshape(-1, P, w.shape[1]).transpose(1, 0, 2).reshape(P, -1)


def half_turned(w):
    return w.reshape(P, 4, 2, 16)[:, :, ::-1].reshape(P, P)


def rope_tables():
    inv_freq = 1.0 / 10000.0 ** (np.arange(0, 32, 2, dtype=np.float32) / 32)
    freqs = np.outer(np.arange(N, dtype=np.float32), inv_freq)
    cos, sin = np.cos(freqs).T.astype(np.float32), np.sin(freqs).T.astype(np.float32)
    return np.tile(np.concatenate([cos, cos]), (4, 1)), np.tile(np.concatenate([-sin, sin]), (4, 1))


def pack(a):
    w = {}
    qkv, bqkv = a["L1_gnn_Wqkv"], a["L1_gnn_bqkv"]
    for tag, ws, bs, wo, bo in (
        ("0", [a["L0_gnn_W" + c] for c in "qkv"], [a["L0_gnn_b" + c] for c in "qkv"], a["L0_gnn_Wo"], a["L0_gnn_bo"]),
        ("1", [qkv[i * D:(i + 1) * D] for i in range(3)], [bqkv[i * D:(i + 1) * D] for i in range(3)], a["L1_gnn_Wo"], a["L1_gnn_bo"]),
    ):
        w["wq" + tag], w["wk" + tag] = (head_columns(x, 8, 16, 2) for x in ws[:2])
        w["bq" + tag], w["bk" + tag] = (head_bias(x, 16, 2) for x in bs[:2])
        w["wv" + tag], w["bv" + tag], w["wo" + tag], w["bo" + tag] = ws[2].T, rows(bs[2]), wo.T, rows(bo)
    w["w_ih"], w["w_hh"] = a["L0_ffn_W_ih"].T, a["L0_ffn_W_hh"].T
    w["b_ih"], w["b_hh"] = a["L0_ffn_b_ih"].reshape(4, P).T, a["L0_ffn_b_hh"].reshape(4, P).T
    w["w_lin"] = np.repeat(a["L0_ffn_W_lin"].T, P, axis=1)
    w["b_lin"] = rows(a["L0_ffn_b_lin"])
    w["fw"], w["bw"] = a["L0_ffn_fw_att"].T, a["L0_ffn_bw_att"].T
    w["f1w1"] = a["L1_gnn_W1"].T
    w["f1w2"] = hidden_rows(a["L1_gnn_W2"].T)
    w["f1b1"] = a["L1_gnn_b1"].reshape(4, P).T
    w["f1b2"], w["g1"], w["be1"], w["g2"], w["be2"] = (rows(a["L1_gnn_" + n]) for n in ("b2", "ln1_g", "ln1_b", "ln2_g", "ln2_b"))
    w["mw1"], w["mw2"], w["mb1"] = a["L1_ffn_w1"], hidden_rows(a["L1_ffn_w2"]), a["L1_ffn_b1"].reshape(4, P).T
    w["mb2"], w["mwr"], w["mbr"] = rows(a["L1_ffn_b2"]), a["L1_ffn_wr"], rows(a["L1_ffn_br"])
    w["gw2"], w["gwt2"], w["ga2"] = a["L2_gnn_W"], a["L2_gnn_W"].T, a["L2_gnn_a"].reshape(2, P).T
    w["gw3"], w["gwt3"], w["ga3"] = a["L3_gnn_W"].T, a["L3_gnn_W"], a["L3_gnn_a"].reshape(2, P).T
    w["ew1"] = a["L2_ffn_W1"].transpose(1, 0, 2).reshape(D, -1)
    w["ew2"] = hidden_rows(a["L2_ffn_W2"].reshape(-1, D))
    w["eb1"] = a["L2_ffn_b1"].reshape(-1, P).T
    w["eb2"] = columns(a["L2_ffn_b2"])
    w["eg"], w["ebt"], w["er"], w["ebr"] = a["L2_ffn_ln_g"].T, a["L2_ffn_ln_b"].T, a["L2_ffn_Wr"], rows(a["L2_ffn_br"])
    w["wq3"], w["wqr3"] = a["L3_ffn_wq"].T, half_turned(a["L3_ffn_wq"].T)
    both = lambda v: np.repeat(v.T.reshape(P, 2, 32), 2, axis=1).reshape(P, P)
    w["wk3"], w["wkr3"], w["wv3"] = both(a["L3_ffn_wk"]), half_turned(both(a["L3_ffn_wk"])), both(a["L3_ffn_wv"])
    w["wo3"], w["ln1w"], w["ln2w"] = a["L3_ffn_wo"].T, a["L3_ffn_ln1_w"].reshape(P, 1), a["L3_ffn_ln2_w"].reshape(P, 1)
    w["cos"], w["sin"] = rope_tables()
    w["hw1"] = a["L3_ffn_w1"].transpose(2, 0, 1).reshape(D, -1)
    w["hw3"] = a["L3_ffn_w3"].transpose(2, 0, 1).reshape(D, -1)
    padded = np.zeros((8, 3 * P, D), np.float32)
    padded[:, :341] = a["L3_ffn_w2"].transpose(0, 2, 1)
    w["hw2"] = hidden_rows(padded.reshape(-1, D))
    w["hr"] = a["L3_ffn_router_w"].T
    out = np.zeros((P, COLUMNS), np.float32)
    for name, (at, n) in PLACE.items():
        out[:, at:at + n] = w[name]
    return out


def kernel(**inputs):
    import concourse.bacc as _bacc
    from concourse.bass_utils import run_bass_kernel_spmd as _run

    a = {name: np.asarray(v) for name, v in inputs.items()}
    sent = {"x": np.ascontiguousarray(a["x"]), "adj": np.ascontiguousarray(a["adj"]), "weights": pack(a)}
    nc = _bacc.Bacc("TRN2", target_bir_lowering=False, num_devices=1)
    dram = {n: nc.dram_tensor(n, v.shape, mybir.dt.from_np(v.dtype), kind="ExternalInput").ap() for n, v in sent.items()}
    dram["out"] = nc.dram_tensor("out", (B, N, D), F32, kind="ExternalOutput").ap()
    with ExitStack() as ctx:
        program(Core(nc, ctx, dram))
    r = _run(nc, [sent], core_ids=[0])
    return r.results[0]["out"]
```

```python
from contextlib import ExitStack

import numpy as np

import concourse.bass as bass
from concourse import mybir

F32 = mybir.dt.float32
BF16 = mybir.dt.bfloat16
I32 = mybir.dt.int32
ALU = mybir.AluOpType
ACT = mybir.ActivationFunctionType
AX = mybir.AxisListType

P = 128
B = 16
N = 512
D = 128
T = N // P
BIG = 1e30
LN_EPS = 1e-5


class Mem:

    def __init__(self, nc, ctx, tag):
        self.nc, self.ctx, self.tag, self.sems = nc, ctx, tag, []
        ctx.callback(self.clear)

    def sb(self, name, shape, dt=F32):
        return self.ctx.enter_context(self.nc.sbuf_tensor(f"{self.tag}_{name}", shape, dt))

    def ps(self, name, shape=(P, 512), dt=F32):
        return self.ctx.enter_context(self.nc.psum_tensor(f"{self.tag}_{name}", list(shape), dt))

    def sem(self, name):
        self.sems.append(self.ctx.enter_context(self.nc.semaphore(f"{self.tag}_{name}")))
        return self.sems[-1]

    def clear(self):
        numbers = sorted(sem.num for sem in self.sems)
        first = min(numbers, default=0)
        for n, after in zip(numbers, numbers[1:] + [None]):
            if after != n + 1:
                self.nc.gpsimd.sem_clear(range(first, n + 1))
                first = after
        self.nc.all_engine_barrier()


class Chain:

    def __init__(self, engine, sem, base=0):
        self.engine, self.sem, self.base, self.n = engine, sem, base, 0

    def step(self, ins):
        ins.then_inc(self.sem, 1)
        self.n += 1

    def settle(self):
        self.engine.wait_ge(self.sem, self.base + self.n)


class Core:

    def __init__(self, nc, ctx, dram):
        m = Mem(nc, ctx, "core")
        self.nc, self.dram = nc, dram
        self.x_res = m.sb("x_res", [P, B, T, D])
        self.mid = m.sb("mid", [P, B, T, D])
        self.x_stat = m.sb("x_stat", [P, B, T, 2])
        self.stat2 = m.sb("stat2", [P, B, T, 2])
        self.gate = m.sb("gate", [P, B, T, 8])
        self.ident = m.sb("ident", [P, P])
        self.ident_bf = m.sb("ident_bf", [P, P], BF16)
        self.passed = {nc.vector.engine: m.sem("passed_dve"), nc.gpsimd.engine: m.sem("passed_pool")}
        self.params = [m.sb(f"params{i}", [P, w]) for i, w in enumerate(REGION)]
        self.params_in = [m.sem(f"params_in{k}") for k in range(len(STAGES))]

    def load_params(self, sp, k):
        if k == len(SPAN):
            return
        lo, hi = SPAN[k]
        sp.dma_start(self.params[k % 2][:, 0:hi - lo], self.dram["weights"][:, lo:hi]).then_inc(self.params_in[k], 16)

    def param(self, k, name):
        lo, n = PLACE[name]
        return self.params[k % 2][:, lo - SPAN[k][0]:lo - SPAN[k][0] + n]


def apart(engine, core):
    engine.sem_inc(core.passed[engine.engine], 1)


class Spare:

    def __init__(self, core, k):
        self.region, self.at = core.params[k % 2], SPAN[k][1] - SPAN[k][0]

    def sb(self, shape, dt=F32):
        words = int(np.prod(shape[1:])) * (2 if dt == BF16 else 4) // 4
        flat_ap = self.region[:, self.at:self.at + words]
        self.at += words
        assert self.at <= self.region.shape[1]
        if dt != F32:
            flat_ap = flat_ap.bitcast(dt)
        if len(shape) == 2:
            return flat_ap
        return flat_ap.rearrange("p (a b) -> p a b", a=shape[1])


def layout():
    return [
        ("mha0", [("wq0", 256), ("wk0", 256), ("wv0", 128), ("wo0", 128), ("bq0", 2), ("bk0", 2), ("bv0", 128), ("bo0", 128)]),
        ("lstm", [("w_ih", 512), ("w_hh", 512), ("b_ih", 4), ("b_hh", 4), ("w_lin", 256), ("b_lin", 2), ("fw", 1), ("bw", 1)]),
        ("mha1", [("wq1", 256), ("wk1", 256), ("wv1", 128), ("wo1", 128), ("bq1", 2), ("bk1", 2), ("bv1", 128), ("bo1", 128)]),
        ("ffn1", [("f1w1", 512), ("f1w2", 512), ("f1b1", 4), ("f1b2", 128), ("g1", 128), ("be1", 128), ("g2", 128), ("be2", 128)]),
        ("mod", [("mw1", 512), ("mw2", 512), ("mb1", 4), ("mb2", 128), ("mwr", 1), ("mbr", 1)]),
        ("gat2", [("gw2", 128), ("gwt2", 128), ("ga2", 2)]),
        ("moe2", [("ew1", 4096), ("ew2", 4096), ("eb1", 32), ("eb2", 128), ("eg", 8), ("ebt", 8), ("er", 8), ("ebr", 8)]),
        ("gat3", [("gw3", 128), ("gwt3", 128), ("ga3", 2)]),
        ("mha3", [("wq3", 128), ("wqr3", 128), ("wk3", 128), ("wkr3", 128), ("wv3", 128), ("wo3", 128), ("ln1w", 1), ("cos", 512), ("sin", 512)]),
        ("moe3", [("hw1", 8 * 341), ("hw3", 8 * 341), ("hw2", 8 * 3 * 128), ("hr", 8), ("ln2w", 1)]),
    ]


def spans():
    place, span, at = {}, [], 0
    for _, parts in layout():
        start = at
        for name, n in parts:
            place[name] = (at, n)
            at += n
        span.append((start, at))
    return place, span, at


PLACE, SPAN, COLUMNS = spans()
STAGES = [name for name, _ in layout()]
REGION = [max(hi - lo for lo, hi in SPAN[i::2]) for i in range(2)]


def row_stats(dve, chain, core, six, two, tile):
    for t in range(T):
        chain.step(dve.bn_stats(six[:, t, :], tile[:, t, :]))
    chain.settle()
    apart(dve, core)
    for t in range(T):
        chain.step(dve.bn_aggr(two[:, t, :], six[:, t, :]))


WRITE_STEPS = 2 * T + 3


def write_x(dve, chain, core, b, change, base, upd, six, two):
    chain.step(dve.tensor_tensor(upd[:, :, :], change, base, ALU.add))
    chain.settle()
    apart(dve, core)
    chain.step(dve.tensor_copy(core.x_res[:, b], upd[:, :, :]))
    row_stats(dve, chain, core, six, two, upd)
    chain.settle()
    apart(dve, core)
    chain.step(dve.tensor_copy(core.x_stat[:, b], two[:, :, :]))
    chain.settle()


def rsqrt_stats(pool, done, rstd, shift, stat, scratch, half, eps, rms=False):
    pool.memset(half, -0.5).then_inc(done, 1)
    if rms:
        pool.tensor_tensor(shift, stat[:, :, :, 0], stat[:, :, :, 0], ALU.mult).then_inc(done, 1)
        pool.wait_ge(done, 2)
        pool.tensor_tensor(scratch, shift, stat[:, :, :, 1], ALU.add).then_inc(done, 1)
        pool.wait_ge(done, 3)
        pool.tensor_scalar(scratch, scratch, eps, None, ALU.add).then_inc(done, 1)
        pool.wait_ge(done, 4)
        pool.tensor_tensor(rstd, scratch, half, ALU.pow).then_inc(done, 1)
        pool.wait_ge(done, 5)
        return
    pool.tensor_scalar(scratch, stat[:, :, :, 1], eps, None, ALU.add).then_inc(done, 1)
    pool.wait_ge(done, 2)
    pool.tensor_tensor(rstd, scratch, half, ALU.pow).then_inc(done, 1)
    pool.wait_ge(done, 3)
    pool.tensor_tensor(shift, stat[:, :, :, 0], rstd, ALU.mult).then_inc(done, 1)
    pool.wait_ge(done, 4)
    pool.tensor_scalar(shift, shift, -1.0, None, ALU.mult).then_inc(done, 1)
    pool.wait_ge(done, 5)


def over_features(ap):
    return ap.unsqueeze(2).broadcast_to([P, T, D])


def flat(ap):
    return ap.rearrange("p a b -> p (a b)")


def load_stage(core):
    nc = core.nc
    with ExitStack() as ctx:
        m = Mem(nc, ctx, "load")
        six = m.sb("six", [P, T, 6])
        two = m.sb("two", [P, T, 2])
        x_in = [m.sem(f"x_in{b}") for b in range(B)]
        ones_set, ident_set, bf_set, chain_sem = m.sem("ones_set"), m.sem("ident_set"), m.sem("bf_set"), m.sem("chain")
        block = ctx.enter_context(nc.Block())

        @block.sync
        def _(sp):
            for b in range(B):
                sp.dma_start(core.x_res[:, b], core.dram["x"][b].rearrange("(t p) d -> p t d", p=P)).then_inc(x_in[b], 16)
                if b == 0:
                    core.load_params(sp, 0)

        @block.gpsimd
        def _(pool):
            pool.memset(core.ident[:, :], 0.0).then_inc(ones_set, 1)
            pool.wait_ge(ones_set, 1)
            pool.affine_select(out=core.ident[:, :], in_=core.ident[:, :], compare_op=ALU.not_equal, fill=1.0,
                               base=0, pattern=[[-1, P]], channel_multiplier=1).then_inc(ident_set, 1)
            pool.wait_ge(ident_set, 1)
            pool.tensor_copy(core.ident_bf[:, :], core.ident[:, :]).then_inc(bf_set, 1)

        @block.vector
        def _(dve):
            chain = Chain(dve, chain_sem)
            for b in range(B):
                dve.wait_ge(x_in[b], 16)
                row_stats(dve, chain, core, six, two, core.x_res[:, b])
                chain.settle()
                apart(dve, core)
                chain.step(dve.tensor_copy(core.x_stat[:, b], two[:, :, :]))


def all_graphs(engine, graph):
    graph(0, 0, first=True)
    with engine.Fori(0, B // 2 - 1) as j:
        for s in (1, 0):
            graph(j * 2 + 2 - s, s)
    graph(B - 1, 1, last=True)


def mha_stage(core, k, tag, heads, head_dim, groups, scale, out_res, sym=False, rope=False, from_xn=False):
    nc = core.nc
    with ExitStack() as ctx:
        m = Mem(nc, ctx, tag)
        items = 4 * T * groups
        rstd, shift = m.sb("rstd", [P, B, T]), m.sb("shift", [P, B, T])
        scratch, half = m.sb("scratch", [P, B, T]), m.sb("half", [P, B, T])
        spare = Spare(core, k)
        adj_raw = None if rope else spare.sb([P, T, N], I32)
        mask = [m.sb(f"mask{s}", [P, T, N], BF16) for s in range(1 if rope else 2)]
        xn = [spare.sb([P, T, D]) for s in range(2)]
        xT = spare.sb([P, N])
        neg_bq = m.sb("neg_bq", [P, 2])
        qT = [[m.sb(f"qT{g}{j}", [P, N]) for j in range(4)] for g in range(2)]
        kT = [m.sb(f"kT{g}", [P, N]) for g in range(2)]
        v32 = m.sb("v32", [P, T, heads, 32])
        PR = 4
        LAG = 3
        prob = m.sb("prob", [P, PR, N])
        bias = m.sb("bias", [P, PR])
        ncos, nsin, part = (m.sb("ncos", [P, N]), m.sb("nsin", [P, N]), spare.sb([P, 4, N])) if rope else (None,) * 3
        total = [m.sb(f"total{s}", [P, T, 4]) for s in range(2)]
        ORDER = (2, 0, 1, 3) if rope else range(T)
        projections = 4
        tile_of = lambda n: ORDER[n // 4 % T]
        keys = lambda t: t + 1 if rope else T
        probT = m.sb("probT", [P, 4, T, N]) if rope or from_xn else core.mid[:, :, :, :].rearrange("p (j u) t d -> p j u (t d)", j=4)
        oT = [spare.sb([P, N]) for g in range(groups)]
        rinv = m.sb("rinv", [P, T, 4])
        ctx_tok = spare.sb([P, T, D])
        ctxT = spare.sb([P, N])
        upd = spare.sb([P, T, D])
        six, two = m.sb("six", [P, T, 6]), m.sb("two", [P, T, 2])
        misc = [m.ps(f"misc{i}") for i in range(2)]
        score = [m.ps(f"score{i}") for i in range(2)]
        tpose = [m.ps(f"tpose{i}") for i in range(2)]
        o_ps = [m.ps(f"o{g}") for g in range(2)]

        names = ["stat_done", "half_mean", "adj_in", "mask_ready", "xn_ready", "batch_free", "xt_in_psum", "xT_ready",
                 "proj_done", "qk_ready", "v_ready", "score_done", "score_taken", "prob_ready", "prob_free",
                 "probT_act", "probT_dve", "pv_done", "oT_ready", "back_done", "ctx_ready", "ctxt_in_psum",
                 "ctxT_ready", "attn_done", "chain", "const_set", "sym_chain", "tail", "adj_zero", "sym_done", "v_done", "adj_free", "rot_ready", "v32_set",
                 "zeros_set"]
        S = {n: m.sem(n) for n in names}
        if rope:
            at = {"values": 3, "back": 4, "ctx": 6, "out": 7, "v": 8, "rows": 9, "early": (10, 12)}
        else:
            at = {"values": 3, "back": 5, "ctx": 8, "out": 10, "v": 11, "late": (12, 13), "rows": 20, "early": (22, 24),
                  "adj": 26}
        wq, wk, wv, wo = (core.param(k, w + tag[-1]) for w in ("wq", "wk", "wv", "wo"))
        if rope:
            wqr, wkr = core.param(k, "wqr3"), core.param(k, "wkr3")
            cos, sin, ln1w = core.param(k, "cos"), core.param(k, "sin"), core.param(k, "ln1w")
        else:
            bq, bk, bv, bo = (core.param(k, w + tag[-1]) for w in ("bq", "bk", "bv", "bo"))
        block = ctx.enter_context(nc.Block())

        @block.sync
        def _(sp):
            core.load_params(sp, k + 1)
            if rope:
                return
            adj = core.dram["adj"].rearrange("b (t p) n -> b p t n", p=P)
            sp.dma_start(adj_raw[:, :, :], adj[0]).then_inc(S["adj_in"], 16)
            with sp.Fori(1, B) as b:
                sp.wait_ge(S["adj_free"], b)
                sp.dma_start(adj_raw[:, :, :], adj[b]).then_inc(S["adj_in"], 16)

        @block.gpsimd
        def _(pool):
            rsqrt_stats(pool, S["stat_done"], rstd[:, :, :], shift[:, :, :], core.stat2 if rope else core.x_stat,
                        scratch[:, :, :], half[:, :, :], 1e-6 if rope else LN_EPS, rms=rope)
            if rope:
                pool.memset(mask[0][:, :, :], 0.0).then_inc(S["adj_zero"], 1)
                pool.wait_ge(S["adj_zero"], 1)
                pool.affine_select(out=mask[0][:, :, :], in_=mask[0][:, :, :], compare_op=ALU.is_ge, fill=BIG, base=0,
                                   pattern=[[P, T], [-1, N]], channel_multiplier=1).then_inc(S["adj_free"], 1)

            def graph(b, s, first=False, last=False):
                if rope:
                    pool.wait_ge(S["xT_ready"], b + 1)
                    pool.tensor_tensor(xn[s][:, :, :], core.mid[:, b], over_features(rstd[:, b]), ALU.mult)\
                        .then_inc(S["xn_ready"], 1)
                    pool.wait_ge(S["qk_ready"], 4 * b + 2 + 1)
                    if first:
                        pool.wait_ge(S["zeros_set"], 8)
                    for j in range(4):
                        rows = slice(32 * j, 32 * j + 32)
                        pool.tensor_tensor(qT[s][j][rows, :], part[rows, 0, :], part[rows, 1, :], ALU.add)\
                            .then_inc(S["rot_ready"], 1)
                    pool.wait_ge(S["rot_ready"], 5 * b + 4 + 5)
                    pool.wait_ge(S["qk_ready"], 4 * b + 4 + 1)
                    pool.tensor_tensor(kT[s][:, :], part[:, 2, :], part[:, 3, :], ALU.add).then_inc(S["rot_ready"], 1)
                    return
                pool.wait_ge(S["batch_free"], b + 1)
                pool.tensor_tensor(xn[s][:, :, :], core.x_res[:, b], over_features(rstd[:, b]), ALU.mult)\
                    .then_inc(S["half_mean"], 1)
                pool.wait_ge(S["half_mean"], b + 1)
                pool.tensor_tensor(xn[s][:, :, :], xn[s][:, :, :], over_features(shift[:, b]), ALU.add)\
                    .then_inc(S["xn_ready"], 1)
                pool.wait_ge(S["adj_in"], 16 * (b + 1))
                apart(pool, core)
                if sym:
                    pool.tensor_scalar(mask[s][:, :, :], adj_raw[:, :, :], 0.0, None, ALU.is_gt)\
                        .then_inc(S["adj_free"], 1)
                else:
                    pool.tensor_scalar(mask[s][:, :, :], adj_raw[:, :, :], 0.0, BIG, ALU.is_equal, ALU.mult)\
                        .then_inc(S["adj_free"], 1)

            if rope:
                pool.sem_inc(S["rot_ready"], 5)
            all_graphs(pool, graph)

        @block.tensor
        def _(pe):
            pe.sem_inc(S["prob_free"], PR)
            pe.sem_inc(S["pv_done"], 1)
            pe.wait_ge(core.params_in[k], 16)

            def rows_in(b, s):
                pe.wait_ge(S["xn_ready"], b + 1)
                if rope:
                    pe.wait_ge(S["v_ready"], b + 1)
                else:
                    pe.wait_ge(S["qk_ready"], projections * b + 1)
                for t in range(T):
                    last = pe.transpose(misc[0][:, t * P:(t + 1) * P], xn[s][:, t, :], core.ident[:, :])
                last.then_inc(S["xt_in_psum"], 1)

            def project(b, n):
                if rope:
                    w = (wq, wqr, wk, wkr)[n]
                else:
                    w = (wq, wk)[n % 2][:, n // 2 * P:(n // 2 + 1) * P]
                if n == 0:
                    pe.wait_ge(S["xT_ready"], b + 1 + 2)
                    if rope:
                        pe.wait_ge(S["batch_free"], b + 1)
                elif n == 2 and not rope:
                    pe.wait_ge(S["batch_free"], b + 2)
                elif n == 3 and not rope:
                    pe.wait_ge(S["v_ready"], b + 1 + 1)
                elif n >= 2:
                    pe.wait_ge(S["qk_ready"], projections * b + n - 1 + 1)
                pe.matmul(misc[(n + 1) % 2][:, :], w, xT[:, :], start=True, stop=True).then_inc(S["proj_done"], 1)

            def project_v(b):
                for t in range(T):
                    last = pe.matmul(misc[0][:, t * D:(t + 1) * D], xT[:, t * P:(t + 1) * P], wv, start=True, stop=True)
                last.then_inc(S["v_done"], 1)

            def turn_adj(b, s):
                pe.wait_ge(S["adj_free"], b + 1)
                pe.wait_ge(S["qk_ready"], projections * b + 2 + 1)
                for t in range(T):
                    bank = misc[t // 2][:, :].bitcast(BF16)
                    for u in range(T):
                        last = pe.transpose(bank[:, t % 2 * N + u * P:t % 2 * N + (u + 1) * P],
                                            mask[s][:, u, t * P:(t + 1) * P], core.ident_bf[:, :])
                last.then_inc(S["sym_done"], 1)

            def scores(b, s, n):
                g, t, j = n // (4 * T), tile_of(n), n % 4
                if n == 0 and rope:
                    pe.wait_ge(S["rot_ready"], 5 * b + 5 + 5)
                elif n % (4 * T) == 0:
                    pe.wait_ge(S["qk_ready"], projections * b + 2 * g + 2 + 1)
                pe.wait_ge(S["score_taken"], items * b + n + 1)
                width = keys(t) * P
                pair = s if rope else g
                pe.matmul(score[n % 2][:, 0:width], qT[pair][j][:, t * P:(t + 1) * P], kT[pair][:, 0:width], start=True, stop=True)\
                    .then_inc(S["score_done"], 1)

            def transposes(b, n):
                pe.wait_ge(S["prob_ready"], items * b + n + 1)
                half_n = (items * b) // 2 if isinstance(b, int) else b * (items // 2)
                pe.wait_ge(S["probT_act"] if n % 2 == 0 else S["probT_dve"], half_n + n // 2 + 1)
                for u in range(keys(tile_of(n))):
                    last = pe.transpose(tpose[n % 2][:, u * P:(u + 1) * P], prob[:, n % PR, u * P:(u + 1) * P],
                                        core.ident[:, :])
                last.then_inc(S["prob_free"], 1)

            def values(b, g):
                done = b * (items // 2) + 2 * T * (g + 1) + 1
                if g == 0:
                    pe.wait_ge(S["v_ready"], b + 1 + 1)
                pe.wait_ge(S["oT_ready"], groups * b + g + 1)
                pe.wait_ge(S["probT_act"], done)
                pe.wait_ge(S["probT_dve"], done)
                for u in range(T):
                    for j in range(4):
                        first = u * P if rope else 0
                        last = pe.matmul(o_ps[g][32 * j:32 * j + 32, first:], v32[:, u, 4 * g + j, :], probT[:, j, u, first:],
                                         start=(u == 0), stop=(u == T - 1))
                last.then_inc(S["pv_done"], 1)

            def back_rows(b):
                for g in range(groups):
                    pe.wait_ge(S["oT_ready"], groups * (b + 1) + g + 1)
                    for t in range(T):
                        last = pe.transpose(misc[g][:, t * P:(t + 1) * P], oT[g][:, t * P:(t + 1) * P], core.ident[:, :])
                    last.then_inc(S["back_done"], 1)

            def turn_ctx(b):
                pe.wait_ge(S["ctx_ready"], groups * (b + 1))
                for t in range(T):
                    last = pe.transpose(misc[0][:, t * P:(t + 1) * P], ctx_tok[:, t, :], core.ident[:, :])
                last.then_inc(S["ctxt_in_psum"], 1)

            def project_out(b):
                pe.wait_ge(S["ctxT_ready"], b + 1)
                for t in range(T):
                    last = pe.matmul(misc[1][:, t * D:(t + 1) * D], ctxT[:, t * P:(t + 1) * P], wo, start=True, stop=True)
                last.then_inc(S["attn_done"], 1)

            def graph(b, s, first=False, last=False):
                for n in range(items):
                    scores(b, s, n)
                    if n == at["values"] and not first:
                        values(b - 1, groups - 1)
                    if n == at["values"] + 4 * T:
                        values(b, 0)
                    if n >= LAG:
                        transposes(b, n - LAG)
                    elif not first:
                        transposes(b - 1, items + n - LAG)
                    if not first:
                        if n == at["back"]:
                            back_rows(b - 1)
                        if n == at["ctx"]:
                            turn_ctx(b - 1)
                        if n == at["out"]:
                            project_out(b - 1)
                    if n == at["v"]:
                        project_v(b)
                    if not rope and n in at["late"]:
                        project(b, 2 + at["late"].index(n))
                    if not last:
                        if n == at["rows"]:
                            rows_in(b + 1, 1 - s)
                        if n in at["early"]:
                            early(b + 1, at["early"].index(n))
                        if sym and n == at["adj"]:
                            turn_adj(b + 1, 1 - s)

            def early(b, part):
                for n in (2 * part, 2 * part + 1) if rope else (part,):
                    project(b, n)

            rows_in(0, 0)
            early(0, 0)
            early(0, 1)
            if sym:
                turn_adj(0, 0)
            all_graphs(pe, graph)
            for n in range(items - LAG, items):
                transposes(B - 1, n)
            values(B - 1, groups - 1)
            back_rows(B - 1)
            turn_ctx(B - 1)
            project_out(B - 1)

        @block.scalar
        def _(act):
            act.sem_inc(S["probT_act"], 1)
            act.wait_ge(core.params_in[k], 16)
            if rope:
                act.mul(ncos[:, :], cos, -scale).then_inc(S["const_set"], 1)
                act.mul(nsin[:, :], sin, -scale).then_inc(S["const_set"], 1)
            else:
                act.mul(neg_bq[:, 0:groups], bq, -scale).then_inc(S["const_set"], 1)
                act.wait_ge(S["const_set"], 1)
                act.wait_ge(S["zeros_set"], 8)

            def copy_probT(b, n):
                act.wait_ge(S["prob_free"], items * b + n + 1 + PR)
                if n % (4 * T) == 0:
                    act.wait_ge(S["pv_done"], groups * b + n // (4 * T) + 1)
                t, j = tile_of(n), n % 4
                act.copy(probT[:, j, 0:keys(t), t * P:(t + 1) * P],
                         tpose[0][:, 0:keys(t) * P].rearrange("p (u q) -> p u q", u=keys(t)))\
                    .then_inc(S["probT_act"], 1)

            def take_qk(b, n):
                act.wait_ge(S["proj_done"], projections * b + n + 1)
                g, bank = n // 2, misc[(n + 1) % 2]
                if n % 2:
                    ins = act.activation(kT[g][:, :], bank[:, :], ACT.Identity, bias=bk[:, g:g + 1])
                else:
                    for j in range(4):
                        rows = slice(32 * j, 32 * j + 32)
                        ins = act.activation(qT[g][j][rows, :], bank[rows, :], ACT.Identity, bias=neg_bq[rows, g:g + 1],
                                             scale=-scale)
                ins.then_inc(S["qk_ready"], 1)

            def take_o(b, g):
                act.wait_ge(S["pv_done"], groups * b + g + 1 + 1)
                act.copy(oT[g][:, :], o_ps[g][:, :]).then_inc(S["oT_ready"], 1)

            def take_ctx(b):
                act.wait_ge(S["ctxt_in_psum"], b + 1)
                act.copy(ctxT[:, :], misc[0][:, :]).then_inc(S["ctxT_ready"], 1)

            def graph(b, s, first=False, last=False):
                for n in range(items):
                    act.wait_ge(S["score_taken"], items * b + n + 1 + 2)
                    tile = prob[:, n % PR, 0:keys(tile_of(n)) * P]
                    sums = {"accum_out": total[s][:, tile_of(n), n % 4:n % 4 + 1]} if rope else {}
                    act.activation(tile, tile, ACT.Exp, bias=bias[:, n % PR:n % PR + 1], scale=-1.0, **sums)\
                        .then_inc(S["prob_ready"], 1)
                    if (n - LAG) % 2 == 0:
                        if n >= LAG:
                            copy_probT(b, n - LAG)
                        elif not first:
                            copy_probT(b - 1, items + n - LAG)
                    if not first:
                        if n == at["values"] + 1:
                            take_o(b - 1, groups - 1)
                        if n == at["ctx"] + 1:
                            take_ctx(b - 1)
                    if rope:
                        continue
                    if n == at["values"] + 4 * T + 1:
                        take_o(b, 0)
                    if n - 1 in at["late"]:
                        take_qk(b, 2 + at["late"].index(n - 1))
                    if not last and n - 1 in at["early"]:
                        take_qk(b + 1, at["early"].index(n - 1))

            act.sem_inc(S["oT_ready"], groups)
            if not rope:
                act.sem_inc(S["qk_ready"], 1)
                take_qk(0, 0)
                take_qk(0, 1)
            all_graphs(act, graph)
            for n in range(items - LAG, items):
                if n % 2 == 0:
                    copy_probT(B - 1, n)
            take_o(B - 1, groups - 1)
            take_ctx(B - 1)

        @block.vector
        def _(dve):
            dve.sem_inc(S["batch_free"], 2)
            dve.sem_inc(S["score_taken"], 2)
            dve.sem_inc(S["probT_dve"], 1)
            dve.sem_inc(S["xT_ready"], 2)
            dve.sem_inc(S["v_ready"], 1)
            if rope:
                dve.sem_inc(S["qk_ready"], 1)
            dve.wait_ge(core.params_in[k], 16)
            for q in qT:
                for j in range(4):
                    dve.memset(q[j][:, :], 0.0).then_inc(S["zeros_set"], 1)
            dve.memset(v32[:, :, :, :], 0.0).then_inc(S["v32_set"], 1)
            dve.wait_ge(S["v32_set"], 1)
            if rope:
                dve.wait_ge(S["const_set"], 2)
                dve.wait_ge(S["adj_free"], 1)
            else:
                dve.memset(v32[:, :, :, head_dim:head_dim + 1], 1.0).then_inc(S["v32_set"], 1)

            def copy_probT(b, n):
                dve.wait_ge(S["prob_free"], items * b + n + 1 + PR)
                if n % (4 * T) == 1:
                    dve.wait_ge(S["pv_done"], groups * b + n // (4 * T) + 1)
                t, j = tile_of(n), n % 4
                dve.tensor_copy(probT[:, j, 0:keys(t), t * P:(t + 1) * P],
                                tpose[1][:, 0:keys(t) * P].rearrange("p (u q) -> p u q", u=keys(t)))\
                    .then_inc(S["probT_dve"], 1)

            def take_rows(b):
                dve.wait_ge(S["xt_in_psum"], b + 1)
                if rope:
                    dve.tensor_scalar(xT[:, :], misc[0][:, :], ln1w, None, ALU.mult).then_inc(S["xT_ready"], 1)
                else:
                    dve.tensor_copy(xT[:, :], misc[0][:, :]).then_inc(S["xT_ready"], 1)

            def rotate(b, half_):
                if half_ == 0:
                    dve.wait_ge(S["rot_ready"], 5 * b + 5)
                for n in (2 * half_, 2 * half_ + 1):
                    dve.wait_ge(S["proj_done"], 4 * b + n + 1)
                    dve.tensor_tensor(part[:, n, :], misc[(n + 1) % 2][:, :], (ncos[:, :], nsin[:, :], cos, sin)[n], ALU.mult)\
                        .then_inc(S["qk_ready"], 1)

            def take_v(b):
                dve.wait_ge(S["v_done"], b + 1)
                got = misc[0][:, :].rearrange("p (t h d) -> p t h d", t=T, h=heads)
                if rope:
                    dve.tensor_copy(v32[:, :, :, :], got).then_inc(S["v_ready"], 1)
                else:
                    dve.tensor_tensor(v32[:, :, :, 0:head_dim], got,
                                      bv.rearrange("p (h d) -> p h d", h=heads).unsqueeze(1).broadcast_to([P, T, heads, head_dim]),
                                      ALU.add).then_inc(S["v_ready"], 1)

            def join_adj(b, s, piece):
                chain = Chain(dve, S["sym_chain"], b * (T + 3) + (0, 1, 2, 2 + T)[piece])
                if piece < 2:
                    if piece == 0:
                        dve.wait_ge(S["sym_done"], b + 1)
                    pair = mask[s][:, 2 * piece:2 * piece + 2, :]
                    chain.step(dve.tensor_tensor(pair, pair, misc[piece][:, :].bitcast(BF16).rearrange("p (t n) -> p t n", t=2), ALU.add))
                elif piece == 2:
                    chain.settle()
                    for t in range(T):
                        own = mask[s][:, t, t * P:(t + 1) * P]
                        chain.step(dve.tensor_tensor(own, own, core.ident_bf[:, :], ALU.add))
                else:
                    chain.settle()
                    chain.step(dve.tensor_scalar(mask[s][:, :, :], mask[s][:, :, :], 0.0, BIG, ALU.is_equal, ALU.mult))
                    chain.settle()

            def normalise(b, s):
                chain = Chain(dve, S["chain"], b * groups)
                for g in range(groups):
                    dve.wait_ge(S["back_done"], groups * b + g + 1)
                    o = misc[g][:, :].rearrange("p (t j c) -> p t j c", t=T, j=4)
                    chain.step(dve.reciprocal(rinv[:, :, :], total[s][:, :, :] if rope else o[:, :, :, head_dim]))
                    chain.settle()
                    dve.tensor_tensor(ctx_tok[:, :, 4 * g * head_dim:4 * (g + 1) * head_dim].rearrange("p t (j c) -> p t j c", j=4),
                                      o[:, :, :, 0:head_dim], rinv[:, :, :].unsqueeze(3).broadcast_to([P, T, 4, head_dim]),
                                      ALU.mult).then_inc(S["ctx_ready"], 1)
                    dve.wait_ge(S["ctx_ready"], groups * b + g + 1)

            def take_out(b, s):
                dve.wait_ge(S["attn_done"], b + 1)
                base = core.mid[:, b] if rope else xn[s][:, :, :] if from_xn else core.x_res[:, b]
                dve.tensor_tensor(upd[:, :, :], misc[1][:, :].rearrange("p (t d) -> p t d", t=T), base, ALU.add)\
                    .then_inc(S["batch_free"], 1)

            def finish(b, piece):
                before = (0, 1, 2, 2 + T // 2, 2 + T, 2 + 2 * T)[piece]
                chain = Chain(dve, S["tail"], b * (2 * T + 3) + before)
                if piece == 0:
                    dve.wait_ge(S["batch_free"], b + 1 + 2)
                    if rope:
                        dve.sem_inc(S["tail"], 1)
                    else:
                        chain.step(dve.tensor_tensor(upd[:, :, :], upd[:, :, :], bo.unsqueeze(1).broadcast_to([P, T, D]), ALU.add))
                elif piece == 1:
                    chain.settle()
                    apart(dve, core)
                    chain.step(dve.tensor_copy(out_res[:, b], upd[:, :, :]))
                elif piece in (2, 3):
                    for t in (2 * piece - 4, 2 * piece - 3):
                        chain.step(dve.bn_stats(six[:, t, :], upd[:, t, :]))
                elif piece == 4:
                    chain.settle()
                    apart(dve, core)
                    for t in range(T):
                        chain.step(dve.bn_aggr(two[:, t, :], six[:, t, :]))
                else:
                    chain.settle()
                    apart(dve, core)
                    chain.step(dve.tensor_copy(core.x_stat[:, b], two[:, :, :]))

            def graph(b, s, first=False, last=False):
                dve.wait_ge(S["adj_free"], 1 if rope else b + 1)
                for n in range(items):
                    t = tile_of(n)
                    dve.wait_ge(S["score_done"], items * b + n + 1)
                    dve.wait_ge(S["prob_free"], items * b + n + 1)
                    apart(dve, core)
                    allowed = mask[0] if rope else mask[s]
                    width = keys(t) * P
                    dve.tensor_tensor_reduce(prob[:, n % PR, 0:width], score[n % 2][:, 0:width], allowed[:, t, 0:width], 1.0, 3e38,
                                             ALU.add, ALU.min, bias[:, n % PR:n % PR + 1])\
                        .then_inc(S["score_taken"], 1)
                    if (n - LAG) % 2 == 1:
                        if n >= LAG:
                            copy_probT(b, n - LAG)
                        elif not first:
                            copy_probT(b - 1, items + n - LAG)
                    if not first:
                        if n == at["back"] + 1:
                            normalise(b - 1, 1 - s)
                        if n == at["out"] + 1:
                            take_out(b - 1, 1 - s)
                        if 0 <= n - at["out"] - 2 < 6:
                            finish(b - 1, n - at["out"] - 2)
                    if n == at["v"] + 1:
                        take_v(b)
                    if not last:
                        if n == at["rows"] + 1:
                            take_rows(b + 1)
                        if rope and n - 1 in at["early"]:
                            rotate(b + 1, at["early"].index(n - 1))
                        if sym and n in JOIN:
                            join_adj(b + 1, 1 - s, JOIN.index(n))

            JOIN = [at["adj"] + i for i in (1, 2, 3, 5)] if sym else []
            take_rows(0)
            if rope:
                rotate(0, 0)
                rotate(0, 1)
            if sym:
                for piece in range(4):
                    join_adj(0, 0, piece)
            all_graphs(dve, graph)
            for n in range(items - LAG, items):
                if n % 2 == 1:
                    copy_probT(B - 1, n)
            normalise(B - 1, 1)
            take_out(B - 1, 1)
            for piece in range(6):
                finish(B - 1, piece)


def lstm_stage(core, k):
    nc = core.nc
    C = 16
    CB = C * B
    CHUNKS = N // C
    H_UNIT = 4096.0
    GATE = [0, 1, 3, 2]
    with ExitStack() as ctx:
        m = Mem(nc, ctx, "lstm")
        rstd, shift = m.sb("rstd", [P, B, T]), m.sb("shift", [P, B, T])
        scratch, half = m.sb("scratch", [P, B, T]), m.sb("half", [P, B, T])
        xn = [m.sb(f"xn{s}", [P, T, D]) for s in range(2)]
        xT = m.sb("xT", [P, N * B])
        hT = core.mid[:, :, :, :].rearrange("p b t d -> p b (t d)")
        w_part = [m.sb(f"w_part{i}", [P, 4 * P], BF16) for i in range(3)]
        w_rest = m.sb("w_rest", [P, 4 * P])
        gate_bias = m.sb("gate_bias", [P, 4])
        xg = [m.sb(f"xg{s}", [P, C, 4, B]) for s in range(2)]
        w_low = [m.sb(f"w_low{i}", [P, 4 * P], BF16) for i in range(2)]
        h_part = m.sb("h_part", [P, 2, B], mybir.dt.float16)
        hist = [m.sb(f"hist{s}", [P, C, B]) for s in range(2)]
        per_unit = m.sb("per_unit", [P, 1])
        sig = m.sb("sig", [P, 3, B])
        gc = m.sb("gc", [P, 2, B])
        prod = m.sb("prod", [P, 2, B])
        tanh_c = m.sb("tanh_c", [P, B])
        w_lin = m.sb("w_lin", [P, 2, P])
        ones = m.sb("ones", [P, N])
        logit0, gated, sums, before, after = (m.sb(n, [P, N]) for n in ("logit0", "gated", "sums", "before", "after"))
        upd = m.sb("upd", [P, T, D])
        six, two = m.sb("six", [P, T, 6]), m.sb("two", [P, T, 2])
        gates = [m.ps(f"gates{i}") for i in range(2)]
        xproj = [m.ps(f"xproj{i}") for i in range(2)]
        logit = [m.ps(f"logit_ps{i}") for i in range(2)]
        tpose = [m.ps(f"tpose{i}") for i in range(2)]
        names = ["stat_done", "half_mean", "xn_ready", "xt_in_psum", "xT_act", "xT_dve", "w_parts", "w_chain", "xproj_done",
                 "xg_ready", "hi_ready", "low_ready", "h_full", "gates_done", "sig_ready", "tg_ready",
                 "prod_done", "c_ready", "tc_ready", "hist_saved", "hist_free", "logits_done", "logits_free",
                 "scan_chain", "out_ready", "out_in_psum", "chain", "bias_set", "unit_set"]
        S = {n: m.sem(n) for n in names}
        par = lambda name: core.param(k, name)
        block = ctx.enter_context(nc.Block())

        @block.sync
        def _(sp):
            core.load_params(sp, k + 1)

        @block.gpsimd
        def _(pool):
            rsqrt_stats(pool, S["stat_done"], rstd[:, :, :], shift[:, :, :], core.x_stat, scratch[:, :, :],
                        half[:, :, :], LN_EPS)

            def normalise(b, s):
                pool.wait_ge(S["xt_in_psum"], b + 1)
                pool.tensor_tensor(xn[s][:, :, :], core.x_res[:, b], over_features(rstd[:, b]), ALU.mult)\
                    .then_inc(S["half_mean"], 1)
                pool.wait_ge(S["half_mean"], b + 1)
                pool.tensor_tensor(xn[s][:, :, :], xn[s][:, :, :], over_features(shift[:, b]), ALU.add)\
                    .then_inc(S["xn_ready"], 1)

            with pool.Fori(0, B // 2) as j:
                for s in range(2):
                    normalise(j * 2 + s, s)

            def save(c, s):
                pool.wait_ge(S["h_full"], C * (c + 1) + 1)
                pool.tensor_tensor(hT[:, :, bass.ds(c * C, C)], hist[s][:, :, :].rearrange("p t b -> p b t"),
                                   per_unit[:, :].unsqueeze(2).broadcast_to([P, B, C]), ALU.mult)\
                    .then_inc(S["hist_saved"], 1)

            pool.memset(per_unit[:, :], 1.0 / H_UNIT).then_inc(S["unit_set"], 1)
            pool.wait_ge(S["unit_set"], 1)
            pool.sem_inc(S["hist_saved"], 2)
            with pool.Fori(0, CHUNKS // 2) as it:
                for s in range(2):
                    save(it * 2 + s, s)

        @block.tensor
        def _(pe):
            pe.sem_inc(S["xt_in_psum"], 2)
            pe.wait_ge(core.params_in[k], 16)

            def turn(b, s):
                pe.wait_ge(S["xn_ready"], b + 1)
                pe.wait_ge(S["xT_act" if s == 0 else "xT_dve"], j + 1)
                for t in range(T):
                    last = pe.transpose(tpose[s][:, t * P:(t + 1) * P], xn[s][:, t, :], core.ident[:, :])
                last.then_inc(S["xt_in_psum"], 1)

            with pe.Fori(0, B // 2) as j:
                for s in range(2):
                    turn(j * 2 + s, s)
            pe.wait_ge(S["xT_act"], B // 2 + 1)
            pe.wait_ge(S["xT_dve"], B // 2 + 1)

            def project(c, n):
                pe.wait_ge(S["xg_ready"], 4 * c + n + 1)
                g = GATE[n]
                pe.matmul(xproj[n % 2][:, 0:CB], par("w_ih")[:, g * P:(g + 1) * P], xT[:, bass.ds(c * CB, CB)],
                          start=True, stop=True).then_inc(S["xproj_done"], 1)

            def seed(step, c, s, t):
                if t == 0:
                    pe.wait_ge(S["xg_ready"], 4 * c + 4 + 2)
                pe.matmul(gates[t % 2][:, 0:4 * B], core.ident[:, :], xg[s][:, t, :, :].rearrange("p g b -> p (g b)"),
                          start=True, stop=False)

            def recur(step, t):
                for part, sem, weights in ((0, "hi_ready", w_part), (1, "low_ready", w_low)):
                    pe.wait_ge(S[sem], step + 1)
                    for w in weights:
                        for n in range(4):
                            g = GATE[n]
                            last = pe.matmul(gates[t % 2][:, n * B:(n + 1) * B], w[:, g * P:(g + 1) * P],
                                             h_part[:, part, :], start=False, stop=(w is w_low[1] and n == 3))
                last.then_inc(S["gates_done"], 1)

            def chunk(c, s, last):
                for t in range(C):
                    recur(c * C + t, t)
                    if t < C - 1:
                        seed(c * C + t + 1, c, s, t + 1)
                    elif not last:
                        seed(c * C + t + 1, c + 1, 1 - s, 0)
                    if not last and 1 <= t <= 4:
                        project(c + 1, t - 1)

            for n in range(4):
                project(0, n)
            pe.wait_ge(S["w_parts"], 5)
            seed(0, 0, 0, 0)
            with pe.Fori(0, CHUNKS // 2 - 1) as it:
                for s in range(2):
                    chunk(it * 2 + s, s, False)
            chunk(CHUNKS - 2, 0, False)
            chunk(CHUNKS - 1, 1, True)

            def label(b):
                pe.wait_ge(S["logits_free"], b + 1)
                for i in range(2):
                    last = pe.matmul(logit[i][:, :], w_lin[:, i, :], hT[:, b, :], start=True, stop=True)
                last.then_inc(S["logits_done"], 1)

            def back(b):
                pe.wait_ge(S["out_ready"], b + 1)
                for t in range(T):
                    last = pe.transpose(tpose[0][:, t * P:(t + 1) * P], before[:, t * P:(t + 1) * P], core.ident[:, :])
                last.then_inc(S["out_in_psum"], 1)

            pe.wait_ge(S["hist_saved"], CHUNKS + 2)
            with pe.Fori(0, B) as b:
                label(b)
                back(b)

        @block.scalar
        def _(act):
            act.sem_inc(S["xT_act"], 1)
            act.sem_inc(S["xg_ready"], 2)
            act.wait_ge(core.params_in[k], 16)
            with act.Fori(0, B // 2) as j:
                act.wait_ge(S["xt_in_psum"], j * 2 + 1 + 2)
                act.copy(xT[:, :].rearrange("p (t b) -> p b t", b=B)[:, j * 2, :], tpose[0][:, :]).then_inc(S["xT_act"], 1)
            act.wait_ge(S["bias_set"], 1)

            def bring(c, s, n):
                act.wait_ge(S["xproj_done"], 4 * c + n + 1)
                act.activation(xg[s][:, :, n, :], xproj[n % 2][:, 0:CB].rearrange("p (t b) -> p t b", b=B),
                               ACT.Identity, bias=gate_bias[:, GATE[n]:GATE[n] + 1]).then_inc(S["xg_ready"], 1)

            def step(g, t):
                act.wait_ge(S["gates_done"], g + 1)
                bank = gates[t % 2]
                act.activation(sig[:, :, :], bank[:, 0:3 * B].rearrange("p (g b) -> p g b", b=B), ACT.Sigmoid)\
                    .then_inc(S["sig_ready"], 1)
                act.activation(gc[:, 0, :], bank[:, 3 * B:4 * B], ACT.Tanh).then_inc(S["tg_ready"], 1)
                act.wait_ge(S["c_ready"], g + 1)
                act.activation(tanh_c[:, :], gc[:, 1, :], ACT.Tanh).then_inc(S["tc_ready"], 1)

            def chunk(c, s, last):
                for t in range(C):
                    step(c * C + t, t)
                    if not last and 1 <= t <= 4:
                        bring(c + 1, 1 - s, t - 1)

            for n in range(4):
                bring(0, 0, n)
            with act.Fori(0, CHUNKS // 2 - 1) as it:
                for s in range(2):
                    chunk(it * 2 + s, s, False)
            chunk(CHUNKS - 2, 0, False)
            chunk(CHUNKS - 1, 1, True)

        @block.vector
        def _(dve):
            dve.sem_inc(S["xT_dve"], 1)
            dve.wait_ge(core.params_in[k], 16)
            dve.tensor_tensor(gate_bias[:, :], par("b_ih"), par("b_hh"), ALU.add).then_inc(S["bias_set"], 1)
            dve.tensor_copy(w_part[0][:, :], par("w_hh")).then_inc(S["w_parts"], 1)
            dve.wait_ge(S["w_parts"], 1)
            dve.tensor_tensor(w_rest[:, :], par("w_hh"), w_part[0][:, :], ALU.subtract).then_inc(S["w_chain"], 1)
            dve.wait_ge(S["w_chain"], 1)
            dve.tensor_copy(w_part[1][:, :], w_rest[:, :]).then_inc(S["w_parts"], 1)
            dve.wait_ge(S["w_parts"], 2)
            dve.tensor_tensor(w_part[2][:, :], w_rest[:, :], w_part[1][:, :], ALU.subtract).then_inc(S["w_parts"], 1)
            for i in range(2):
                dve.tensor_scalar(w_low[i][:, :], w_part[i][:, :], 1.0 / H_UNIT, None, ALU.mult).then_inc(S["w_parts"], 1)
            dve.memset(ones[:, :], 1.0).then_inc(S["w_chain"], 1)
            for i in range(2):
                dve.tensor_copy(w_lin[:, i, :], par("w_lin")[:, i * P:(i + 1) * P]).then_inc(S["w_chain"], 1)
            dve.memset(gc[:, :, :], 0.0).then_inc(S["h_full"], 1)
            for part, sem in enumerate(("hi_ready", "low_ready")):
                dve.memset(h_part[:, part, :], 0.0).then_inc(S[sem], 1)
            with dve.Fori(0, B // 2) as j:
                dve.wait_ge(S["xt_in_psum"], j * 2 + 2 + 2)
                dve.tensor_copy(xT[:, :].rearrange("p (t b) -> p b t", b=B)[:, j * 2 + 1, :], tpose[1][:, :])\
                    .then_inc(S["xT_dve"], 1)

            def step(g, s, t):
                dve.wait_ge(S["sig_ready"], g + 1)
                dve.wait_ge(S["tg_ready"], g + 1)
                dve.tensor_tensor(prod[:, :, :], sig[:, 0:2, :], gc[:, :, :], ALU.mult).then_inc(S["prod_done"], 1)
                dve.wait_ge(S["prod_done"], g + 1)
                dve.tensor_tensor(gc[:, 1, :], prod[:, 0, :], prod[:, 1, :], ALU.add).then_inc(S["c_ready"], 1)
                dve.wait_ge(S["tc_ready"], g + 1)
                dve.tensor_tensor(h_part[:, 0, :], sig[:, 2, :], tanh_c[:, :], ALU.mult).then_inc(S["hi_ready"], 1)
                dve.scalar_tensor_tensor(hist[s][:, t, :], sig[:, 2, :], H_UNIT, tanh_c[:, :], ALU.mult, ALU.mult)\
                    .then_inc(S["h_full"], 1)
                dve.wait_ge(S["hi_ready"], g + 2)
                dve.wait_ge(S["h_full"], g + 2)
                dve.scalar_tensor_tensor(h_part[:, 1, :], h_part[:, 0, :], -H_UNIT, hist[s][:, t, :], ALU.mult, ALU.add)\
                    .then_inc(S["low_ready"], 1)

            def chunk(c, s):
                dve.wait_ge(S["hist_saved"], c + 1)
                for t in range(C):
                    step(c * C + t, s, t)

            with dve.Fori(0, CHUNKS // 2) as it:
                for s in range(2):
                    chunk(it * 2 + s, s)

            dve.sem_inc(S["logits_free"], 1)
            dve.wait_ge(S["hist_saved"], CHUNKS + 2)
            with dve.Fori(0, B) as b:
                steps = 8 + 2 * T + 2
                chain = Chain(dve, S["chain"], b * steps)
                h = hT[:, b, :]
                dve.wait_ge(S["logits_done"], b + 1)
                chain.step(dve.tensor_scalar(logit0[:, :], logit[0][:, :], par("b_lin")[:, 0:1], None, ALU.add))
                chain.settle()
                dve.scalar_tensor_tensor(gated[:, :], logit[1][:, :], par("b_lin")[:, 1:2], logit0[:, :], ALU.add,
                                         ALU.is_gt).then_inc(S["logits_free"], 1)
                dve.wait_ge(S["logits_free"], b + 2)
                chain.step(dve.tensor_tensor(gated[:, :], gated[:, :], h, ALU.mult))
                chain.settle()
                chain.step(dve.tensor_tensor_scan(sums[:, :], ones[:, :], gated[:, :], 0.0, ALU.mult, ALU.add))
                chain.settle()
                chain.step(dve.tensor_tensor(before[:, :], sums[:, :], gated[:, :], ALU.subtract))
                chain.step(dve.tensor_scalar(after[:, :], sums[:, :], -1.0, sums[:, N - 1:N], ALU.mult, ALU.add))
                chain.settle()
                chain.step(dve.scalar_tensor_tensor(before[:, :], before[:, :], par("fw"), h, ALU.mult, ALU.add))
                chain.step(dve.scalar_tensor_tensor(after[:, :], after[:, :], par("bw"), h, ALU.mult, ALU.add))
                chain.settle()
                dve.tensor_tensor(before[:, :], before[:, :], after[:, :], ALU.add).then_inc(S["out_ready"], 1)
                dve.wait_ge(S["out_in_psum"], b + 1)
                chain.step(dve.tensor_tensor(upd[:, :, :], tpose[0][:, :].rearrange("p (t d) -> p t d", t=T),
                                             core.x_res[:, b], ALU.add))
                chain.settle()
                row_stats(dve, chain, core, six, two, upd)
                chain.step(dve.tensor_copy(core.x_res[:, b], upd[:, :, :]))
                chain.settle()
                apart(dve, core)
                chain.step(dve.tensor_copy(core.x_stat[:, b], two[:, :, :]))
                chain.settle()
                assert chain.n == steps + 0, chain.n


def ffn_tiles(pe, hid_ps, hid_done, hid_free, w1, xT, base, tiles):
    for n in range(tiles):
        pe.wait_ge(hid_free, base + n + 1)
        pe.matmul(hid_ps[n % len(hid_ps)][:, :], w1[:, n * P:(n + 1) * P], xT, start=True, stop=True)\
            .then_inc(hid_done, 1)


def ffn1_stage(core, k):
    nc = core.nc
    H = 4
    with ExitStack() as ctx:
        m = Mem(nc, ctx, "ffn1")
        rstd, shift = m.sb("rstd", [P, B, T]), m.sb("shift", [P, B, T])
        scratch, half = m.sb("scratch", [P, B, T]), m.sb("half", [P, B, T])
        y = [m.sb(f"y{s}", [P, T, D]) for s in range(2)]
        yT = [m.sb(f"yT{s}", [P, N]) for s in range(2)]
        hid = [m.sb(f"hid{s}", [P, H, N]) for s in range(2)]
        r = [m.sb(f"r{s}", [P, T, D]) for s in range(2)]
        upd = m.sb("upd", [P, T, D])
        six, two = m.sb("six", [P, T, 6]), m.sb("two", [P, T, 2])
        rstat = [m.sb(f"rstat{s}", [P, T, 2]) for s in range(2)]
        rv, rr, rs = m.sb("rv", [P, T]), [m.sb(f"rr{s}", [P, T]) for s in range(2)], [m.sb(f"rs{s}", [P, T]) for s in range(2)]
        tp = [m.ps(f"tp{s}") for s in range(2)]
        hid_ps = [m.ps(f"hid_ps{i}") for i in range(2)]
        out_ps = [m.ps(f"out_ps{s}") for s in range(2)]
        names = ["stat_done", "y_chain", "y_ready", "y_free", "y_in_psum", "yT_ready", "hid_done", "hid_free",
                 "out_done", "r_chain", "r_ready", "norm_ready", "chain", "x_chain"]
        S = {n: m.sem(n) for n in names}
        par = lambda name: core.param(k, name)
        block = ctx.enter_context(nc.Block())

        @block.sync
        def _(sp):
            core.load_params(sp, k + 1)

        @block.gpsimd
        def _(pool):
            rsqrt_stats(pool, S["stat_done"], rstd[:, :, :], shift[:, :, :], core.x_stat, scratch[:, :, :],
                        half[:, :, :], LN_EPS)
            pool.wait_ge(core.params_in[k], 16)
            row = lambda name: par(name).unsqueeze(1).broadcast_to([P, T, D])

            def first(b, s):
                chain = Chain(pool, S["y_chain"], b * 3)
                pool.wait_ge(S["y_free"], b + 1)
                chain.step(pool.tensor_tensor(y[s][:, :, :], core.mid[:, b], over_features(rstd[:, b]), ALU.mult))
                chain.settle()
                chain.step(pool.tensor_tensor(y[s][:, :, :], y[s][:, :, :], over_features(shift[:, b]), ALU.add))
                chain.settle()
                chain.step(pool.tensor_tensor(y[s][:, :, :], y[s][:, :, :], row("g1"), ALU.mult))
                chain.settle()
                pool.tensor_tensor(y[s][:, :, :], y[s][:, :, :], row("be1"), ALU.add).then_inc(S["y_ready"], 1)

            def second(b, s):
                chain = Chain(pool, S["r_chain"], b * 2)
                pool.wait_ge(S["r_ready"], b + 1)
                apart(pool, core)
                chain.step(pool.tensor_scalar(rv[:, :], rstat[s][:, :, 1], LN_EPS, None, ALU.add))
                chain.settle()
                chain.step(pool.tensor_tensor(rr[s][:, :], rv[:, :], half[:, 0, :], ALU.pow))
                chain.settle()
                pool.tensor_tensor(rs[s][:, :], rstat[s][:, :, 0], rr[s][:, :], ALU.mult).then_inc(S["norm_ready"], 1)

            first(0, 0)
            with pool.Fori(0, B // 2 - 1) as j:
                first(j * 2 + 1, 1)
                second(j * 2, 0)
                first(j * 2 + 2, 0)
                second(j * 2 + 1, 1)
            first(B - 1, 1)
            second(B - 2, 0)
            second(B - 1, 1)

        @block.tensor
        def _(pe):
            pe.wait_ge(core.params_in[k], 16)

            def graph(b, s):
                pe.wait_ge(S["y_ready"], b + 1)
                for t in range(T):
                    last = pe.transpose(tp[s][:, t * P:(t + 1) * P], y[s][:, t, :], core.ident[:, :])
                last.then_inc(S["y_in_psum"], 1)
                pe.wait_ge(S["yT_ready"], b + 1)
                ffn_tiles(pe, hid_ps, S["hid_done"], S["hid_free"], par("f1w1"), yT[s][:, :], H * b, H)
                pe.wait_ge(S["hid_free"], H * (b + 1) + 2)
                for t in range(T):
                    for n in range(H):
                        last = pe.matmul(out_ps[s][:, t * D:(t + 1) * D], hid[s][:, n, t * P:(t + 1) * P],
                                         par("f1w2")[:, n * D:(n + 1) * D], start=(n == 0), stop=(n == H - 1))
                last.then_inc(S["out_done"], 1)

            with pe.Fori(0, B // 2) as j:
                for s in range(2):
                    graph(j * 2 + s, s)

        @block.scalar
        def _(act):
            act.sem_inc(S["hid_free"], 2)
            act.wait_ge(core.params_in[k], 16)

            def graph(b, s):
                act.wait_ge(S["y_in_psum"], b + 1)
                act.copy(yT[s][:, :], tp[s][:, :]).then_inc(S["yT_ready"], 1)
                for n in range(H):
                    act.wait_ge(S["hid_done"], H * b + n + 1)
                    act.activation(hid[s][:, n, :], hid_ps[n % 2][:, :], ACT.Relu, bias=par("f1b1")[:, n:n + 1])\
                        .then_inc(S["hid_free"], 1)

            with act.Fori(0, B // 2) as j:
                for s in range(2):
                    graph(j * 2 + s, s)

        @block.vector
        def _(dve):
            dve.sem_inc(S["y_free"], 2)
            dve.wait_ge(core.params_in[k], 16)
            row = lambda name: par(name).unsqueeze(1).broadcast_to([P, T, D])

            def graph(b, s):
                chain = Chain(dve, S["chain"], b * STEPS)
                dve.wait_ge(S["out_done"], b + 1)
                o = out_ps[s][:, :].rearrange("p (t d) -> p t d", t=T)
                chain.step(dve.tensor_tensor(r[s][:, :, :], o, row("f1b2"), ALU.add))
                chain.settle()
                dve.tensor_tensor(r[s][:, :, :], r[s][:, :, :], y[s][:, :, :], ALU.add).then_inc(S["y_free"], 1)
                dve.wait_ge(S["y_free"], b + 1 + 2)
                for t in range(T):
                    chain.step(dve.bn_stats(six[:, t, :], r[s][:, t, :]))
                chain.settle()
                apart(dve, core)
                for t in range(T):
                    ins = dve.bn_aggr(rstat[s][:, t, :], six[:, t, :])
                ins.then_inc(S["r_ready"], 1)
                dve.wait_ge(S["norm_ready"], b + 1)
                for t in range(T):
                    chain.step(dve.tensor_scalar(r[s][:, t, :], r[s][:, t, :], rr[s][:, t:t + 1], rs[s][:, t:t + 1],
                                                 ALU.mult, ALU.subtract))
                chain.settle()
                chain.step(dve.tensor_tensor(r[s][:, :, :], r[s][:, :, :], row("g2"), ALU.mult))
                chain.settle()
                chain.step(dve.tensor_tensor(r[s][:, :, :], r[s][:, :, :], row("be2"), ALU.add))
                chain.settle()
                write_x(dve, chain, core, b, r[s][:, :, :], core.x_res[:, b], upd, six, two)
                assert chain.n == STEPS, chain.n

            STEPS = 3 + 2 * T + WRITE_STEPS
            with dve.Fori(0, B // 2) as j:
                for s in range(2):
                    graph(j * 2 + s, s)


class Rows:

    def __init__(self, m, core, S, source, shifted=True):
        self.core, self.S, self.source, self.shifted = core, S, source, shifted
        self.rstd, self.shift = m.sb("rstd", [P, B, T]), m.sb("shift", [P, B, T])
        self.scratch, self.half = m.sb("scratch", [P, B, T]), m.sb("half", [P, B, T])
        self.xn = [m.sb(f"xn{s}", [P, T, D]) for s in range(2)]

    def scales(self, pool, stat, eps):
        rsqrt_stats(pool, self.S["stat_done"], self.rstd[:, :, :], self.shift[:, :, :], stat,
                    self.scratch[:, :, :], self.half[:, :, :], eps, rms=not self.shifted)

    def normalise(self, pool, b, s):
        S, xn = self.S, self.xn[s][:, :, :]
        pool.wait_ge(S["xn_free"], b + 1)
        if not self.shifted:
            pool.tensor_tensor(xn, self.source[:, b], over_features(self.rstd[:, b]), ALU.mult).then_inc(S["xn_ready"], 1)
            return
        pool.tensor_tensor(xn, self.source[:, b], over_features(self.rstd[:, b]), ALU.mult).then_inc(S["half_mean"], 1)
        pool.wait_ge(S["half_mean"], b + 1)
        pool.tensor_tensor(xn, xn, over_features(self.shift[:, b]), ALU.add).then_inc(S["xn_ready"], 1)

    NAMES = ["stat_done", "xn_free", "half_mean", "xn_ready"]


def pairs(engine, graph, first=0, last=B):
    with engine.Fori(first // 2, last // 2) as j:
        for s in range(2):
            graph(j * 2 + s, s)


def turn(pe, core, bank, tile):
    for t in range(T):
        last = pe.transpose(bank[:, t * P:(t + 1) * P], tile[:, t, :], core.ident[:, :])
    return last


def mod_stage(core, k):
    nc = core.nc
    H = 4
    KEPT = max(1, N // 2) - 1
    with ExitStack() as ctx:
        m = Mem(nc, ctx, "mod")
        names = Rows.NAMES + ["xt_done", "xT_ready", "w_done", "wcol_ready", "wide_ready", "wrow_done", "ranked",
                              "hid_done", "hid_free", "out_done", "out_taken", "tri_set", "tri_chain", "chain"]
        S = {n: m.sem(n) for n in names}
        rows_ = Rows(m, core, S, core.x_res)
        xT = [m.sb(f"xT{s}", [P, N]) for s in range(2)]
        wcol = [m.sb(f"wcol{s}", [P, T]) for s in range(2)]
        wide = m.sb("wide", [P, T, P])
        earlier, later = m.sb("earlier", [P, T, N], BF16), m.sb("later", [P, T, N], BF16)
        hits = m.sb("hits", [P, 2 * T, N], BF16)
        count = m.sb("count", [P, 2, T])
        rank, coef = m.sb("rank", [P, T]), m.sb("coef", [P, T])
        hid = [m.sb(f"hid{s}", [P, H, N]) for s in range(2)]
        y = m.sb("y", [P, T, D])
        upd = m.sb("upd", [P, T, D])
        six, two = m.sb("six", [P, T, 6]), m.sb("two", [P, T, 2])
        tp = m.ps("tp")
        w_ps = m.ps("w_ps")
        wrow = m.ps("wrow")
        hid_ps = [m.ps(f"hid_ps{i}") for i in range(2)]
        out_ps = [m.ps(f"out_ps{s}") for s in range(2)]
        par = lambda name: core.param(k, name)
        block = ctx.enter_context(nc.Block())

        @block.sync
        def _(sp):
            core.load_params(sp, k + 1)

        @block.gpsimd
        def _(pool):
            rows_.scales(pool, core.x_stat, LN_EPS)
            for n, (tri, op, sign) in enumerate(((earlier, ALU.is_gt, 1), (later, ALU.is_ge, -1))):
                pool.memset(tri[:, :, :], 1.0).then_inc(S["tri_chain"], 1)
                pool.wait_ge(S["tri_chain"], n + 1)
                pool.affine_select(out=tri[:, :, :], in_=tri[:, :, :], compare_op=op, fill=0.0, base=0,
                                   pattern=[[sign * P, T], [-sign, N]], channel_multiplier=sign).then_inc(S["tri_set"], 1)
            pairs(pool, lambda b, s: rows_.normalise(pool, b, s))

        @block.tensor
        def _(pe):
            pe.wait_ge(core.params_in[k], 16)

            def graph(b, s):
                pe.wait_ge(S["xn_ready"], b + 1)
                turn(pe, core, tp, rows_.xn[s]).then_inc(S["xt_done"], 1)
                pe.wait_ge(S["xT_ready"], b + 1)
                for t in range(T):
                    last = pe.matmul(w_ps[:, t:t + 1], xT[s][:, t * P:(t + 1) * P], par("mwr"), start=True, stop=True)
                last.then_inc(S["w_done"], 1)
                ffn_tiles(pe, hid_ps, S["hid_done"], S["hid_free"], par("mw1"), xT[s][:, :], H * b, H)
                pe.wait_ge(S["wide_ready"], b + 1)
                turn(pe, core, wrow, wide).then_inc(S["wrow_done"], 1)
                pe.wait_ge(S["hid_free"], H * (b + 1) + 2)
                for t in range(T):
                    for n in range(H):
                        last = pe.matmul(out_ps[s][:, t * D:(t + 1) * D], hid[s][:, n, t * P:(t + 1) * P],
                                         par("mw2")[:, n * D:(n + 1) * D], start=(n == 0), stop=(n == H - 1))
                last.then_inc(S["out_done"], 1)

            pairs(pe, graph)

        @block.scalar
        def _(act):
            act.sem_inc(S["hid_free"], 2)
            act.wait_ge(core.params_in[k], 16)

            def graph(b, s):
                act.wait_ge(S["xt_done"], b + 1)
                act.copy(xT[s][:, :], tp[:, :]).then_inc(S["xT_ready"], 1)
                for n in range(H):
                    act.wait_ge(S["hid_done"], H * b + n + 1)
                    act.activation(hid[s][:, n, :], hid_ps[n % 2][:, :], ACT.Gelu_apprx_tanh,
                                   bias=par("mb1")[:, n:n + 1]).then_inc(S["hid_free"], 1)

            pairs(act, graph)

        @block.vector
        def _(dve):
            dve.sem_inc(S["xn_free"], 2)
            dve.wait_ge(core.params_in[k], 16)
            dve.wait_ge(S["tri_set"], 2)
            STEPS = 2 * T + 2 + 1 + T - 1 + WRITE_STEPS

            def graph(b, s):
                chain = Chain(dve, S["chain"], b * STEPS)
                dve.wait_ge(S["w_done"], b + 1)
                dve.tensor_scalar(wcol[s][:, :], w_ps[:, 0:T], par("mbr"), None, ALU.add).then_inc(S["wcol_ready"], 1)
                dve.wait_ge(S["wcol_ready"], b + 1)
                dve.tensor_copy(wide[:, :, :], wcol[s][:, :].unsqueeze(2).broadcast_to([P, T, P])).then_inc(S["wide_ready"], 1)
                dve.wait_ge(S["wrow_done"], b + 1)
                for t in range(T):
                    for i, (tri, op) in enumerate(((earlier, ALU.is_ge), (later, ALU.is_gt))):
                        chain.step(dve.scalar_tensor_tensor(hits[:, 2 * t + i, :], wrow[:, :], wcol[s][:, t:t + 1],
                                                            tri[:, t, :], op, ALU.mult, accum_out=count[:, i, t:t + 1]))
                chain.settle()
                chain.step(dve.tensor_tensor(rank[:, :], count[:, 0, :], count[:, 1, :], ALU.add))
                chain.settle()
                chain.step(dve.scalar_tensor_tensor(coef[:, :], rank[:, :], float(KEPT), wcol[s][:, :], ALU.is_lt, ALU.mult))
                dve.wait_ge(S["out_done"], b + 1)
                chain.step(dve.tensor_tensor(y[:, :, :], out_ps[s][:, :].rearrange("p (t d) -> p t d", t=T),
                                             par("mb2").unsqueeze(1).broadcast_to([P, T, D]), ALU.add))
                chain.settle()
                for t in range(T):
                    ins = dve.scalar_tensor_tensor(y[:, t, :], y[:, t, :], coef[:, t:t + 1], rows_.xn[s][:, t, :],
                                                   ALU.mult, ALU.add)
                    if t < T - 1:
                        chain.step(ins)
                ins.then_inc(S["xn_free"], 1)
                chain.settle()
                dve.wait_ge(S["xn_free"], b + 1 + 2)
                write_x(dve, chain, core, b, y[:, :, :], core.x_res[:, b], upd, six, two)
                assert chain.n == STEPS, (chain.n, STEPS)

            pairs(dve, graph)


def gat_stage(core, k, i):
    nc = core.nc
    with ExitStack() as ctx:
        m = Mem(nc, ctx, f"gat{i}")
        names = Rows.NAMES + ["adj_in", "adj_free", "xt_done", "xT_ready", "wa_done", "wa_ready", "h_done", "h_ready",
                              "t_done", "s_ready", "masked", "low_ready", "nmax_ready", "prob_ready", "prob_turned",
                              "probT_act", "probT_dve", "pv_done", "x_done", "chain", "wide_set", "s_low", "prep", "leaky"]
        S = {n: m.sem(n) for n in names}
        rows_ = Rows(m, core, S, core.x_res)
        adj_raw = m.sb("adj_raw", [P, T, N], I32)
        mask = [m.sb(f"mask{s}", [P, T, N], BF16) for s in range(2)]
        xT = m.sb("xT", [P, N])
        a_wide = m.sb("a_wide", [P, P])
        wa = m.sb("wa", [P, P + 1])
        h = m.sb("h", [P, T, D])
        s_col, s_low = m.sb("s_col", [P, T]), m.sb("s_low", [P, T])
        tmax, zmax, low, nmax = (m.sb(n, [P, T]) for n in ("tmax", "zmax", "low", "nmax"))
        z = m.sb("z", [P, T, N])
        zlow = m.sb("zlow", [P, T, N])
        total, rinv = m.sb("total", [P, T]), m.sb("rinv", [P, T])
        probT = m.sb("probT", [P, T, T, P])
        y = m.sb("y", [P, T, D])
        upd = m.sb("upd", [P, T, D])
        six, two = m.sb("six", [P, T, 6]), m.sb("two", [P, T, 2])
        tp, h_ps, s_ps, t_ps, o_ps = (m.ps(n) for n in ("tp", "h_ps", "s_ps", "t_ps", "o_ps"))
        tpose = [m.ps(f"tpose{n}") for n in range(2)]
        par = lambda name: core.param(k, name)
        w, wt, a = par(f"gw{i}"), par(f"gwt{i}"), par(f"ga{i}")
        SLOPE = 0.2
        block = ctx.enter_context(nc.Block())

        @block.sync
        def _(sp):
            core.load_params(sp, k + 1)
            adj = core.dram["adj"].rearrange("b (t p) n -> b p t n", p=P)
            sp.dma_start(adj_raw[:, :, :], adj[0]).then_inc(S["adj_in"], 16)
            with sp.Fori(1, B) as b:
                sp.wait_ge(S["adj_free"], b)
                sp.dma_start(adj_raw[:, :, :], adj[b]).then_inc(S["adj_in"], 16)

        @block.gpsimd
        def _(pool):
            rows_.scales(pool, core.x_stat, LN_EPS)

            def graph(b, s):
                rows_.normalise(pool, b, s)
                pool.wait_ge(S["adj_in"], 16 * (b + 1))
                pool.wait_ge(S["x_done"], b + 1)
                apart(pool, core)
                pool.tensor_scalar(mask[s][:, :, :], adj_raw[:, :, :], 0.0, -BIG, ALU.is_le if i == 2 else ALU.is_equal,
                                   ALU.mult).then_inc(S["adj_free"], 1)

            pairs(pool, graph)

        @block.tensor
        def _(pe):
            pe.sem_inc(S["xn_free"], 2)
            pe.sem_inc(S["pv_done"], 1)
            pe.wait_ge(core.params_in[k], 16)
            pe.wait_ge(S["wide_set"], 1)
            pe.matmul(s_ps[:, 0:P], wt, a_wide[:, :], start=True, stop=True).then_inc(S["wa_done"], 1)
            pe.matmul(t_ps[:, 0:1], wt, a[:, 0:1], start=True, stop=True).then_inc(S["wa_done"], 1)
            pe.wait_ge(S["wa_ready"], 2)

            def graph(b, s):
                pe.wait_ge(S["xn_ready"], b + 1)
                turn(pe, core, tp, rows_.xn[s]).then_inc(S["xn_free"], 1)
                pe.wait_ge(S["xT_ready"], b + 1)
                pe.matmul(t_ps[:, :], wa[:, 0:P], xT[:, :], start=True, stop=True).then_inc(S["t_done"], 1)
                for t in range(T):
                    last = pe.matmul(s_ps[:, t:t + 1], xT[:, t * P:(t + 1) * P], wa[:, P:P + 1], start=True, stop=True)
                last.then_inc(S["t_done"], 1)
                for t in range(T):
                    last = pe.matmul(h_ps[:, t * D:(t + 1) * D], xT[:, t * P:(t + 1) * P], w, start=True, stop=True)
                last.then_inc(S["h_done"], 1)
                for t in range(T):
                    pe.wait_ge(S["prob_ready"], T * b + t + 1)
                    pe.wait_ge(S["probT_act"] if t % 2 == 0 else S["probT_dve"], 2 * b + t // 2 + 1)
                    for u in range(T):
                        last = pe.transpose(tpose[t % 2][:, u * P:(u + 1) * P], zlow[:, t, u * P:(u + 1) * P],
                                            core.ident[:, :])
                    last.then_inc(S["prob_turned"], 1)
                    if t >= 1:
                        values(b, t - 1)
                values(b, T - 1)

            def values(b, t):
                if t == 0:
                    pe.wait_ge(S["h_ready"], b + 1)
                pe.wait_ge(S["probT_act"] if t % 2 == 0 else S["probT_dve"], 2 * b + t // 2 + 2)
                for u in range(T):
                    last = pe.matmul(o_ps[:, t * D:(t + 1) * D], probT[:, t, u, :], h[:, u, :],
                                     start=(u == 0), stop=(u == T - 1))
                if t == T - 1:
                    last.then_inc(S["pv_done"], 1)

            pairs(pe, graph)

        @block.scalar
        def _(act):
            act.sem_inc(S["probT_act"], 1)
            act.wait_ge(S["wa_done"], 2)
            act.copy(wa[:, 0:P], s_ps[:, 0:P]).then_inc(S["wa_ready"], 1)
            act.copy(wa[:, P:P + 1], t_ps[:, 0:1]).then_inc(S["wa_ready"], 1)

            def graph(b, s):
                act.wait_ge(S["xn_free"], b + 1 + 2)
                act.copy(xT[:, :], tp[:, :]).then_inc(S["xT_ready"], 1)
                act.wait_ge(S["t_done"], 2 * (b + 1))
                act.copy(s_col[:, :], s_ps[:, 0:T]).then_inc(S["s_ready"], 1)
                act.mul(s_low[:, :], s_ps[:, 0:T], SLOPE).then_inc(S["s_low"], 1)
                act.wait_ge(S["h_done"], b + 1)
                act.copy(flat(h[:, :, :]), h_ps[:, :]).then_inc(S["h_ready"], 1)
                act.wait_ge(S["s_low"], b + 1)
                for t in range(T):
                    act.wait_ge(S["masked"], T * b + t + 1)
                    act.activation(zlow[:, t, :], z[:, t, :], ACT.Identity, bias=s_low[:, t:t + 1], scale=SLOPE)\
                        .then_inc(S["low_ready"], 1)
                for t in range(T):
                    act.wait_ge(S["leaky"], T * b + t + 1)
                    act.activation(zlow[:, t, :], z[:, t, :], ACT.Exp, bias=nmax[:, t:t + 1],
                                   accum_out=total[:, t:t + 1]).then_inc(S["prob_ready"], 1)
                    if t % 2 == 1:
                        copy_probT(b, t - 1)

            def copy_probT(b, t):
                act.wait_ge(S["prob_turned"], T * b + t + 1)
                if t == 0:
                    act.wait_ge(S["pv_done"], b + 1)
                act.copy(probT[:, t, :, :].rearrange("p u q -> p (u q)"), tpose[t % 2][:, :]).then_inc(S["probT_act"], 1)

            pairs(act, graph)

        @block.vector
        def _(dve):
            dve.sem_inc(S["probT_dve"], 1)
            dve.sem_inc(S["x_done"], 2)
            dve.wait_ge(core.params_in[k], 16)
            dve.tensor_copy(a_wide[:, :], a[:, 1:2].broadcast_to([P, P])).then_inc(S["wide_set"], 1)
            STEPS = 3 + 1 + T + 2 * T + 1

            def graph(b, s):
                chain = Chain(dve, S["chain"], b * STEPS)
                dve.wait_ge(S["t_done"], 2 * b + 1)
                dve.wait_ge(S["adj_free"], b + 1)
                apart(dve, core)
                for t in range(T):
                    dve.tensor_tensor_reduce(z[:, t, :], t_ps[:, :], mask[s][:, t, :], 1.0, -3e38, ALU.add, ALU.max,
                                             tmax[:, t:t + 1]).then_inc(S["masked"], 1)
                dve.wait_ge(S["s_ready"], b + 1)
                dve.wait_ge(S["masked"], T * (b + 1))
                chain.step(dve.tensor_tensor(zmax[:, :], tmax[:, :], s_col[:, :], ALU.add))
                chain.settle()
                chain.step(dve.scalar_tensor_tensor(low[:, :], zmax[:, :], SLOPE, zmax[:, :], ALU.mult, ALU.max))
                chain.settle()
                chain.step(dve.tensor_scalar(nmax[:, :], low[:, :], -1.0, None, ALU.mult))
                chain.settle()
                for t in range(T):
                    dve.wait_ge(S["low_ready"], T * b + t + 1)
                    dve.scalar_tensor_tensor(z[:, t, :], z[:, t, :], s_col[:, t:t + 1], zlow[:, t, :], ALU.add, ALU.max)\
                        .then_inc(S["leaky"], 1)
                for t in (1, 3):
                    dve.wait_ge(S["prob_turned"], T * b + t + 1)
                    if t == 1:
                        dve.wait_ge(S["pv_done"], b + 1)
                    dve.tensor_copy(probT[:, t, :, :].rearrange("p u q -> p (u q)"), tpose[1][:, :])\
                        .then_inc(S["probT_dve"], 1)
                dve.wait_ge(S["prob_ready"], T * (b + 1))
                chain.step(dve.reciprocal(rinv[:, :], total[:, :]))
                chain.settle()
                dve.wait_ge(S["pv_done"], b + 1 + 1)
                for t in range(T):
                    chain.step(dve.scalar_tensor_tensor(upd[:, t, :], o_ps[:, t * D:(t + 1) * D], rinv[:, t:t + 1],
                                                        core.x_res[:, b, t, :], ALU.mult, ALU.add))
                chain.settle()
                apart(dve, core)
                chain.step(dve.tensor_copy(core.x_res[:, b], upd[:, :, :]))
                row_stats(dve, chain, core, six, two, upd)
                chain.settle()
                apart(dve, core)
                dve.tensor_copy(core.x_stat[:, b], two[:, :, :]).then_inc(S["x_done"], 1)
                assert chain.n == STEPS, (chain.n, STEPS)

            pairs(dve, graph)


E_ = 8
TOP = 2


def prep_stage(core, k, kind):
    nc = core.nc
    renorm, router = "renorm" in kind, "router" in kind
    tag = f"prep{k}"
    R = B * T
    with ExitStack() as ctx:
        m = Mem(nc, ctx, tag)
        names = Rows.NAMES + ["saved", "xt_done", "xT_ready", "logit_done", "logit_taken", "chain", "gate_chain",
                              "low_ready", "exp_ready", "tri_zero", "tri_set"]
        S = {n: m.sem(n) for n in names}
        rows_ = Rows(m, core, S, core.x_res if renorm else core.mid, shifted=renorm)
        xT = [m.sb(f"xT{s}", [P, N]) for s in range(2)]
        six, two = m.sb("six", [P, T, 6]), m.sb("two", [P, T, 2])
        tp = [m.ps(f"tp{s}") for s in range(2)]
        lg = [m.ps(f"lg{s}") for s in range(2)]
        if router:
            logits = m.sb("logits", [P, R, E_])
            prob = m.sb("prob", [P, R, E_])
            above, ties = m.sb("above", [P, R, E_, E_], BF16), m.sb("ties", [P, R, E_, E_], BF16)
            order = m.sb("order", [P, E_, E_], BF16)
            rank = m.sb("rank", [P, R, E_])
            row = [m.sb(f"row{i}", [P, R]) for i in range(5)]
            w_router = core.param(k, "er" if renorm else "hr")
        block = ctx.enter_context(nc.Block())

        @block.gpsimd
        def _(pool):
            rows_.scales(pool, core.x_stat, LN_EPS if renorm else 1e-6)
            if router:
                pool.memset(order[:, :, :], 1.0).then_inc(S["tri_zero"], 1)
                pool.wait_ge(S["tri_zero"], 1)
                pool.affine_select(out=order[:, :, :], in_=order[:, :, :], compare_op=ALU.is_gt, fill=0.0, base=0,
                                   pattern=[[1, E_], [-1, E_]], channel_multiplier=0).then_inc(S["tri_set"], 1)
            pairs(pool, lambda b, s: rows_.normalise(pool, b, s))

        @block.tensor
        def _(pe):
            if not router:
                return
            pe.wait_ge(core.params_in[k], 16)

            def graph(b, s):
                pe.wait_ge(S["xn_ready"], b + 1)
                turn(pe, core, tp[s], rows_.xn[s]).then_inc(S["xt_done"], 1)
                pe.wait_ge(S["xT_ready"], b + 1)
                pe.wait_ge(S["logit_taken"], b + 1)
                for t in range(T):
                    last = pe.matmul(lg[s][:, t * E_:(t + 1) * E_], xT[s][:, t * P:(t + 1) * P], w_router,
                                     start=True, stop=True)
                last.then_inc(S["logit_done"], 1)

            pairs(pe, graph)

        @block.scalar
        def _(act):
            act.sem_inc(S["saved"], 2)
            if router:
                act.wait_ge(core.params_in[k], 16)

            def graph(b, s):
                if renorm:
                    act.wait_ge(S["xn_ready"], b + 1)
                    act.copy(core.mid[:, b], rows_.xn[s][:, :, :]).then_inc(S["saved"], 1)
                if router:
                    act.wait_ge(S["xt_done"], b + 1)
                    if renorm:
                        ins = act.copy(xT[s][:, :], tp[s][:, :])
                    else:
                        ins = act.activation(xT[s][:, :], tp[s][:, :], ACT.Identity, scale=core.param(k, "ln2w"))
                    ins.then_inc(S["xT_ready"], 1)

            pairs(act, graph)
            if router:
                act.wait_ge(S["low_ready"], 1)
                act.activation(logits[:, :, :], logits[:, :, :], ACT.Exp).then_inc(S["exp_ready"], 1)

        @block.vector
        def _(dve):
            dve.sem_inc(S["xn_free"], 2)
            dve.sem_inc(S["logit_taken"], 2)
            if router:
                dve.wait_ge(core.params_in[k], 16)
                dve.wait_ge(S["tri_set"], 1)

            def graph(b, s):
                chain = Chain(dve, S["chain"], b * STEPS)
                if renorm:
                    dve.wait_ge(S["xn_ready"], b + 1)
                    row_stats(dve, chain, core, six, two, rows_.xn[s])
                    chain.settle()
                    apart(dve, core)
                    chain.step(dve.tensor_copy(core.stat2[:, b], two[:, :, :]))
                    dve.wait_ge(S["saved"], b + 1 + 2)
                if router:
                    dve.wait_ge(S["logit_done"], b + 1)
                    apart(dve, core)
                    out = logits[:, bass.ds(b * T, T), :]
                    got = lg[s][:, 0:T * E_].rearrange("p (t e) -> p t e", t=T)
                    if renorm:
                        ins = dve.tensor_tensor(out, got, core.param(k, "ebr").unsqueeze(1).broadcast_to([P, T, E_]), ALU.add)
                    else:
                        ins = dve.tensor_copy(out, got)
                    ins.then_inc(S["logit_taken"], 1)
                chain.settle() if chain.n else None
                dve.sem_inc(S["xn_free"], 1)

            STEPS = 2 * T + 1 if renorm else 0
            pairs(dve, graph)
            if not router:
                return
            g = Chain(dve, S["gate_chain"])
            dve.wait_ge(S["logit_taken"], B + 2)
            top, total, inv, kept, inv2 = (r[:, :] for r in row)
            wide = lambda ap: ap.unsqueeze(2).broadcast_to([P, R, E_])
            g.step(dve.tensor_reduce(top, logits[:, :, :], AX.X, ALU.max))
            g.settle()
            dve.tensor_tensor(logits[:, :, :], logits[:, :, :], wide(top), ALU.subtract).then_inc(S["low_ready"], 1)
            dve.wait_ge(S["exp_ready"], 1)
            g.step(dve.tensor_reduce(total, logits[:, :, :], AX.X, ALU.add))
            g.settle()
            g.step(dve.reciprocal(inv, total))
            g.settle()
            g.step(dve.tensor_tensor(prob[:, :, :], logits[:, :, :], wide(inv), ALU.mult))
            g.settle()
            other = prob[:, :, :].unsqueeze(2).broadcast_to([P, R, E_, E_])
            own = prob[:, :, :].unsqueeze(3).broadcast_to([P, R, E_, E_])
            g.step(dve.tensor_tensor(above[:, :, :, :], other, own, ALU.is_gt))
            g.step(dve.tensor_tensor(ties[:, :, :, :], other, own, ALU.is_ge))
            g.settle()
            g.step(dve.tensor_tensor(ties[:, :, :, :], ties[:, :, :, :],
                                     order[:, :, :].unsqueeze(1).broadcast_to([P, R, E_, E_]), ALU.mult))
            g.settle()
            g.step(dve.tensor_tensor(above[:, :, :, :], above[:, :, :, :], ties[:, :, :, :], ALU.max))
            g.settle()
            g.step(dve.tensor_reduce(rank[:, :, :], above[:, :, :, :], AX.X, ALU.add))
            g.settle()
            g.step(dve.scalar_tensor_tensor(prob[:, :, :], rank[:, :, :], float(TOP), prob[:, :, :], ALU.is_lt, ALU.mult))
            g.settle()
            g.step(dve.tensor_reduce(kept, prob[:, :, :], AX.X, ALU.add))
            g.settle()
            if not renorm:
                g.step(dve.tensor_scalar(kept, kept, 1e-9, None, ALU.add))
                g.settle()
            g.step(dve.reciprocal(inv2, kept))
            g.settle()
            g.step(dve.tensor_tensor(core.gate[:, :, :, :].rearrange("p b t e -> p (b t) e"), prob[:, :, :], wide(inv2), ALU.mult))
            g.settle()


def moe_stage(core, k, swiglu, store=False):
    nc = core.nc
    if swiglu:
        FULL = 341
        WID = [P, P, FULL - 2 * P]
    else:
        FULL = 512
        WID = [P] * 4
    HT = len(WID)
    with ExitStack() as ctx:
        m = Mem(nc, ctx, f"moe{k}")
        names = Rows.NAMES + ["xT_ready", "hid_done", "hid_read", "out_done", "combined", "gate_ready", "b1_done",
                              "w1_ready", "b1_ready", "gT_done", "gT_ready", "bias_done", "chain", "x_chain", "silu_ready",
                              "acc_init", "stored"]
        S = {n: m.sem(n) for n in names}
        rows_ = Rows(m, core, S, core.mid, shifted=not swiglu)
        xT = [m.sb(f"xT{s}", [P, N]) for s in range(2)]
        hid = [m.sb(f"hid{s}", [P, HT, N]) for s in range(2)]
        gates = [m.sb(f"gate{s}", [P, T, E_]) for s in range(2)]
        acc = [m.sb(f"acc{s}", [P, T, D]) for s in range(2)]
        upd = m.sb("upd", [P, T, D])
        six, two = m.sb("six", [P, T, 6]), m.sb("two", [P, T, 2])
        tp, gb = m.ps("tp"), m.ps("gb")
        hid_ps = [m.ps(f"hid_ps{i}") for i in range(4)]
        out_ps = [m.ps(f"out_ps{s}") for s in range(2)]
        par = lambda name: core.param(k, name)
        if swiglu:
            silu = [m.sb(f"silu{i}", [P, N]) for i in range(2)]
        else:
            b1 = m.sb("b1", [P, E_ * HT])
            gT = m.sb("gT", [E_, N])
        PAIRS = 2 if swiglu else 4
        block = ctx.enter_context(nc.Block())

        @block.sync
        def _(sp):
            core.load_params(sp, k + 1)
            if store:
                with sp.Fori(0, B) as b:
                    sp.wait_ge(S["x_chain"], b + 1)
                    sp.dma_start(core.dram["out"][b].rearrange("(t p) d -> p t d", p=P), core.x_res[:, b])\
                        .then_inc(S["stored"], 16)
                sp.wait_ge(S["stored"], 16 * B)

        @block.gpsimd
        def _(pool):
            rows_.scales(pool, core.x_stat if swiglu else core.stat2, 1e-6 if swiglu else LN_EPS)
            pairs(pool, lambda b, s: rows_.normalise(pool, b, s))

        @block.tensor
        def _(pe):
            pe.sem_inc(S["xn_free"], 2)
            pe.wait_ge(core.params_in[k], 16)
            if not swiglu:
                for e in range(E_):
                    for n in range(HT):
                        last = pe.matmul(gb[:, e * HT + n:e * HT + n + 1], par("ew1")[:, e * FULL + n * P:e * FULL + (n + 1) * P],
                                         par("ebt")[:, e:e + 1], start=True, stop=True)
                last.then_inc(S["b1_done"], 1)

            def front(b, s):
                pe.wait_ge(S["xn_ready"], b + 1)
                turn(pe, core, tp, rows_.xn[s]).then_inc(S["xn_free"], 1)

            def hidden(b, s, e):
                if e == 0:
                    pe.wait_ge(S["xT_ready"], b + 1)
                for n, wid in enumerate(WID):
                    i = e * HT + n
                    pe.wait_ge(S["hid_read"], E_ * HT * b + i + 1)
                    col = e * FULL + n * P
                    if swiglu:
                        pe.matmul(hid_ps[2 * (i % 2)][0:wid, :], par("hw1")[:, col:col + wid], xT[s][:, :], start=True, stop=True)\
                            .then_inc(S["hid_done"], 1)
                        pe.matmul(hid_ps[2 * (i % 2) + 1][0:wid, :], par("hw3")[:, col:col + wid], xT[s][:, :], start=True, stop=True)\
                            .then_inc(S["hid_done"], 1)
                    else:
                        pe.matmul(hid_ps[i % 4][:, :], par("ew1")[:, col:col + wid], xT[s][:, :], start=True, stop=True)\
                            .then_inc(S["hid_done"], 1)

            def output(b, e):
                pe.wait_ge(S["combined"], E_ * b + e + 1)
                pe.wait_ge(S["hid_read"], HT * (E_ * b + e + 1) + PAIRS)
                w2 = par("hw2" if swiglu else "ew2")
                for t in range(T):
                    for n, wid in enumerate(WID):
                        last = pe.matmul(out_ps[e % 2][:, t * D:(t + 1) * D], hid[e % 2][0:wid, n, t * P:(t + 1) * P],
                                         w2[0:wid, (e * HT + n) * D:(e * HT + n + 1) * D], start=(n == 0), stop=(n == HT - 1))
                last.then_inc(S["out_done"], 1)

            def graph(b, s, last=False):
                for e in range(E_):
                    if e == 0 and not swiglu:
                        pe.wait_ge(S["gate_ready"], b + 1)
                        for t in range(T):
                            ins = pe.transpose(tp[0:E_, t * P:(t + 1) * P], gates[s][:, t, :], core.ident[:, :])
                        ins.then_inc(S["gT_done"], 1)
                    if e < E_ - 1:
                        hidden(b, s, e + 1)
                    elif not last:
                        hidden(b + 1, 1 - s, 0)
                    if e == 0 and not swiglu:
                        pe.wait_ge(S["gT_ready"], b + 1)
                        for t in range(T):
                            ins = pe.matmul(gb[:, t * D:(t + 1) * D], gT[:, t * P:(t + 1) * P], par("eb2")[0:E_, :],
                                            start=True, stop=True)
                        ins.then_inc(S["bias_done"], 1)
                    if e == 3 and not last:
                        front(b + 1, 1 - s)
                    output(b, e)

            front(0, 0)
            if not swiglu:
                pe.wait_ge(S["w1_ready"], E_)
            hidden(0, 0, 0)
            pairs(pe, graph, 0, B - 2)
            graph(B - 2, 0)
            graph(B - 1, 1, last=True)

        @block.scalar
        def _(act):
            act.wait_ge(core.params_in[k], 16)
            if not swiglu:
                act.sem_inc(S["hid_read"], PAIRS)
                act.wait_ge(S["b1_ready"], 1)

            def front(b, s):
                act.wait_ge(S["xn_free"], b + 1 + 2)
                if swiglu:
                    ins = act.activation(xT[s][:, :], tp[:, :], ACT.Identity, scale=par("ln2w"))
                else:
                    ins = act.copy(xT[s][:, :], tp[:, :])
                ins.then_inc(S["xT_ready"], 1)

            def hidden(b, e):
                for n, wid in enumerate(WID):
                    i = e * HT + n
                    if swiglu:
                        act.wait_ge(S["hid_done"], 2 * (E_ * HT * b + i) + 1)
                        act.activation(silu[i % 2][0:wid, :], hid_ps[2 * (i % 2)][0:wid, :], ACT.Silu).then_inc(S["silu_ready"], 1)
                    else:
                        act.wait_ge(S["hid_done"], E_ * HT * b + i + 1)
                        act.activation(hid[e % 2][:, n, :], hid_ps[i % 4][:, :], ACT.Gelu, bias=b1[:, i:i + 1])\
                            .then_inc(S["hid_read"], 1)

            def graph(b, s, last=False):
                for e in range(E_):
                    if e == 0 and not swiglu:
                        act.wait_ge(S["gT_done"], b + 1)
                        act.copy(gT[:, :], tp[0:E_, :]).then_inc(S["gT_ready"], 1)
                    if e < E_ - 1:
                        hidden(b, e + 1)
                    elif not last:
                        hidden(b + 1, 0)
                    if e == 3 and not last:
                        front(b + 1, 1 - s)

            front(0, 0)
            hidden(0, 0)
            pairs(act, graph, 0, B - 2)
            graph(B - 2, 0)
            graph(B - 1, 1, last=True)

        @block.vector
        def _(dve):
            dve.sem_inc(S["combined"], 2)
            dve.wait_ge(core.params_in[k], 16)
            if swiglu:
                dve.sem_inc(S["hid_read"], PAIRS)
            else:
                dve.wait_ge(S["b1_done"], 1)
                dve.tensor_tensor(b1[:, :], gb[:, 0:E_ * HT], par("eb1"), ALU.add).then_inc(S["b1_ready"], 1)
                for e in range(E_):
                    w1 = par("ew1")[:, e * FULL:(e + 1) * FULL]
                    dve.tensor_scalar(w1, w1, par("eg")[:, e:e + 1], None, ALU.mult).then_inc(S["w1_ready"], 1)

            def product(b, e):
                for n, wid in enumerate(WID):
                    i = e * HT + n
                    dve.wait_ge(S["silu_ready"], E_ * HT * b + i + 1)
                    dve.wait_ge(S["hid_done"], 2 * (E_ * HT * b + i) + 2)
                    dve.tensor_tensor(hid[e % 2][0:wid, n, :], hid_ps[2 * (i % 2) + 1][0:wid, :], silu[i % 2][0:wid, :],
                                      ALU.mult).then_inc(S["hid_read"], 1)

            def take_gate(b, s):
                dve.tensor_copy(gates[s][:, :, :], core.gate[:, b]).then_inc(S["gate_ready"], 1)

            def graph(b, s, last=False):
                chain = Chain(dve, S["chain"], b * STEPS)
                gate = gates[s]
                dve.wait_ge(S["gate_ready"], b + 1)
                if not swiglu:
                    dve.wait_ge(S["bias_done"], b + 1)
                    dve.tensor_copy(flat(acc[s][:, :, :]), gb[:, :]).then_inc(S["acc_init"], 1)
                    dve.wait_ge(S["acc_init"], b + 1)
                for e in range(E_):
                    if swiglu:
                        if e < E_ - 1:
                            product(b, e + 1)
                        elif not last:
                            product(b + 1, 0)
                    dve.wait_ge(S["out_done"], E_ * b + e + 1)
                    for t in range(T):
                        before = core.mid[:, b, t, :] if e == 0 and swiglu else acc[s][:, t, :]
                        ins = dve.scalar_tensor_tensor(acc[s][:, t, :], out_ps[e % 2][:, t * D:(t + 1) * D], gate[:, t, e:e + 1],
                                                       before, ALU.mult, ALU.add)
                        if t < T - 1:
                            chain.step(ins)
                    ins.then_inc(S["combined"], 1)
                    if e == 3 and not last:
                        take_gate(b + 1, 1 - s)
                    chain.settle()
                    dve.wait_ge(S["combined"], E_ * b + e + 1 + 2)
                if store:
                    dve.tensor_tensor(core.x_res[:, b], acc[s][:, :, :], core.x_res[:, b], ALU.add).then_inc(S["x_chain"], 1)
                    dve.wait_ge(S["x_chain"], b + 1)
                else:
                    write_x(dve, chain, core, b, acc[s][:, :, :], core.x_res[:, b], upd, six, two)
                assert chain.n == STEPS, (chain.n, STEPS)

            STEPS = E_ * (T - 1) + (0 if store else WRITE_STEPS)
            take_gate(0, 0)
            if swiglu:
                product(0, 0)
            pairs(dve, graph, 0, B - 2)
            graph(B - 2, 0)
            graph(B - 1, 1, last=True)


def program(core):
    load_stage(core)
    mha_stage(core, 0, "mha0", 8, 16, 2, 0.25, core.x_res)
    lstm_stage(core, 1)
    mha_stage(core, 2, "mha1", 8, 16, 2, 0.25, core.mid, sym=True, from_xn=True)
    ffn1_stage(core, 3)
    mod_stage(core, 4)
    gat_stage(core, 5, 2)
    prep_stage(core, 6, "renorm+router")
    moe_stage(core, 6, False)
    gat_stage(core, 7, 3)
    prep_stage(core, 8, "renorm")
    mha_stage(core, 8, "mha3", 4, 32, 1, 32 ** -0.5, core.mid, rope=True)
    prep_stage(core, 9, "router")
    moe_stage(core, 9, True, store=True)


def columns(a):
    out = np.zeros((P, a.shape[1]), np.float32)
    out[:a.shape[0]] = a
    return out


def rows(v):
    return np.broadcast_to(v.reshape(1, -1), (P, v.size))


def head_columns(w, heads, dim, groups):
    out = np.zeros((P, groups, 4, 32), np.float32)
    out[..., :dim] = w.T.reshape(P, groups, 4, dim)
    return out.reshape(P, groups * P)


def head_bias(v, dim, groups):
    out = np.zeros((4, 32, groups), np.float32)
    out[:, :dim] = v.reshape(groups, 4, dim).transpose(1, 2, 0)
    return out.reshape(P, groups)


def hidden_rows(w):
    return w.reshape(-1, P, w.shape[1]).transpose(1, 0, 2).reshape(P, -1)


def half_turned(w):
    return w.reshape(P, 4, 2, 16)[:, :, ::-1].reshape(P, P)


def rope_tables():
    inv_freq = 1.0 / 10000.0 ** (np.arange(0, 32, 2, dtype=np.float32) / 32)
    freqs = np.outer(np.arange(N, dtype=np.float32), inv_freq)
    cos, sin = np.cos(freqs).T.astype(np.float32), np.sin(freqs).T.astype(np.float32)
    return np.tile(np.concatenate([cos, cos]), (4, 1)), np.tile(np.concatenate([-sin, sin]), (4, 1))


def pack(a):
    w = {}
    qkv, bqkv = a["L1_gnn_Wqkv"], a["L1_gnn_bqkv"]
    for tag, ws, bs, wo, bo in (
        ("0", [a["L0_gnn_W" + c] for c in "qkv"], [a["L0_gnn_b" + c] for c in "qkv"], a["L0_gnn_Wo"], a["L0_gnn_bo"]),
        ("1", [qkv[i * D:(i + 1) * D] for i in range(3)], [bqkv[i * D:(i + 1) * D] for i in range(3)], a["L1_gnn_Wo"], a["L1_gnn_bo"]),
    ):
        w["wq" + tag], w["wk" + tag] = (head_columns(x, 8, 16, 2) for x in ws[:2])
        w["bq" + tag], w["bk" + tag] = (head_bias(x, 16, 2) for x in bs[:2])
        w["wv" + tag], w["bv" + tag], w["wo" + tag], w["bo" + tag] = ws[2].T, rows(bs[2]), wo.T, rows(bo)
    w["w_ih"], w["w_hh"] = a["L0_ffn_W_ih"].T, a["L0_ffn_W_hh"].T
    w["b_ih"], w["b_hh"] = a["L0_ffn_b_ih"].reshape(4, P).T, a["L0_ffn_b_hh"].reshape(4, P).T
    w["w_lin"] = np.repeat(a["L0_ffn_W_lin"].T, P, axis=1)
    w["b_lin"] = rows(a["L0_ffn_b_lin"])
    w["fw"], w["bw"] = a["L0_ffn_fw_att"].T, a["L0_ffn_bw_att"].T
    w["f1w1"] = a["L1_gnn_W1"].T
    w["f1w2"] = hidden_rows(a["L1_gnn_W2"].T)
    w["f1b1"] = a["L1_gnn_b1"].reshape(4, P).T
    w["f1b2"], w["g1"], w["be1"], w["g2"], w["be2"] = (rows(a["L1_gnn_" + n]) for n in ("b2", "ln1_g", "ln1_b", "ln2_g", "ln2_b"))
    w["mw1"], w["mw2"], w["mb1"] = a["L1_ffn_w1"], hidden_rows(a["L1_ffn_w2"]), a["L1_ffn_b1"].reshape(4, P).T
    w["mb2"], w["mwr"], w["mbr"] = rows(a["L1_ffn_b2"]), a["L1_ffn_wr"], rows(a["L1_ffn_br"])
    w["gw2"], w["gwt2"], w["ga2"] = a["L2_gnn_W"], a["L2_gnn_W"].T, a["L2_gnn_a"].reshape(2, P).T
    w["gw3"], w["gwt3"], w["ga3"] = a["L3_gnn_W"].T, a["L3_gnn_W"], a["L3_gnn_a"].reshape(2, P).T
    w["ew1"] = a["L2_ffn_W1"].transpose(1, 0, 2).reshape(D, -1)
    w["ew2"] = hidden_rows(a["L2_ffn_W2"].reshape(-1, D))
    w["eb1"] = a["L2_ffn_b1"].reshape(-1, P).T
    w["eb2"] = columns(a["L2_ffn_b2"])
    w["eg"], w["ebt"], w["er"], w["ebr"] = a["L2_ffn_ln_g"].T, a["L2_ffn_ln_b"].T, a["L2_ffn_Wr"], rows(a["L2_ffn_br"])
    w["wq3"], w["wqr3"] = a["L3_ffn_wq"].T, half_turned(a["L3_ffn_wq"].T)
    both = lambda v: np.repeat(v.T.reshape(P, 2, 32), 2, axis=1).reshape(P, P)
    w["wk3"], w["wkr3"], w["wv3"] = both(a["L3_ffn_wk"]), half_turned(both(a["L3_ffn_wk"])), both(a["L3_ffn_wv"])
    w["wo3"], w["ln1w"], w["ln2w"] = a["L3_ffn_wo"].T, a["L3_ffn_ln1_w"].reshape(P, 1), a["L3_ffn_ln2_w"].reshape(P, 1)
    w["cos"], w["sin"] = rope_tables()
    w["hw1"] = a["L3_ffn_w1"].transpose(2, 0, 1).reshape(D, -1)
    w["hw3"] = a["L3_ffn_w3"].transpose(2, 0, 1).reshape(D, -1)
    padded = np.zeros((8, 3 * P, D), np.float32)
    padded[:, :341] = a["L3_ffn_w2"].transpose(0, 2, 1)
    w["hw2"] = hidden_rows(padded.reshape(-1, D))
    w["hr"] = a["L3_ffn_router_w"].T
    out = np.zeros((P, COLUMNS), np.float32)
    for name, (at, n) in PLACE.items():
        out[:, at:at + n] = w[name]
    return out


def kernel(**inputs):
    import concourse.bacc as _bacc
    from concourse.bass_utils import run_bass_kernel_spmd as _run

    a = {name: np.asarray(v) for name, v in inputs.items()}
    sent = {"x": np.ascontiguousarray(a["x"]), "adj": np.ascontiguousarray(a["adj"]), "weights": pack(a)}
    nc = _bacc.Bacc("TRN2", target_bir_lowering=False, num_devices=1)
    dram = {n: nc.dram_tensor(n, v.shape, mybir.dt.from_np(v.dtype), kind="ExternalInput").ap() for n, v in sent.items()}
    dram["out"] = nc.dram_tensor("out", (B, N, D), F32, kind="ExternalOutput").ap()
    with ExitStack() as ctx:
        program(Core(nc, ctx, dram))
    r = _run(nc, [sent], core_ids=[0])
    return r.results[0]["out"]
```

```python
from contextlib import ExitStack

import numpy as np

import concourse.bass as bass
from concourse import mybir

F32 = mybir.dt.float32
BF16 = mybir.dt.bfloat16
I32 = mybir.dt.int32
ALU = mybir.AluOpType
ACT = mybir.ActivationFunctionType
AX = mybir.AxisListType

P = 128
B = 16
N = 512
D = 128
T = N // P
BIG = 1e30
LN_EPS = 1e-5


class Mem:

    def __init__(self, nc, ctx, tag):
        self.nc, self.ctx, self.tag, self.sems = nc, ctx, tag, []
        ctx.callback(self.clear)

    def sb(self, name, shape, dt=F32):
        return self.ctx.enter_context(self.nc.sbuf_tensor(f"{self.tag}_{name}", shape, dt))

    def ps(self, name, shape=(P, 512), dt=F32):
        return self.ctx.enter_context(self.nc.psum_tensor(f"{self.tag}_{name}", list(shape), dt))

    def sem(self, name):
        self.sems.append(self.ctx.enter_context(self.nc.semaphore(f"{self.tag}_{name}")))
        return self.sems[-1]

    def clear(self):
        numbers = sorted(sem.num for sem in self.sems)
        first = min(numbers, default=0)
        for n, after in zip(numbers, numbers[1:] + [None]):
            if after != n + 1:
                self.nc.gpsimd.sem_clear(range(first, n + 1))
                first = after
        self.nc.all_engine_barrier()


class Chain:

    def __init__(self, engine, sem, base=0):
        self.engine, self.sem, self.base, self.n = engine, sem, base, 0

    def step(self, ins):
        ins.then_inc(self.sem, 1)
        self.n += 1

    def settle(self):
        self.engine.wait_ge(self.sem, self.base + self.n)


class Core:

    def __init__(self, nc, ctx, dram):
        m = Mem(nc, ctx, "core")
        self.nc, self.dram = nc, dram
        self.x_res = m.sb("x_res", [P, B, T, D])
        self.mid = m.sb("mid", [P, B, T, D])
        self.x_stat = m.sb("x_stat", [P, B, T, 2])
        self.stat2 = m.sb("stat2", [P, B, T, 2])
        self.gate = m.sb("gate", [P, B, T, 8])
        self.ident = m.sb("ident", [P, P])
        self.ident_bf = m.sb("ident_bf", [P, P], BF16)
        self.passed = {nc.vector.engine: m.sem("passed_dve"), nc.gpsimd.engine: m.sem("passed_pool")}
        self.params = [m.sb(f"params{i}", [P, w]) for i, w in enumerate(REGION)]
        self.params_in = [m.sem(f"params_in{k}") for k in range(len(STAGES))]

    def load_params(self, sp, k):
        if k == len(SPAN):
            return
        lo, hi = SPAN[k]
        sp.dma_start(self.params[k % 2][:, 0:hi - lo], self.dram["weights"][:, lo:hi]).then_inc(self.params_in[k], 16)

    def param(self, k, name):
        lo, n = PLACE[name]
        return self.params[k % 2][:, lo - SPAN[k][0]:lo - SPAN[k][0] + n]


def apart(engine, core):
    engine.sem_inc(core.passed[engine.engine], 1)


class Spare:

    def __init__(self, core, k):
        self.region, self.at = core.params[k % 2], SPAN[k][1] - SPAN[k][0]

    def sb(self, shape, dt=F32):
        words = int(np.prod(shape[1:])) * (2 if dt == BF16 else 4) // 4
        flat_ap = self.region[:, self.at:self.at + words]
        self.at += words
        assert self.at <= self.region.shape[1]
        if dt != F32:
            flat_ap = flat_ap.bitcast(dt)
        if len(shape) == 2:
            return flat_ap
        return flat_ap.rearrange("p (a b) -> p a b", a=shape[1])


def layout():
    return [
        ("mha0", [("wq0", 256), ("wk0", 256), ("wv0", 128), ("wo0", 128), ("bq0", 2), ("bk0", 2), ("bv0", 128), ("bo0", 128)]),
        ("lstm", [("w_ih", 512), ("w_hh", 512), ("b_ih", 4), ("b_hh", 4), ("w_lin", 256), ("b_lin", 2), ("fw", 1), ("bw", 1)]),
        ("mha1", [("wq1", 256), ("wk1", 256), ("wv1", 128), ("wo1", 128), ("bq1", 2), ("bk1", 2), ("bv1", 128), ("bo1", 128)]),
        ("ffn1", [("f1w1", 512), ("f1w2", 512), ("f1b1", 4), ("f1b2", 128), ("g1", 128), ("be1", 128), ("g2", 128), ("be2", 128)]),
        ("mod", [("mw1", 512), ("mw2", 512), ("mb1", 4), ("mb2", 128), ("mwr", 1), ("mbr", 1)]),
        ("gat2", [("gw2", 128), ("gwt2", 128), ("ga2", 2)]),
        ("moe2", [("ew1", 4096), ("ew2", 4096), ("eb1", 32), ("eb2", 128), ("eg", 8), ("ebt", 8), ("er", 8), ("ebr", 8)]),
        ("gat3", [("gw3", 128), ("gwt3", 128), ("ga3", 2)]),
        ("mha3", [("wq3", 128), ("wqr3", 128), ("wk3", 128), ("wkr3", 128), ("wv3", 128), ("wo3", 128), ("ln1w", 1), ("cos", 512), ("sin", 512)]),
        ("moe3", [("hw1", 8 * 341), ("hw3", 8 * 341), ("hw2", 8 * 3 * 128), ("hr", 8), ("ln2w", 1)]),
    ]


def spans():
    place, span, at = {}, [], 0
    for _, parts in layout():
        start = at
        for name, n in parts:
            place[name] = (at, n)
            at += n
        span.append((start, at))
    return place, span, at


PLACE, SPAN, COLUMNS = spans()
STAGES = [name for name, _ in layout()]
REGION = [max(hi - lo for lo, hi in SPAN[i::2]) for i in range(2)]


def row_stats(dve, chain, core, six, two, tile):
    for t in range(T):
        chain.step(dve.bn_stats(six[:, t, :], tile[:, t, :]))
    chain.settle()
    apart(dve, core)
    for t in range(T):
        chain.step(dve.bn_aggr(two[:, t, :], six[:, t, :]))


WRITE_STEPS = 2 * T + 3


def write_x(dve, chain, core, b, change, base, upd, six, two):
    chain.step(dve.tensor_tensor(upd[:, :, :], change, base, ALU.add))
    chain.settle()
    apart(dve, core)
    chain.step(dve.tensor_copy(core.x_res[:, b], upd[:, :, :]))
    row_stats(dve, chain, core, six, two, upd)
    chain.settle()
    apart(dve, core)
    chain.step(dve.tensor_copy(core.x_stat[:, b], two[:, :, :]))
    chain.settle()


def rsqrt_stats(pool, done, rstd, shift, stat, scratch, half, eps, rms=False, part=None):
    chain = Chain(pool, done, 5 if part == 1 else 0)
    if part != 1:
        chain.step(pool.memset(half, -0.5))
    if part is not None:
        some = slice(0, 1) if part == 0 else slice(1, B)
        rstd, shift, stat, scratch, half = (x[:, some] for x in (rstd, shift, stat, scratch, half))
    if rms:
        chain.step(pool.tensor_tensor(shift, stat[:, :, :, 0], stat[:, :, :, 0], ALU.mult))
        chain.settle()
        chain.step(pool.tensor_tensor(scratch, shift, stat[:, :, :, 1], ALU.add))
        chain.settle()
        chain.step(pool.tensor_scalar(scratch, scratch, eps, None, ALU.add))
    else:
        chain.step(pool.tensor_scalar(scratch, stat[:, :, :, 1], eps, None, ALU.add))
    chain.settle()
    chain.step(pool.tensor_tensor(rstd, scratch, half, ALU.pow))
    chain.settle()
    if not rms:
        chain.step(pool.tensor_tensor(shift, stat[:, :, :, 0], rstd, ALU.mult))
        chain.settle()
        chain.step(pool.tensor_scalar(shift, shift, -1.0, None, ALU.mult))
        chain.settle()


def over_features(ap):
    return ap.unsqueeze(2).broadcast_to([P, T, D])


def flat(ap):
    return ap.rearrange("p a b -> p (a b)")


def load_stage(core):
    nc = core.nc
    with ExitStack() as ctx:
        m = Mem(nc, ctx, "load")
        six = m.sb("six", [P, T, 6])
        two = m.sb("two", [P, T, 2])
        x_in = [m.sem(f"x_in{b}") for b in range(B)]
        ones_set, ident_set, bf_set, chain_sem = m.sem("ones_set"), m.sem("ident_set"), m.sem("bf_set"), m.sem("chain")
        block = ctx.enter_context(nc.Block())

        @block.sync
        def _(sp):
            for b in range(B):
                sp.dma_start(core.x_res[:, b], core.dram["x"][b].rearrange("(t p) d -> p t d", p=P)).then_inc(x_in[b], 16)
                if b == 0:
                    core.load_params(sp, 0)

        @block.gpsimd
        def _(pool):
            pool.memset(core.ident[:, :], 0.0).then_inc(ones_set, 1)
            pool.wait_ge(ones_set, 1)
            pool.affine_select(out=core.ident[:, :], in_=core.ident[:, :], compare_op=ALU.not_equal, fill=1.0,
                               base=0, pattern=[[-1, P]], channel_multiplier=1).then_inc(ident_set, 1)
            pool.wait_ge(ident_set, 1)
            pool.tensor_copy(core.ident_bf[:, :], core.ident[:, :]).then_inc(bf_set, 1)

        @block.vector
        def _(dve):
            chain = Chain(dve, chain_sem)
            for b in range(B):
                dve.wait_ge(x_in[b], 16)
                row_stats(dve, chain, core, six, two, core.x_res[:, b])
                chain.settle()
                apart(dve, core)
                chain.step(dve.tensor_copy(core.x_stat[:, b], two[:, :, :]))


def all_graphs(engine, graph):
    graph(0, 0, first=True)
    with engine.Fori(0, B // 2 - 1) as j:
        for s in (1, 0):
            graph(j * 2 + 2 - s, s)
    graph(B - 1, 1, last=True)


def mha_stage(core, k, tag, heads, head_dim, groups, scale, out_res, sym=False, rope=False, from_xn=False):
    nc = core.nc
    with ExitStack() as ctx:
        m = Mem(nc, ctx, tag)
        items = 4 * T * groups
        rstd, shift = m.sb("rstd", [P, B, T]), m.sb("shift", [P, B, T])
        scratch, half = m.sb("scratch", [P, B, T]), m.sb("half", [P, B, T])
        spare = Spare(core, k)
        adj_raw = None if rope else spare.sb([P, T, N], I32)
        mask = [m.sb(f"mask{s}", [P, T, N], BF16) for s in range(1 if rope else 2)]
        xn = [spare.sb([P, T, D]) for s in range(2)]
        xT = spare.sb([P, N])
        neg_bq = m.sb("neg_bq", [P, 2])
        qT = [[m.sb(f"qT{g}{j}", [P, N]) for j in range(4)] for g in range(2)]
        kT = [m.sb(f"kT{g}", [P, N]) for g in range(2)]
        v32 = m.sb("v32", [P, T, heads, 32])
        PR = 4
        LAG = 3
        prob = m.sb("prob", [P, PR, N])
        bias = m.sb("bias", [P, PR])
        ncos, nsin, part = (m.sb("ncos", [P, N]), m.sb("nsin", [P, N]), spare.sb([P, 4, N])) if rope else (None,) * 3
        total = [m.sb(f"total{s}", [P, T, 4]) for s in range(2)]
        ORDER = (2, 0, 1, 3) if rope else range(T)
        projections = 4
        tile_of = lambda n: ORDER[n // 4 % T]
        keys = lambda t: t + 1 if rope else T
        probT = m.sb("probT", [P, 4, T, N]) if rope or from_xn else core.mid[:, :, :, :].rearrange("p (j u) t d -> p j u (t d)", j=4)
        oT = [spare.sb([P, N]) for g in range(groups)]
        rinv = m.sb("rinv", [P, T, 4])
        ctx_tok = spare.sb([P, T, D])
        ctxT = spare.sb([P, N])
        upd = spare.sb([P, T, D])
        six, two = m.sb("six", [P, T, 6]), m.sb("two", [P, T, 2])
        misc = [m.ps(f"misc{i}") for i in range(2)]
        score = [m.ps(f"score{i}") for i in range(2)]
        tpose = [m.ps(f"tpose{i}") for i in range(2)]
        o_ps = [m.ps(f"o{g}") for g in range(2)]

        names = ["stat_done", "half_mean", "adj_in", "xn_ready", "batch_free", "xt_in_psum", "xT_ready",
                 "proj_done", "qk_ready", "v_ready", "score_done", "score_taken", "prob_ready", "prob_free",
                 "probT_act", "probT_dve", "pv_done", "oT_ready", "back_done", "ctx_ready", "ctxt_in_psum",
                 "ctxT_ready", "attn_done", "chain", "const_set", "sym_chain", "tail", "adj_zero", "sym_done", "v_done", "adj_free", "rot_ready", "v32_set",
                 "zeros_set"]
        S = {n: m.sem(n) for n in names}
        if rope:
            at = {"values": 3, "back": 4, "ctx": 6, "out": 7, "v": 8, "rows": 9, "early": (10, 12)}
        else:
            at = {"values": 3, "back": 5, "ctx": 8, "out": 10, "v": 11, "late": (12, 13), "rows": 20, "early": (22, 24),
                  "adj": 26}
        wq, wk, wv, wo = (core.param(k, w + tag[-1]) for w in ("wq", "wk", "wv", "wo"))
        if rope:
            wqr, wkr = core.param(k, "wqr3"), core.param(k, "wkr3")
            cos, sin, ln1w = core.param(k, "cos"), core.param(k, "sin"), core.param(k, "ln1w")
        else:
            bq, bk, bv, bo = (core.param(k, w + tag[-1]) for w in ("bq", "bk", "bv", "bo"))
        block = ctx.enter_context(nc.Block())

        @block.sync
        def _(sp):
            core.load_params(sp, k + 1)
            if rope:
                return
            adj = core.dram["adj"].rearrange("b (t p) n -> b p t n", p=P)
            sp.dma_start(adj_raw[:, :, :], adj[0]).then_inc(S["adj_in"], 16)
            with sp.Fori(1, B) as b:
                sp.wait_ge(S["adj_free"], b)
                sp.dma_start(adj_raw[:, :, :], adj[b]).then_inc(S["adj_in"], 16)

        @block.gpsimd
        def _(pool):
            def scales(part):
                rsqrt_stats(pool, S["stat_done"], rstd[:, :, :], shift[:, :, :], core.stat2[:, :, :, :] if rope else core.x_stat[:, :, :, :],
                            scratch[:, :, :], half[:, :, :], 1e-6 if rope else LN_EPS, rms=rope, part=part)

            scales(0)
            if rope:
                pool.memset(mask[0][:, :, :], 0.0).then_inc(S["adj_zero"], 1)
                pool.wait_ge(S["adj_zero"], 1)
                pool.affine_select(out=mask[0][:, :, :], in_=mask[0][:, :, :], compare_op=ALU.is_ge, fill=BIG, base=0,
                                   pattern=[[P, T], [-1, N]], channel_multiplier=1).then_inc(S["adj_free"], 1)

            def graph(b, s, first=False, last=False):
                if rope:
                    pool.wait_ge(S["xT_ready"], b + 1)
                    pool.tensor_tensor(xn[s][:, :, :], core.mid[:, b], over_features(rstd[:, b]), ALU.mult)\
                        .then_inc(S["xn_ready"], 1)
                    if first:
                        scales(1)
                    pool.wait_ge(S["qk_ready"], 4 * b + 2 + 1)
                    if first:
                        pool.wait_ge(S["zeros_set"], 8)
                    for j in range(4):
                        rows = slice(32 * j, 32 * j + 32)
                        pool.tensor_tensor(qT[s][j][rows, :], part[rows, 0, :], part[rows, 1, :], ALU.add)\
                            .then_inc(S["rot_ready"], 1)
                    pool.wait_ge(S["rot_ready"], 5 * b + 4 + 5)
                    pool.wait_ge(S["qk_ready"], 4 * b + 4 + 1)
                    pool.tensor_tensor(kT[s][:, :], part[:, 2, :], part[:, 3, :], ALU.add).then_inc(S["rot_ready"], 1)
                    return
                pool.wait_ge(S["batch_free"], b + 1)
                pool.tensor_tensor(xn[s][:, :, :], core.x_res[:, b], over_features(rstd[:, b]), ALU.mult)\
                    .then_inc(S["half_mean"], 1)
                pool.wait_ge(S["half_mean"], b + 1)
                pool.tensor_tensor(xn[s][:, :, :], xn[s][:, :, :], over_features(shift[:, b]), ALU.add)\
                    .then_inc(S["xn_ready"], 1)
                pool.wait_ge(S["adj_in"], 16 * (b + 1))
                apart(pool, core)
                if sym:
                    pool.tensor_scalar(mask[s][:, :, :], adj_raw[:, :, :], 0.0, None, ALU.is_gt)\
                        .then_inc(S["adj_free"], 1)
                else:
                    pool.tensor_scalar(mask[s][:, :, :], adj_raw[:, :, :], 0.0, BIG, ALU.is_equal, ALU.mult)\
                        .then_inc(S["adj_free"], 1)
                if first:
                    scales(1)

            if rope:
                pool.sem_inc(S["rot_ready"], 5)
            all_graphs(pool, graph)

        @block.tensor
        def _(pe):
            pe.sem_inc(S["prob_free"], PR)
            pe.sem_inc(S["pv_done"], 1)
            pe.wait_ge(core.params_in[k], 16)

            def rows_in(b, s):
                pe.wait_ge(S["xn_ready"], b + 1)
                if rope:
                    pe.wait_ge(S["v_ready"], b + 1)
                else:
                    pe.wait_ge(S["qk_ready"], projections * b + 1)
                for t in range(T):
                    last = pe.transpose(misc[0][:, t * P:(t + 1) * P], xn[s][:, t, :], core.ident[:, :])
                last.then_inc(S["xt_in_psum"], 1)

            def project(b, n):
                if rope:
                    w = (wq, wqr, wk, wkr)[n]
                else:
                    w = (wq, wk)[n % 2][:, n // 2 * P:(n // 2 + 1) * P]
                if n == 0:
                    pe.wait_ge(S["xT_ready"], b + 1 + 2)
                    if rope:
                        pe.wait_ge(S["batch_free"], b + 1)
                elif n == 2 and not rope:
                    pe.wait_ge(S["batch_free"], b + 2)
                elif n == 3 and not rope:
                    pe.wait_ge(S["v_ready"], b + 1 + 1)
                elif n >= 2:
                    pe.wait_ge(S["qk_ready"], projections * b + n - 1 + 1)
                pe.matmul(misc[(n + 1) % 2][:, :], w, xT[:, :], start=True, stop=True).then_inc(S["proj_done"], 1)

            def project_v(b):
                for t in range(T):
                    last = pe.matmul(misc[0][:, t * D:(t + 1) * D], xT[:, t * P:(t + 1) * P], wv, start=True, stop=True)
                last.then_inc(S["v_done"], 1)

            def turn_adj(b, s):
                pe.wait_ge(S["adj_free"], b + 1)
                pe.wait_ge(S["qk_ready"], projections * b + 2 + 1)
                for t in range(T):
                    bank = misc[t // 2][:, :].bitcast(BF16)
                    for u in range(T):
                        last = pe.transpose(bank[:, t % 2 * N + u * P:t % 2 * N + (u + 1) * P],
                                            mask[s][:, u, t * P:(t + 1) * P], core.ident_bf[:, :])
                last.then_inc(S["sym_done"], 1)

            def scores(b, s, n):
                g, t, j = n // (4 * T), tile_of(n), n % 4
                if n == 0 and rope:
                    pe.wait_ge(S["rot_ready"], 5 * b + 5 + 5)
                elif n % (4 * T) == 0:
                    pe.wait_ge(S["qk_ready"], projections * b + 2 * g + 2 + 1)
                pe.wait_ge(S["score_taken"], items * b + n + 1)
                width = keys(t) * P
                pair = s if rope else g
                pe.matmul(score[n % 2][:, 0:width], qT[pair][j][:, t * P:(t + 1) * P], kT[pair][:, 0:width], start=True, stop=True)\
                    .then_inc(S["score_done"], 1)

            def transposes(b, n):
                pe.wait_ge(S["prob_ready"], items * b + n + 1)
                half_n = (items * b) // 2 if isinstance(b, int) else b * (items // 2)
                pe.wait_ge(S["probT_act"] if n % 2 == 0 else S["probT_dve"], half_n + n // 2 + 1)
                for u in range(keys(tile_of(n))):
                    last = pe.transpose(tpose[n % 2][:, u * P:(u + 1) * P], prob[:, n % PR, u * P:(u + 1) * P],
                                        core.ident[:, :])
                last.then_inc(S["prob_free"], 1)

            def values(b, g):
                done = b * (items // 2) + 2 * T * (g + 1) + 1
                if g == 0:
                    pe.wait_ge(S["v_ready"], b + 1 + 1)
                pe.wait_ge(S["oT_ready"], groups * b + g + 1)
                pe.wait_ge(S["probT_act"], done)
                pe.wait_ge(S["probT_dve"], done)
                for u in range(T):
                    for j in range(4):
                        first = u * P if rope else 0
                        last = pe.matmul(o_ps[g][32 * j:32 * j + 32, first:], v32[:, u, 4 * g + j, :], probT[:, j, u, first:],
                                         start=(u == 0), stop=(u == T - 1))
                last.then_inc(S["pv_done"], 1)

            def back_rows(b):
                for g in range(groups):
                    pe.wait_ge(S["oT_ready"], groups * (b + 1) + g + 1)
                    for t in range(T):
                        last = pe.transpose(misc[g][:, t * P:(t + 1) * P], oT[g][:, t * P:(t + 1) * P], core.ident[:, :])
                    last.then_inc(S["back_done"], 1)

            def turn_ctx(b):
                pe.wait_ge(S["ctx_ready"], groups * (b + 1))
                for t in range(T):
                    last = pe.transpose(misc[0][:, t * P:(t + 1) * P], ctx_tok[:, t, :], core.ident[:, :])
                last.then_inc(S["ctxt_in_psum"], 1)

            def project_out(b):
                pe.wait_ge(S["ctxT_ready"], b + 1)
                for t in range(T):
                    last = pe.matmul(misc[1][:, t * D:(t + 1) * D], ctxT[:, t * P:(t + 1) * P], wo, start=True, stop=True)
                last.then_inc(S["attn_done"], 1)

            def graph(b, s, first=False, last=False):
                for n in range(items):
                    scores(b, s, n)
                    if n == at["values"] and not first:
                        values(b - 1, groups - 1)
                    if n == at["values"] + 4 * T:
                        values(b, 0)
                    if n >= LAG:
                        transposes(b, n - LAG)
                    elif not first:
                        transposes(b - 1, items + n - LAG)
                    if not first:
                        if n == at["back"]:
                            back_rows(b - 1)
                        if n == at["ctx"]:
                            turn_ctx(b - 1)
                        if n == at["out"]:
                            project_out(b - 1)
                    if n == at["v"]:
                        project_v(b)
                    if not rope and n in at["late"]:
                        project(b, 2 + at["late"].index(n))
                    if not last:
                        if n == at["rows"]:
                            rows_in(b + 1, 1 - s)
                        if n in at["early"]:
                            early(b + 1, at["early"].index(n))
                        if sym and n == at["adj"]:
                            turn_adj(b + 1, 1 - s)

            def early(b, part):
                for n in (2 * part, 2 * part + 1) if rope else (part,):
                    project(b, n)

            rows_in(0, 0)
            early(0, 0)
            early(0, 1)
            if sym:
                turn_adj(0, 0)
            all_graphs(pe, graph)
            for n in range(items - LAG, items):
                transposes(B - 1, n)
            values(B - 1, groups - 1)
            back_rows(B - 1)
            turn_ctx(B - 1)
            project_out(B - 1)

        @block.scalar
        def _(act):
            act.sem_inc(S["probT_act"], 1)
            act.wait_ge(core.params_in[k], 16)
            if rope:
                act.mul(ncos[:, :], cos, -scale).then_inc(S["const_set"], 1)
                act.mul(nsin[:, :], sin, -scale).then_inc(S["const_set"], 1)
            else:
                act.mul(neg_bq[:, 0:groups], bq, -scale).then_inc(S["const_set"], 1)
                act.wait_ge(S["const_set"], 1)
                act.wait_ge(S["zeros_set"], 8)

            def copy_probT(b, n):
                act.wait_ge(S["prob_free"], items * b + n + 1 + PR)
                if n % (4 * T) == 0:
                    act.wait_ge(S["pv_done"], groups * b + n // (4 * T) + 1)
                t, j = tile_of(n), n % 4
                act.copy(probT[:, j, 0:keys(t), t * P:(t + 1) * P],
                         tpose[0][:, 0:keys(t) * P].rearrange("p (u q) -> p u q", u=keys(t)))\
                    .then_inc(S["probT_act"], 1)

            def take_qk(b, n):
                act.wait_ge(S["proj_done"], projections * b + n + 1)
                g, bank = n // 2, misc[(n + 1) % 2]
                if n % 2:
                    ins = act.activation(kT[g][:, :], bank[:, :], ACT.Identity, bias=bk[:, g:g + 1])
                else:
                    for j in range(4):
                        rows = slice(32 * j, 32 * j + 32)
                        ins = act.activation(qT[g][j][rows, :], bank[rows, :], ACT.Identity, bias=neg_bq[rows, g:g + 1],
                                             scale=-scale)
                ins.then_inc(S["qk_ready"], 1)

            def take_o(b, g):
                act.wait_ge(S["pv_done"], groups * b + g + 1 + 1)
                act.copy(oT[g][:, :], o_ps[g][:, :]).then_inc(S["oT_ready"], 1)

            def take_ctx(b):
                act.wait_ge(S["ctxt_in_psum"], b + 1)
                act.copy(ctxT[:, :], misc[0][:, :]).then_inc(S["ctxT_ready"], 1)

            def graph(b, s, first=False, last=False):
                for n in range(items):
                    act.wait_ge(S["score_taken"], items * b + n + 1 + 2)
                    tile = prob[:, n % PR, 0:keys(tile_of(n)) * P]
                    sums = {"accum_out": total[s][:, tile_of(n), n % 4:n % 4 + 1]} if rope else {}
                    act.activation(tile, tile, ACT.Exp, bias=bias[:, n % PR:n % PR + 1], scale=-1.0, **sums)\
                        .then_inc(S["prob_ready"], 1)
                    if (n - LAG) % 2 == 0:
                        if n >= LAG:
                            copy_probT(b, n - LAG)
                        elif not first:
                            copy_probT(b - 1, items + n - LAG)
                    if not first:
                        if n == at["values"] + 1:
                            take_o(b - 1, groups - 1)
                        if n == at["ctx"] + 1:
                            take_ctx(b - 1)
                    if rope:
                        continue
                    if n == at["values"] + 4 * T + 1:
                        take_o(b, 0)
                    if n - 1 in at["late"]:
                        take_qk(b, 2 + at["late"].index(n - 1))
                    if not last and n - 1 in at["early"]:
                        take_qk(b + 1, at["early"].index(n - 1))

            act.sem_inc(S["oT_ready"], groups)
            if not rope:
                act.sem_inc(S["qk_ready"], 1)
                take_qk(0, 0)
                take_qk(0, 1)
            all_graphs(act, graph)
            for n in range(items - LAG, items):
                if n % 2 == 0:
                    copy_probT(B - 1, n)
            take_o(B - 1, groups - 1)
            take_ctx(B - 1)

        @block.vector
        def _(dve):
            dve.sem_inc(S["batch_free"], 2)
            dve.sem_inc(S["score_taken"], 2)
            dve.sem_inc(S["probT_dve"], 1)
            dve.sem_inc(S["xT_ready"], 2)
            dve.sem_inc(S["v_ready"], 1)
            if rope:
                dve.sem_inc(S["qk_ready"], 1)
            dve.wait_ge(core.params_in[k], 16)
            for q in qT:
                for j in range(4):
                    dve.memset(q[j][:, :], 0.0).then_inc(S["zeros_set"], 1)
            dve.memset(v32[:, :, :, :], 0.0).then_inc(S["v32_set"], 1)
            dve.wait_ge(S["v32_set"], 1)
            if rope:
                dve.wait_ge(S["const_set"], 2)
                dve.wait_ge(S["adj_free"], 1)
            else:
                dve.memset(v32[:, :, :, head_dim:head_dim + 1], 1.0).then_inc(S["v32_set"], 1)

            def copy_probT(b, n):
                dve.wait_ge(S["prob_free"], items * b + n + 1 + PR)
                if n % (4 * T) == 1:
                    dve.wait_ge(S["pv_done"], groups * b + n // (4 * T) + 1)
                t, j = tile_of(n), n % 4
                dve.tensor_copy(probT[:, j, 0:keys(t), t * P:(t + 1) * P],
                                tpose[1][:, 0:keys(t) * P].rearrange("p (u q) -> p u q", u=keys(t)))\
                    .then_inc(S["probT_dve"], 1)

            def take_rows(b):
                dve.wait_ge(S["xt_in_psum"], b + 1)
                if rope:
                    dve.tensor_scalar(xT[:, :], misc[0][:, :], ln1w, None, ALU.mult).then_inc(S["xT_ready"], 1)
                else:
                    dve.tensor_copy(xT[:, :], misc[0][:, :]).then_inc(S["xT_ready"], 1)

            def rotate(b, half_):
                if half_ == 0:
                    dve.wait_ge(S["rot_ready"], 5 * b + 5)
                for n in (2 * half_, 2 * half_ + 1):
                    dve.wait_ge(S["proj_done"], 4 * b + n + 1)
                    dve.tensor_tensor(part[:, n, :], misc[(n + 1) % 2][:, :], (ncos[:, :], nsin[:, :], cos, sin)[n], ALU.mult)\
                        .then_inc(S["qk_ready"], 1)

            def take_v(b):
                dve.wait_ge(S["v_done"], b + 1)
                got = misc[0][:, :].rearrange("p (t h d) -> p t h d", t=T, h=heads)
                if rope:
                    dve.tensor_copy(v32[:, :, :, :], got).then_inc(S["v_ready"], 1)
                else:
                    dve.tensor_tensor(v32[:, :, :, 0:head_dim], got,
                                      bv.rearrange("p (h d) -> p h d", h=heads).unsqueeze(1).broadcast_to([P, T, heads, head_dim]),
                                      ALU.add).then_inc(S["v_ready"], 1)

            def join_adj(b, s, piece):
                chain = Chain(dve, S["sym_chain"], b * (T + 3) + (0, 1, 2, 2 + T)[piece])
                if piece < 2:
                    if piece == 0:
                        dve.wait_ge(S["sym_done"], b + 1)
                    pair = mask[s][:, 2 * piece:2 * piece + 2, :]
                    chain.step(dve.tensor_tensor(pair, pair, misc[piece][:, :].bitcast(BF16).rearrange("p (t n) -> p t n", t=2), ALU.add))
                elif piece == 2:
                    chain.settle()
                    for t in range(T):
                        own = mask[s][:, t, t * P:(t + 1) * P]
                        chain.step(dve.tensor_tensor(own, own, core.ident_bf[:, :], ALU.add))
                else:
                    chain.settle()
                    chain.step(dve.tensor_scalar(mask[s][:, :, :], mask[s][:, :, :], 0.0, BIG, ALU.is_equal, ALU.mult))
                    chain.settle()

            def normalise(b, s):
                chain = Chain(dve, S["chain"], b * groups)
                for g in range(groups):
                    dve.wait_ge(S["back_done"], groups * b + g + 1)
                    o = misc[g][:, :].rearrange("p (t j c) -> p t j c", t=T, j=4)
                    chain.step(dve.reciprocal(rinv[:, :, :], total[s][:, :, :] if rope else o[:, :, :, head_dim]))
                    chain.settle()
                    dve.tensor_tensor(ctx_tok[:, :, 4 * g * head_dim:4 * (g + 1) * head_dim].rearrange("p t (j c) -> p t j c", j=4),
                                      o[:, :, :, 0:head_dim], rinv[:, :, :].unsqueeze(3).broadcast_to([P, T, 4, head_dim]),
                                      ALU.mult).then_inc(S["ctx_ready"], 1)
                    dve.wait_ge(S["ctx_ready"], groups * b + g + 1)

            def take_out(b, s):
                dve.wait_ge(S["attn_done"], b + 1)
                base = core.mid[:, b] if rope else xn[s][:, :, :] if from_xn else core.x_res[:, b]
                dve.tensor_tensor(upd[:, :, :], misc[1][:, :].rearrange("p (t d) -> p t d", t=T), base, ALU.add)\
                    .then_inc(S["batch_free"], 1)

            def finish(b, piece):
                before = (0, 1, 2, 2 + T // 2, 2 + T, 2 + 2 * T)[piece]
                chain = Chain(dve, S["tail"], b * (2 * T + 3) + before)
                if piece == 0:
                    dve.wait_ge(S["batch_free"], b + 1 + 2)
                    if rope:
                        dve.sem_inc(S["tail"], 1)
                    else:
                        chain.step(dve.tensor_tensor(upd[:, :, :], upd[:, :, :], bo.unsqueeze(1).broadcast_to([P, T, D]), ALU.add))
                elif piece == 1:
                    chain.settle()
                    apart(dve, core)
                    chain.step(dve.tensor_copy(out_res[:, b], upd[:, :, :]))
                elif piece in (2, 3):
                    for t in (2 * piece - 4, 2 * piece - 3):
                        chain.step(dve.bn_stats(six[:, t, :], upd[:, t, :]))
                elif piece == 4:
                    chain.settle()
                    apart(dve, core)
                    for t in range(T):
                        chain.step(dve.bn_aggr(two[:, t, :], six[:, t, :]))
                else:
                    chain.settle()
                    apart(dve, core)
                    chain.step(dve.tensor_copy(core.x_stat[:, b], two[:, :, :]))

            def graph(b, s, first=False, last=False):
                dve.wait_ge(S["adj_free"], 1 if rope else b + 1)
                for n in range(items):
                    t = tile_of(n)
                    dve.wait_ge(S["score_done"], items * b + n + 1)
                    dve.wait_ge(S["prob_free"], items * b + n + 1)
                    apart(dve, core)
                    allowed = mask[0] if rope else mask[s]
                    width = keys(t) * P
                    dve.tensor_tensor_reduce(prob[:, n % PR, 0:width], score[n % 2][:, 0:width], allowed[:, t, 0:width], 1.0, 3e38,
                                             ALU.add, ALU.min, bias[:, n % PR:n % PR + 1])\
                        .then_inc(S["score_taken"], 1)
                    if (n - LAG) % 2 == 1:
                        if n >= LAG:
                            copy_probT(b, n - LAG)
                        elif not first:
                            copy_probT(b - 1, items + n - LAG)
                    if not first:
                        if n == at["back"] + 1:
                            normalise(b - 1, 1 - s)
                        if n == at["out"] + 1:
                            take_out(b - 1, 1 - s)
                        if 0 <= n - at["out"] - 2 < 6:
                            finish(b - 1, n - at["out"] - 2)
                    if n == at["v"] + 1:
                        take_v(b)
                    if not last:
                        if n == at["rows"] + 1:
                            take_rows(b + 1)
                        if rope and n - 1 in at["early"]:
                            rotate(b + 1, at["early"].index(n - 1))
                        if sym and n in JOIN:
                            join_adj(b + 1, 1 - s, JOIN.index(n))

            JOIN = [at["adj"] + i for i in (1, 2, 3, 5)] if sym else []
            take_rows(0)
            if rope:
                rotate(0, 0)
                rotate(0, 1)
            if sym:
                for piece in range(4):
                    join_adj(0, 0, piece)
            all_graphs(dve, graph)
            for n in range(items - LAG, items):
                if n % 2 == 1:
                    copy_probT(B - 1, n)
            normalise(B - 1, 1)
            take_out(B - 1, 1)
            for piece in range(6):
                finish(B - 1, piece)


def lstm_stage(core, k):
    nc = core.nc
    C = 16
    CB = C * B
    CHUNKS = N // C
    H_UNIT = 4096.0
    GATE = [0, 1, 3, 2]
    with ExitStack() as ctx:
        m = Mem(nc, ctx, "lstm")
        rstd, shift = m.sb("rstd", [P, B, T]), m.sb("shift", [P, B, T])
        scratch, half = m.sb("scratch", [P, B, T]), m.sb("half", [P, B, T])
        xn = [m.sb(f"xn{s}", [P, T, D]) for s in range(2)]
        xT = m.sb("xT", [P, N * B])
        hT = core.mid[:, :, :, :].rearrange("p b t d -> p b (t d)")
        w_part = [m.sb(f"w_part{i}", [P, 4 * P], BF16) for i in range(3)]
        w_rest = m.sb("w_rest", [P, 4 * P])
        gate_bias = m.sb("gate_bias", [P, 4])
        xg = [m.sb(f"xg{s}", [P, C, 4, B]) for s in range(2)]
        w_low = [m.sb(f"w_low{i}", [P, 4 * P], BF16) for i in range(2)]
        h_part = m.sb("h_part", [P, 2, B], mybir.dt.float16)
        hist = [m.sb(f"hist{s}", [P, C, B]) for s in range(2)]
        per_unit = m.sb("per_unit", [P, 1])
        sig = m.sb("sig", [P, 3, B])
        gc = m.sb("gc", [P, 2, B])
        prod = m.sb("prod", [P, 2, B])
        tanh_c = m.sb("tanh_c", [P, B])
        w_lin = m.sb("w_lin", [P, 2, P])
        ones = m.sb("ones", [P, N])
        logit0, gated, sums, before, after = ([m.sb(n, [P, N]), xT[:, i * N:(i + 1) * N]]
                                              for i, n in enumerate(("logit0", "gated", "sums", "before", "after")))
        upd = [m.sb(f"upd{s}", [P, T, D]) for s in range(2)]
        six, two = ([m.sb(f"{n}{s}", [P, T, w]) for s in range(2)] for n, w in (("six", 6), ("two", 2)))
        gates = [m.ps(f"gates{i}") for i in range(2)]
        xproj = [m.ps(f"xproj{i}") for i in range(2)]
        logit = [[m.ps(f"logit_ps{i}") for i in range(2)], xproj]
        tpose = [m.ps(f"tpose{i}") for i in range(2)]
        names = ["stat_done", "half_mean", "xn_ready", "xt_in_psum", "xT_act", "xT_dve", "w_parts", "w_chain", "xproj_done",
                 "xg_ready", "hi_ready", "low_ready", "h_full", "gates_done", "sig_ready", "tg_ready",
                 "prod_done", "c_ready", "tc_ready", "hist_saved", "logits_done", "logits_free",
                 "out_ready", "out_in_psum", "chain", "bias_set", "unit_set"]
        S = {n: m.sem(n) for n in names}
        par = lambda name: core.param(k, name)
        block = ctx.enter_context(nc.Block())

        @block.sync
        def _(sp):
            core.load_params(sp, k + 1)

        @block.gpsimd
        def _(pool):
            rsqrt_stats(pool, S["stat_done"], rstd[:, :, :], shift[:, :, :], core.x_stat, scratch[:, :, :],
                        half[:, :, :], LN_EPS)

            def normalise(b, s):
                pool.wait_ge(S["xt_in_psum"], b + 1)
                pool.tensor_tensor(xn[s][:, :, :], core.x_res[:, b], over_features(rstd[:, b]), ALU.mult)\
                    .then_inc(S["half_mean"], 1)

            with pool.Fori(0, B // 2) as j:
                for s in range(2):
                    normalise(j * 2 + s, s)

            def save(c, s):
                pool.wait_ge(S["h_full"], C * (c + 1) + 1)
                pool.tensor_tensor(hT[:, :, bass.ds(c * C, C)], hist[s][:, :, :].rearrange("p t b -> p b t"),
                                   per_unit[:, :].unsqueeze(2).broadcast_to([P, B, C]), ALU.mult)\
                    .then_inc(S["hist_saved"], 1)

            pool.memset(per_unit[:, :], 1.0 / H_UNIT).then_inc(S["unit_set"], 1)
            pool.wait_ge(S["unit_set"], 1)
            pool.sem_inc(S["hist_saved"], 2)
            with pool.Fori(0, CHUNKS // 2) as it:
                for s in range(2):
                    save(it * 2 + s, s)

        @block.tensor
        def _(pe):
            pe.sem_inc(S["xt_in_psum"], 2)
            pe.wait_ge(core.params_in[k], 16)

            def turn(b, s):
                pe.wait_ge(S["xn_ready"], b + 1)
                pe.wait_ge(S["xT_act" if s == 0 else "xT_dve"], j + 1)
                for t in range(T):
                    last = pe.transpose(tpose[s][:, t * P:(t + 1) * P], xn[s][:, t, :], core.ident[:, :])
                last.then_inc(S["xt_in_psum"], 1)

            with pe.Fori(0, B // 2) as j:
                for s in range(2):
                    turn(j * 2 + s, s)
            pe.wait_ge(S["xT_act"], B // 2 + 1)
            pe.wait_ge(S["xT_dve"], B // 2 + 1)

            def project(c, n):
                pe.wait_ge(S["xg_ready"], 4 * c + n + 1)
                g = GATE[n]
                pe.matmul(xproj[n % 2][:, 0:CB], par("w_ih")[:, g * P:(g + 1) * P], xT[:, bass.ds(c * CB, CB)],
                          start=True, stop=True).then_inc(S["xproj_done"], 1)

            def seed(step, c, s, t):
                if t == 0:
                    pe.wait_ge(S["xg_ready"], 4 * c + 4 + 2)
                pe.matmul(gates[t % 2][:, 0:4 * B], core.ident[:, :], xg[s][:, t, :, :].rearrange("p g b -> p (g b)"),
                          start=True, stop=False)

            def recur(step, t):
                for part, sem, weights in ((0, "hi_ready", w_part), (1, "low_ready", w_low)):
                    pe.wait_ge(S[sem], step + 1)
                    for w in weights:
                        for n in range(4):
                            g = GATE[n]
                            last = pe.matmul(gates[t % 2][:, n * B:(n + 1) * B], w[:, g * P:(g + 1) * P],
                                             h_part[:, part, :], start=False, stop=(w is w_low[1] and n == 3))
                last.then_inc(S["gates_done"], 1)

            def chunk(c, s, last):
                for t in range(C):
                    recur(c * C + t, t)
                    if t < C - 1:
                        seed(c * C + t + 1, c, s, t + 1)
                    elif not last:
                        seed(c * C + t + 1, c + 1, 1 - s, 0)
                    if not last and 1 <= t <= 4:
                        project(c + 1, t - 1)

            for n in range(4):
                project(0, n)
            pe.wait_ge(S["w_parts"], 5)
            seed(0, 0, 0, 0)
            with pe.Fori(0, CHUNKS // 2 - 1) as it:
                for s in range(2):
                    chunk(it * 2 + s, s, False)
            chunk(CHUNKS - 2, 0, False)
            chunk(CHUNKS - 1, 1, True)

            def labels(j):
                for s in range(2):
                    pe.wait_ge(S["logits_free"], j * 2 + s + 1)
                    for i in range(2):
                        last = pe.matmul(logit[s][i][:, :], w_lin[:, i, :], hT[:, j * 2 + s, :], start=True, stop=True)
                    last.then_inc(S["logits_done"], 1)

            def back(j):
                for s in range(2):
                    pe.wait_ge(S["out_ready"], j * 2 + s + 1)
                    for t in range(T):
                        last = pe.transpose(tpose[s][:, t * P:(t + 1) * P], before[s][:, t * P:(t + 1) * P],
                                            core.ident[:, :])
                    last.then_inc(S["out_in_psum"], 1)

            pe.wait_ge(S["hist_saved"], CHUNKS + 2)
            labels(0)
            with pe.Fori(0, B // 2 - 1) as j:
                labels(j + 1)
                back(j)
            back(B // 2 - 1)

        @block.scalar
        def _(act):
            act.sem_inc(S["xT_act"], 1)
            act.sem_inc(S["xg_ready"], 2)
            act.wait_ge(core.params_in[k], 16)
            with act.Fori(0, B // 2) as j:
                act.wait_ge(S["xt_in_psum"], j * 2 + 1 + 2)
                act.copy(xT[:, :].rearrange("p (t b) -> p b t", b=B)[:, j * 2, :], tpose[0][:, :]).then_inc(S["xT_act"], 1)
            act.wait_ge(S["bias_set"], 1)

            def bring(c, s, n):
                act.wait_ge(S["xproj_done"], 4 * c + n + 1)
                act.activation(xg[s][:, :, n, :], xproj[n % 2][:, 0:CB].rearrange("p (t b) -> p t b", b=B),
                               ACT.Identity, bias=gate_bias[:, GATE[n]:GATE[n] + 1]).then_inc(S["xg_ready"], 1)

            def step(g, t):
                act.wait_ge(S["gates_done"], g + 1)
                bank = gates[t % 2]
                act.activation(sig[:, :, :], bank[:, 0:3 * B].rearrange("p (g b) -> p g b", b=B), ACT.Sigmoid)\
                    .then_inc(S["sig_ready"], 1)
                act.activation(gc[:, 0, :], bank[:, 3 * B:4 * B], ACT.Tanh).then_inc(S["tg_ready"], 1)
                act.wait_ge(S["c_ready"], g + 1)
                act.activation(tanh_c[:, :], gc[:, 1, :], ACT.Tanh).then_inc(S["tc_ready"], 1)

            def chunk(c, s, last):
                for t in range(C):
                    step(c * C + t, t)
                    if not last and 1 <= t <= 4:
                        bring(c + 1, 1 - s, t - 1)

            for n in range(4):
                bring(0, 0, n)
            with act.Fori(0, CHUNKS // 2 - 1) as it:
                for s in range(2):
                    chunk(it * 2 + s, s, False)
            chunk(CHUNKS - 2, 0, False)
            chunk(CHUNKS - 1, 1, True)

        @block.vector
        def _(dve):
            dve.sem_inc(S["xT_dve"], 1)
            dve.wait_ge(core.params_in[k], 16)
            dve.tensor_tensor(gate_bias[:, :], par("b_ih"), par("b_hh"), ALU.add).then_inc(S["bias_set"], 1)
            dve.tensor_copy(w_part[0][:, :], par("w_hh")).then_inc(S["w_parts"], 1)
            dve.wait_ge(S["w_parts"], 1)
            dve.tensor_tensor(w_rest[:, :], par("w_hh"), w_part[0][:, :], ALU.subtract).then_inc(S["w_chain"], 1)
            dve.wait_ge(S["w_chain"], 1)
            dve.tensor_copy(w_part[1][:, :], w_rest[:, :]).then_inc(S["w_parts"], 1)
            dve.wait_ge(S["w_parts"], 2)
            dve.tensor_tensor(w_part[2][:, :], w_rest[:, :], w_part[1][:, :], ALU.subtract).then_inc(S["w_parts"], 1)
            for i in range(2):
                dve.tensor_scalar(w_low[i][:, :], w_part[i][:, :], 1.0 / H_UNIT, None, ALU.mult).then_inc(S["w_parts"], 1)
            dve.memset(ones[:, :], 1.0).then_inc(S["w_chain"], 1)
            for i in range(2):
                dve.tensor_copy(w_lin[:, i, :], par("w_lin")[:, i * P:(i + 1) * P]).then_inc(S["w_chain"], 1)
            dve.memset(gc[:, :, :], 0.0).then_inc(S["h_full"], 1)
            for part, sem in enumerate(("hi_ready", "low_ready")):
                dve.memset(h_part[:, part, :], 0.0).then_inc(S[sem], 1)
            with dve.Fori(0, B // 2) as j:
                for s in range(2):
                    dve.wait_ge(S["half_mean"], j * 2 + s + 1)
                    dve.tensor_tensor(xn[s][:, :, :], xn[s][:, :, :], over_features(shift[:, j * 2 + s]), ALU.add)\
                        .then_inc(S["xn_ready"], 1)
                dve.wait_ge(S["xt_in_psum"], j * 2 + 2 + 2)
                dve.tensor_copy(xT[:, :].rearrange("p (t b) -> p b t", b=B)[:, j * 2 + 1, :], tpose[1][:, :])\
                    .then_inc(S["xT_dve"], 1)

            def step(g, s, t):
                dve.wait_ge(S["sig_ready"], g + 1)
                dve.wait_ge(S["tg_ready"], g + 1)
                dve.tensor_tensor(prod[:, :, :], sig[:, 0:2, :], gc[:, :, :], ALU.mult).then_inc(S["prod_done"], 1)
                dve.wait_ge(S["prod_done"], g + 1)
                dve.tensor_tensor(gc[:, 1, :], prod[:, 0, :], prod[:, 1, :], ALU.add).then_inc(S["c_ready"], 1)
                dve.wait_ge(S["tc_ready"], g + 1)
                dve.tensor_tensor(h_part[:, 0, :], sig[:, 2, :], tanh_c[:, :], ALU.mult).then_inc(S["hi_ready"], 1)
                dve.scalar_tensor_tensor(hist[s][:, t, :], sig[:, 2, :], H_UNIT, tanh_c[:, :], ALU.mult, ALU.mult)\
                    .then_inc(S["h_full"], 1)
                dve.wait_ge(S["hi_ready"], g + 2)
                dve.wait_ge(S["h_full"], g + 2)
                dve.scalar_tensor_tensor(h_part[:, 1, :], h_part[:, 0, :], -H_UNIT, hist[s][:, t, :], ALU.mult, ALU.add)\
                    .then_inc(S["low_ready"], 1)

            def chunk(c, s):
                dve.wait_ge(S["hist_saved"], c + 1)
                for t in range(C):
                    step(c * C + t, s, t)

            with dve.Fori(0, CHUNKS // 2) as it:
                for s in range(2):
                    chunk(it * 2 + s, s)

            dve.sem_inc(S["logits_free"], 2)
            dve.wait_ge(S["hist_saved"], CHUNKS + 2)
            STEPS = 2 * (7 + 2 * T + 3)
            with dve.Fori(0, B // 2) as j:
                chain = Chain(dve, S["chain"], j * STEPS)
                h = [hT[:, j * 2 + s, :] for s in range(2)]
                for s in range(2):
                    dve.wait_ge(S["logits_done"], j * 2 + s + 1)
                    chain.step(dve.tensor_scalar(logit0[s][:, :], logit[s][0][:, :], par("b_lin")[:, 0:1], None, ALU.add))
                chain.settle()
                for s in range(2):
                    dve.scalar_tensor_tensor(gated[s][:, :], logit[s][1][:, :], par("b_lin")[:, 1:2], logit0[s][:, :], ALU.add,
                                             ALU.is_gt).then_inc(S["logits_free"], 1)
                dve.wait_ge(S["logits_free"], j * 2 + 2 + 2)
                for s in range(2):
                    chain.step(dve.tensor_tensor(gated[s][:, :], gated[s][:, :], h[s], ALU.mult))
                chain.settle()
                for s in range(2):
                    chain.step(dve.tensor_tensor_scan(sums[s][:, :], ones[:, :], gated[s][:, :], 0.0, ALU.mult, ALU.add))
                chain.settle()
                for s in range(2):
                    chain.step(dve.tensor_tensor(before[s][:, :], sums[s][:, :], gated[s][:, :], ALU.subtract))
                    chain.step(dve.tensor_scalar(after[s][:, :], sums[s][:, :], -1.0, sums[s][:, N - 1:N], ALU.mult, ALU.add))
                chain.settle()
                for s in range(2):
                    chain.step(dve.scalar_tensor_tensor(before[s][:, :], before[s][:, :], par("fw"), h[s], ALU.mult, ALU.add))
                    chain.step(dve.scalar_tensor_tensor(after[s][:, :], after[s][:, :], par("bw"), h[s], ALU.mult, ALU.add))
                chain.settle()
                for s in range(2):
                    dve.tensor_tensor(before[s][:, :], before[s][:, :], after[s][:, :], ALU.add).then_inc(S["out_ready"], 1)
                for s in range(2):
                    dve.wait_ge(S["out_in_psum"], j * 2 + s + 1)
                    chain.step(dve.tensor_tensor(upd[s][:, :, :], tpose[s][:, :].rearrange("p (t d) -> p t d", t=T),
                                                 core.x_res[:, j * 2 + s], ALU.add))
                chain.settle()
                for s in range(2):
                    for t in range(T):
                        chain.step(dve.bn_stats(six[s][:, t, :], upd[s][:, t, :]))
                for s in range(2):
                    chain.step(dve.tensor_copy(core.x_res[:, j * 2 + s], upd[s][:, :, :]))
                chain.settle()
                apart(dve, core)
                for s in range(2):
                    for t in range(T):
                        chain.step(dve.bn_aggr(two[s][:, t, :], six[s][:, t, :]))
                chain.settle()
                apart(dve, core)
                for s in range(2):
                    chain.step(dve.tensor_copy(core.x_stat[:, j * 2 + s], two[s][:, :, :]))
                chain.settle()
                assert chain.n == STEPS, (chain.n, STEPS)


def ffn_tiles(pe, hid_ps, hid_done, hid_free, w1, xT, base, tiles):
    for n in range(tiles):
        pe.wait_ge(hid_free, base + n + 1)
        pe.matmul(hid_ps[n % len(hid_ps)][:, :], w1[:, n * P:(n + 1) * P], xT, start=True, stop=True)\
            .then_inc(hid_done, 1)


def ffn1_stage(core, k):
    nc = core.nc
    H = 4
    with ExitStack() as ctx:
        m = Mem(nc, ctx, "ffn1")
        rstd, shift = m.sb("rstd", [P, B, T]), m.sb("shift", [P, B, T])
        scratch, half = m.sb("scratch", [P, B, T]), m.sb("half", [P, B, T])
        y = [m.sb(f"y{s}", [P, T, D]) for s in range(2)]
        yT = [m.sb(f"yT{s}", [P, N]) for s in range(2)]
        hid = [m.sb(f"hid{s}", [P, H, N]) for s in range(2)]
        r = [m.sb(f"r{s}", [P, T, D]) for s in range(2)]
        upd = m.sb("upd", [P, T, D])
        six, two = m.sb("six", [P, T, 6]), m.sb("two", [P, T, 2])
        rstat = [m.sb(f"rstat{s}", [P, T, 2]) for s in range(2)]
        rv, rr, rs = m.sb("rv", [P, T]), [m.sb(f"rr{s}", [P, T]) for s in range(2)], [m.sb(f"rs{s}", [P, T]) for s in range(2)]
        tp = [m.ps(f"tp{s}") for s in range(2)]
        hid_ps = [m.ps(f"hid_ps{i}") for i in range(4)]
        out_ps = [m.ps(f"out_ps{s}") for s in range(2)]
        names = ["stat_done", "y_chain", "y_ready", "y_in_psum", "yT_ready", "hid_done", "hid_free",
                 "out_done", "r_chain", "r_ready", "norm_ready", "chain", "take_chain", "out_taken"]
        S = {n: m.sem(n) for n in names}
        par = lambda name: core.param(k, name)
        block = ctx.enter_context(nc.Block())

        @block.sync
        def _(sp):
            core.load_params(sp, k + 1)

        @block.gpsimd
        def _(pool):
            def scales(part):
                rsqrt_stats(pool, S["stat_done"], rstd[:, :, :], shift[:, :, :], core.x_stat[:, :, :, :], scratch[:, :, :],
                            half[:, :, :], LN_EPS, part=part)

            scales(0)
            pool.wait_ge(core.params_in[k], 16)
            row = lambda name: par(name).unsqueeze(1).broadcast_to([P, T, D])

            def first(b, s):
                chain = Chain(pool, S["y_chain"], b * 3)
                pool.wait_ge(S["y_in_psum"], b + 1)
                chain.step(pool.tensor_tensor(y[s][:, :, :], core.mid[:, b], over_features(rstd[:, b]), ALU.mult))
                chain.settle()
                chain.step(pool.tensor_tensor(y[s][:, :, :], y[s][:, :, :], over_features(shift[:, b]), ALU.add))
                chain.settle()
                chain.step(pool.tensor_tensor(y[s][:, :, :], y[s][:, :, :], row("g1"), ALU.mult))
                chain.settle()
                pool.tensor_tensor(y[s][:, :, :], y[s][:, :, :], row("be1"), ALU.add).then_inc(S["y_ready"], 1)

            def second(b, s):
                chain = Chain(pool, S["r_chain"], b * 2)
                pool.wait_ge(S["r_ready"], b + 1)
                apart(pool, core)
                chain.step(pool.tensor_scalar(rv[:, :], rstat[s][:, :, 1], LN_EPS, None, ALU.add))
                chain.settle()
                chain.step(pool.tensor_tensor(rr[s][:, :], rv[:, :], half[:, 0, :], ALU.pow))
                chain.settle()
                pool.tensor_tensor(rs[s][:, :], rstat[s][:, :, 0], rr[s][:, :], ALU.mult).then_inc(S["norm_ready"], 1)

            first(0, 0)
            scales(1)
            first(1, 1)
            with pool.Fori(0, B // 2 - 1) as j:
                for s in range(2):
                    first(j * 2 + s + 2, s)
                    second(j * 2 + s, s)
            second(B - 2, 0)
            second(B - 1, 1)

        @block.tensor
        def _(pe):
            pe.wait_ge(core.params_in[k], 16)

            pe.sem_inc(S["y_in_psum"], 2)

            def rows_in(b, s):
                pe.wait_ge(S["y_ready"], b + 1)
                turn(pe, core, tp[s], y[s]).then_inc(S["y_in_psum"], 1)

            def graph(b, s, first=False, last=False):
                pe.wait_ge(S["yT_ready"], b + 1)
                ffn_tiles(pe, hid_ps, S["hid_done"], S["hid_free"], par("f1w1"), yT[s][:, :], H * b, H)
                if not last:
                    rows_in(b + 1, 1 - s)
                pe.wait_ge(S["hid_free"], H * (b + 1) + 4)
                pe.wait_ge(S["out_taken"], b + 1)
                for t in range(T):
                    pe.matmul(out_ps[s][:, t * D:(t + 1) * D], yT[s][:, t * P:(t + 1) * P], core.ident[:, :],
                              start=True, stop=False)
                    for n in range(H):
                        ins = pe.matmul(out_ps[s][:, t * D:(t + 1) * D], hid[s][:, n, t * P:(t + 1) * P],
                                        par("f1w2")[:, n * D:(n + 1) * D], start=False, stop=(n == H - 1))
                ins.then_inc(S["out_done"], 1)

            rows_in(0, 0)
            all_graphs(pe, graph)

        @block.scalar
        def _(act):
            act.sem_inc(S["hid_free"], 4)
            act.wait_ge(core.params_in[k], 16)

            def rows_in(b, s):
                act.wait_ge(S["y_in_psum"], b + 1 + 2)
                act.copy(yT[s][:, :], tp[s][:, :]).then_inc(S["yT_ready"], 1)

            def graph(b, s, first=False, last=False):
                for n in range(H):
                    act.wait_ge(S["hid_done"], H * b + n + 1)
                    act.activation(hid[s][:, n, :], hid_ps[n][:, :], ACT.Relu, bias=par("f1b1")[:, n:n + 1])\
                        .then_inc(S["hid_free"], 1)
                if not last:
                    rows_in(b + 1, 1 - s)

            rows_in(0, 0)
            all_graphs(act, graph)

        @block.vector
        def _(dve):
            dve.sem_inc(S["out_taken"], 2)
            dve.wait_ge(core.params_in[k], 16)
            row = lambda name: par(name).unsqueeze(1).broadcast_to([P, T, D])

            def take(b, s):
                chain = Chain(dve, S["take_chain"], b * T)
                dve.wait_ge(S["out_done"], b + 1)
                o = out_ps[s][:, :].rearrange("p (t d) -> p t d", t=T)
                dve.tensor_tensor(r[s][:, :, :], o, row("f1b2"), ALU.add).then_inc(S["out_taken"], 1)
                dve.wait_ge(S["out_taken"], b + 1 + 2)
                for t in range(T):
                    chain.step(dve.bn_stats(six[:, t, :], r[s][:, t, :]))
                chain.settle()
                apart(dve, core)
                for t in range(T):
                    ins = dve.bn_aggr(rstat[s][:, t, :], six[:, t, :])
                ins.then_inc(S["r_ready"], 1)

            def give(b, s):
                chain = Chain(dve, S["chain"], b * STEPS)
                dve.wait_ge(S["norm_ready"], b + 1)
                for t in range(T):
                    chain.step(dve.tensor_scalar(r[s][:, t, :], r[s][:, t, :], rr[s][:, t:t + 1], rs[s][:, t:t + 1],
                                                 ALU.mult, ALU.subtract))
                chain.settle()
                chain.step(dve.tensor_tensor(r[s][:, :, :], r[s][:, :, :], row("g2"), ALU.mult))
                chain.settle()
                chain.step(dve.tensor_tensor(r[s][:, :, :], r[s][:, :, :], row("be2"), ALU.add))
                chain.settle()
                write_x(dve, chain, core, b, r[s][:, :, :], core.x_res[:, b], upd, six, two)
                assert chain.n == STEPS, chain.n

            def graph(b, s, first=False, last=False):
                take(b, s)
                if not first:
                    give(b - 1, 1 - s)

            STEPS = 2 + T + WRITE_STEPS
            all_graphs(dve, graph)
            give(B - 1, 1)


class Rows:

    def __init__(self, m, core, S, source, shifted=True):
        self.core, self.S, self.source, self.shifted = core, S, source, shifted
        self.rstd, self.shift = m.sb("rstd", [P, B, T]), m.sb("shift", [P, B, T])
        self.scratch, self.half = m.sb("scratch", [P, B, T]), m.sb("half", [P, B, T])
        self.xn = [m.sb(f"xn{s}", [P, T, D]) for s in range(2)]

    def scales(self, pool, stat, eps, part=None):
        rsqrt_stats(pool, self.S["stat_done"], self.rstd[:, :, :], self.shift[:, :, :], stat[:, :, :, :],
                    self.scratch[:, :, :], self.half[:, :, :], eps, rms=not self.shifted, part=part)

    def normalise_all(self, pool, stat, eps):
        def graph(b, s, first=False, last=False):
            self.normalise(pool, b, s)
            if first:
                self.scales(pool, stat, eps, part=1)

        self.scales(pool, stat, eps, part=0)
        all_graphs(pool, graph)

    def normalise(self, pool, b, s):
        S, xn = self.S, self.xn[s][:, :, :]
        pool.wait_ge(S["xn_free"], b + 1)
        if not self.shifted:
            pool.tensor_tensor(xn, self.source[:, b], over_features(self.rstd[:, b]), ALU.mult).then_inc(S["xn_ready"], 1)
            return
        pool.tensor_tensor(xn, self.source[:, b], over_features(self.rstd[:, b]), ALU.mult).then_inc(S["half_mean"], 1)
        pool.wait_ge(S["half_mean"], b + 1)
        pool.tensor_tensor(xn, xn, over_features(self.shift[:, b]), ALU.add).then_inc(S["xn_ready"], 1)

    NAMES = ["stat_done", "xn_free", "half_mean", "xn_ready"]


def pairs(engine, graph, first=0, last=B):
    with engine.Fori(first // 2, last // 2) as j:
        for s in range(2):
            graph(j * 2 + s, s)


def turn(pe, core, bank, tile):
    for t in range(T):
        last = pe.transpose(bank[:, t * P:(t + 1) * P], tile[:, t, :], core.ident[:, :])
    return last


def mod_stage(core, k):
    nc = core.nc
    H = 4
    KEPT = max(1, N // 2) - 1
    with ExitStack() as ctx:
        m = Mem(nc, ctx, "mod")
        names = Rows.NAMES + ["xt_done", "xT_ready", "w_done", "wcol_ready", "wide_ready", "wrow_done",
                              "hid_done", "hid_free", "out_done", "out_taken", "tri_set", "tri_chain", "rank_chain", "chain"]
        S = {n: m.sem(n) for n in names}
        rows_ = Rows(m, core, S, core.x_res)
        xT = [m.sb(f"xT{s}", [P, N]) for s in range(2)]
        wcol = [m.sb(f"wcol{s}", [P, T]) for s in range(2)]
        wide = m.sb("wide", [P, T, P])
        earlier, later = m.sb("earlier", [P, T, N], BF16), m.sb("later", [P, T, N], BF16)
        hits = m.sb("hits", [P, 2 * T, N], BF16)
        count = m.sb("count", [P, 2, T])
        rank, coef = m.sb("rank", [P, T]), m.sb("coef", [P, T])
        hid = [m.sb(f"hid{s}", [P, H, N]) for s in range(2)]
        y = m.sb("y", [P, T, D])
        upd = m.sb("upd", [P, T, D])
        six, two = m.sb("six", [P, T, 6]), m.sb("two", [P, T, 2])
        tp = m.ps("tp")
        w_ps = m.ps("w_ps")
        wrow = m.ps("wrow")
        hid_ps = [m.ps(f"hid_ps{i}") for i in range(3)]
        out_ps = [m.ps(f"out_ps{s}") for s in range(2)]
        par = lambda name: core.param(k, name)
        block = ctx.enter_context(nc.Block())

        @block.sync
        def _(sp):
            core.load_params(sp, k + 1)

        @block.gpsimd
        def _(pool):
            for n, (tri, op, sign) in enumerate(((earlier, ALU.is_gt, 1), (later, ALU.is_ge, -1))):
                pool.memset(tri[:, :, :], 1.0).then_inc(S["tri_chain"], 1)
                pool.wait_ge(S["tri_chain"], n + 1)
                pool.affine_select(out=tri[:, :, :], in_=tri[:, :, :], compare_op=op, fill=0.0, base=0,
                                   pattern=[[sign * P, T], [-sign, N]], channel_multiplier=sign).then_inc(S["tri_set"], 1)
            rows_.normalise_all(pool, core.x_stat, LN_EPS)

        @block.tensor
        def _(pe):
            pe.wait_ge(core.params_in[k], 16)

            def rows_in(b, s, first=False):
                pe.wait_ge(S["xn_ready"], b + 1)
                turn(pe, core, tp, rows_.xn[s]).then_inc(S["xt_done"], 1)
                pe.wait_ge(S["xT_ready"], b + 1)
                if not first:
                    pe.wait_ge(S["wcol_ready"], b)
                for t in range(T):
                    last = pe.matmul(w_ps[:, t:t + 1], xT[s][:, t * P:(t + 1) * P], par("mwr"), start=True, stop=True)
                last.then_inc(S["w_done"], 1)

            def spread(b):
                pe.wait_ge(S["wide_ready"], b + 1)
                turn(pe, core, wrow, wide).then_inc(S["wrow_done"], 1)

            def graph(b, s, first=False, last=False):
                ffn_tiles(pe, hid_ps, S["hid_done"], S["hid_free"], par("mw1"), xT[s][:, :], H * b, H)
                if not last:
                    rows_in(b + 1, 1 - s)
                pe.wait_ge(S["hid_free"], H * (b + 1) + 3)
                pe.wait_ge(S["out_taken"], b + 1)
                for t in range(T):
                    for n in range(H):
                        ins = pe.matmul(out_ps[s][:, t * D:(t + 1) * D], hid[s][:, n, t * P:(t + 1) * P],
                                        par("mw2")[:, n * D:(n + 1) * D], start=(n == 0), stop=(n == H - 1))
                ins.then_inc(S["out_done"], 1)
                if not last:
                    spread(b + 1)

            rows_in(0, 0, first=True)
            spread(0)
            all_graphs(pe, graph)

        @block.scalar
        def _(act):
            act.sem_inc(S["hid_free"], 3)
            act.wait_ge(core.params_in[k], 16)

            def rows_in(b, s):
                act.wait_ge(S["xt_done"], b + 1)
                act.activation(xT[s][:, :], tp[:, :], ACT.Identity).then_inc(S["xT_ready"], 1)

            def graph(b, s, first=False, last=False):
                for n in range(H):
                    act.wait_ge(S["hid_done"], H * b + n + 1)
                    act.activation(hid[s][:, n, :], hid_ps[n % 3][:, :], ACT.Gelu_apprx_tanh,
                                   bias=par("mb1")[:, n:n + 1]).then_inc(S["hid_free"], 1)
                if not last:
                    rows_in(b + 1, 1 - s)

            rows_in(0, 0)
            all_graphs(act, graph)

        @block.vector
        def _(dve):
            dve.sem_inc(S["xn_free"], 2)
            dve.wait_ge(core.params_in[k], 16)
            dve.wait_ge(S["tri_set"], 2)
            dve.sem_inc(S["out_taken"], 2)
            STEPS = T - 1 + WRITE_STEPS

            def weigh(b, s):
                dve.wait_ge(S["w_done"], b + 1)
                dve.tensor_scalar(wcol[s][:, :], w_ps[:, 0:T], par("mbr"), None, ALU.add).then_inc(S["wcol_ready"], 1)
                dve.wait_ge(S["wcol_ready"], b + 1)
                dve.tensor_copy(wide[:, :, :], wcol[s][:, :].unsqueeze(2).broadcast_to([P, T, P])).then_inc(S["wide_ready"], 1)

            def rank_tokens(b, s):
                chain = Chain(dve, S["rank_chain"], b * (2 * T + 2))
                dve.wait_ge(S["wrow_done"], b + 1)
                for t in range(T):
                    for i, (tri, op) in enumerate(((earlier, ALU.is_ge), (later, ALU.is_gt))):
                        chain.step(dve.scalar_tensor_tensor(hits[:, 2 * t + i, :], wrow[:, :], wcol[s][:, t:t + 1],
                                                            tri[:, t, :], op, ALU.mult, accum_out=count[:, i, t:t + 1]))
                chain.settle()
                chain.step(dve.tensor_tensor(rank[:, :], count[:, 0, :], count[:, 1, :], ALU.add))
                chain.settle()
                chain.step(dve.scalar_tensor_tensor(coef[:, :], rank[:, :], float(KEPT), wcol[s][:, :], ALU.is_lt, ALU.mult))
                chain.settle()

            def graph(b, s, first=False, last=False):
                rank_tokens(b, s)
                if not last:
                    weigh(b + 1, 1 - s)
                chain = Chain(dve, S["chain"], b * STEPS)
                dve.wait_ge(S["out_done"], b + 1)
                dve.tensor_tensor(y[:, :, :], out_ps[s][:, :].rearrange("p (t d) -> p t d", t=T),
                                  par("mb2").unsqueeze(1).broadcast_to([P, T, D]), ALU.add).then_inc(S["out_taken"], 1)
                dve.wait_ge(S["out_taken"], b + 1 + 2)
                for t in range(T):
                    ins = dve.scalar_tensor_tensor(y[:, t, :], y[:, t, :], coef[:, t:t + 1], rows_.xn[s][:, t, :],
                                                   ALU.mult, ALU.add)
                    if t < T - 1:
                        chain.step(ins)
                ins.then_inc(S["xn_free"], 1)
                chain.settle()
                dve.wait_ge(S["xn_free"], b + 1 + 2)
                write_x(dve, chain, core, b, y[:, :, :], core.x_res[:, b], upd, six, two)
                assert chain.n == STEPS, (chain.n, STEPS)

            weigh(0, 0)
            all_graphs(dve, graph)


def gat_stage(core, k, i):
    nc = core.nc
    with ExitStack() as ctx:
        m = Mem(nc, ctx, f"gat{i}")
        names = Rows.NAMES + ["adj_in0", "adj_in1", "adj_free", "xT_ready", "wa_done", "wa_ready", "h_done", "h_ready",
                              "t_done", "s_ready", "masked", "low_ready", "prob_ready", "prob_turned",
                              "probT_ready", "pv_done", "chain", "wide_set", "s_low", "o_taken", "max_chain", "leaky"]
        S = {n: m.sem(n) for n in names}
        rows_ = Rows(m, core, S, core.x_res)
        adj_raw = [m.sb(f"adj_raw{s}", [P, T, N], I32) for s in range(2)]
        mask = [m.sb(f"mask{s}", [P, T, N], BF16) for s in range(2)]
        xT = m.sb("xT", [P, N])
        a_wide = m.sb("a_wide", [P, P])
        wa = m.sb("wa", [P, P + 1])
        h = [m.sb(f"h{s}", [P, T, D]) for s in range(2)]
        s_col, s_low, nmax = ([m.sb(f"{n}{s}", [P, T]) for s in range(2)] for n in ("s_col", "s_low", "nmax"))
        tmax, zmax, low = (m.sb(n, [P, T]) for n in ("tmax", "zmax", "low"))
        z = [m.sb(f"z{s}", [P, T, N]) for s in range(2)]
        zlow = m.sb("zlow", [P, T, N])
        total, rinv = [m.sb(f"total{s}", [P, T]) for s in range(2)], m.sb("rinv", [P, T])
        probT = m.sb("probT", [P, T, T, P])
        y = m.sb("y", [P, T, D])
        upd = m.sb("upd", [P, T, D])
        six, two = m.sb("six", [P, T, 6]), m.sb("two", [P, T, 2])
        tp, h_ps, s_ps, o_ps = (m.ps(n) for n in ("tp", "h_ps", "s_ps", "o_ps"))
        t_ps = [m.ps(f"t_ps{s}") for s in range(2)]
        tpose = [m.ps(f"tpose{n}") for n in range(2)]
        par = lambda name: core.param(k, name)
        w, wt, a = par(f"gw{i}"), par(f"gwt{i}"), par(f"ga{i}")
        SLOPE = 0.2
        block = ctx.enter_context(nc.Block())

        @block.sync
        def _(sp):
            core.load_params(sp, k + 1)
            adj = core.dram["adj"].rearrange("b (t p) n -> b p t n", p=P)
            def fetch(b, s):
                sp.wait_ge(S["adj_free"], b + 1)
                sp.dma_start(adj_raw[s][:, :, :], adj[b]).then_inc(S[f"adj_in{s}"], 16)

            pairs(sp, fetch)

        @block.gpsimd
        def _(pool):
            def graph(half_b, b, s):
                rows_.normalise(pool, b, s)
                pool.wait_ge(S[f"adj_in{s}"], 16 * (half_b + 1))
                pool.wait_ge(S["masked"], T * (b + 1))
                apart(pool, core)
                pool.tensor_scalar(mask[s][:, :, :], adj_raw[s][:, :, :], 0.0, -BIG, ALU.is_le if i == 2 else ALU.is_equal,
                                   ALU.mult).then_inc(S["adj_free"], 1)

            pool.sem_inc(S["adj_free"], 2)
            rows_.scales(pool, core.x_stat, LN_EPS)
            with pool.Fori(0, B // 2) as j:
                for s in range(2):
                    graph(j, j * 2 + s, s)

        @block.tensor
        def _(pe):
            pe.sem_inc(S["xn_free"], 2)
            pe.sem_inc(S["pv_done"], 1)
            pe.wait_ge(core.params_in[k], 16)
            pe.wait_ge(S["wide_set"], 1)
            pe.matmul(s_ps[:, 0:P], wt, a_wide[:, :], start=True, stop=True).then_inc(S["wa_done"], 1)
            pe.matmul(t_ps[0][:, 0:1], wt, a[:, 0:1], start=True, stop=True).then_inc(S["wa_done"], 1)
            pe.wait_ge(S["wa_ready"], 2)

            def front(b, s, first=False):
                pe.wait_ge(S["xn_ready"], b + 1)
                if not first:
                    pe.wait_ge(S["xT_ready"], b)
                    pe.wait_ge(S["s_low"], b)
                    pe.wait_ge(S["h_ready"], b)
                turn(pe, core, tp, rows_.xn[s]).then_inc(S["xn_free"], 1)
                pe.wait_ge(S["xT_ready"], b + 1)
                pe.wait_ge(S["masked"], T * (b + 1))
                pe.matmul(t_ps[s][:, :], wa[:, 0:P], xT[:, :], start=True, stop=True).then_inc(S["t_done"], 1)
                for t in range(T):
                    last = pe.matmul(s_ps[:, t:t + 1], xT[:, t * P:(t + 1) * P], wa[:, P:P + 1], start=True, stop=True)
                last.then_inc(S["t_done"], 1)
                for t in range(T):
                    last = pe.matmul(h_ps[:, t * D:(t + 1) * D], xT[:, t * P:(t + 1) * P], w, start=True, stop=True)
                last.then_inc(S["h_done"], 1)

            def graph(b, s, first=False, last=False):
                if not last:
                    front(b + 1, 1 - s)
                for t in range(T):
                    pe.wait_ge(S["prob_ready"], T * b + t + 1)
                    pe.wait_ge(S["probT_ready"], T * b + t + 1)
                    for u in range(T):
                        ins = pe.transpose(tpose[t % 2][:, u * P:(u + 1) * P], z[s][:, t, u * P:(u + 1) * P],
                                           core.ident[:, :])
                    ins.then_inc(S["prob_turned"], 1)
                    if t >= 1:
                        values(b, s, t - 1)
                values(b, s, T - 1)

            def values(b, s, t):
                if t == 0:
                    pe.wait_ge(S["h_ready"], b + 1)
                    pe.wait_ge(S["o_taken"], b + 1)
                pe.wait_ge(S["probT_ready"], T * b + t + 1 + 2)
                for u in range(T):
                    last = pe.matmul(o_ps[:, t * D:(t + 1) * D], probT[:, t, u, :], h[s][:, u, :],
                                     start=(u == 0), stop=(u == T - 1))
                if t == T - 1:
                    last.then_inc(S["pv_done"], 1)

            front(0, 0, first=True)
            all_graphs(pe, graph)

        @block.scalar
        def _(act):
            act.sem_inc(S["probT_ready"], 2)
            act.wait_ge(S["wa_done"], 2)
            act.copy(wa[:, 0:P], s_ps[:, 0:P]).then_inc(S["wa_ready"], 1)
            act.copy(wa[:, P:P + 1], t_ps[0][:, 0:1]).then_inc(S["wa_ready"], 1)

            def front(b, s):
                act.wait_ge(S["xn_free"], b + 1 + 2)
                act.copy(xT[:, :], tp[:, :]).then_inc(S["xT_ready"], 1)
                act.wait_ge(S["t_done"], 2 * (b + 1))
                act.copy(s_col[s][:, :], s_ps[:, 0:T]).then_inc(S["s_ready"], 1)
                act.mul(s_low[s][:, :], s_ps[:, 0:T], SLOPE).then_inc(S["s_low"], 1)
                act.wait_ge(S["h_done"], b + 1)
                act.copy(flat(h[s][:, :, :]), h_ps[:, :]).then_inc(S["h_ready"], 1)

            def graph(b, s, first=False, last=False):
                act.wait_ge(S["s_low"], b + 1)
                for t in range(T):
                    act.wait_ge(S["masked"], T * b + t + 1 + 2 * T)
                    act.activation(zlow[:, t, :], z[s][:, t, :], ACT.Identity, bias=s_low[s][:, t:t + 1], scale=SLOPE)\
                        .then_inc(S["low_ready"], 1)
                if not last:
                    front(b + 1, 1 - s)
                for t in range(T):
                    act.wait_ge(S["leaky"], T * b + t + 1)
                    act.activation(z[s][:, t, :], z[s][:, t, :], ACT.Exp, bias=nmax[s][:, t:t + 1],
                                   accum_out=total[s][:, t:t + 1]).then_inc(S["prob_ready"], 1)
                    if t >= 1:
                        copy_probT(b, t - 1)
                copy_probT(b, T - 1)

            def copy_probT(b, t):
                act.wait_ge(S["prob_turned"], T * b + t + 1)
                if t == 0:
                    act.wait_ge(S["pv_done"], b + 1)
                act.copy(probT[:, t, :, :].rearrange("p u q -> p (u q)"), tpose[t % 2][:, :]).then_inc(S["probT_ready"], 1)

            front(0, 0)
            all_graphs(act, graph)

        @block.vector
        def _(dve):
            dve.sem_inc(S["masked"], 2 * T)
            dve.sem_inc(S["o_taken"], 1)
            dve.wait_ge(core.params_in[k], 16)
            dve.tensor_copy(a_wide[:, :], a[:, 1:2].broadcast_to([P, P])).then_inc(S["wide_set"], 1)
            STEPS = 1 + T - 1 + 1 + 2 * T + 1

            def masked(b, s):
                chain = Chain(dve, S["max_chain"], b * 3)
                dve.wait_ge(S["t_done"], 2 * b + 1)
                dve.wait_ge(S["adj_free"], b + 1 + 2)
                apart(dve, core)
                for t in range(T):
                    dve.tensor_tensor_reduce(z[s][:, t, :], t_ps[s][:, :], mask[s][:, t, :], 1.0, -3e38, ALU.add, ALU.max,
                                             tmax[:, t:t + 1]).then_inc(S["masked"], 1)
                dve.wait_ge(S["s_ready"], b + 1)
                dve.wait_ge(S["masked"], T * (b + 1) + 2 * T)
                chain.step(dve.tensor_tensor(zmax[:, :], tmax[:, :], s_col[s][:, :], ALU.add))
                chain.settle()
                chain.step(dve.scalar_tensor_tensor(low[:, :], zmax[:, :], SLOPE, zmax[:, :], ALU.mult, ALU.max))
                chain.settle()
                chain.step(dve.tensor_scalar(nmax[s][:, :], low[:, :], -1.0, None, ALU.mult))
                chain.settle()

            def out(b, s):
                chain = Chain(dve, S["chain"], b * STEPS)
                dve.wait_ge(S["prob_ready"], T * (b + 1))
                chain.step(dve.reciprocal(rinv[:, :], total[s][:, :]))
                chain.settle()
                dve.wait_ge(S["pv_done"], b + 1 + 1)
                for t in range(T):
                    ins = dve.scalar_tensor_tensor(upd[:, t, :], o_ps[:, t * D:(t + 1) * D], rinv[:, t:t + 1],
                                                   core.x_res[:, b, t, :], ALU.mult, ALU.add)
                    if t < T - 1:
                        chain.step(ins)
                ins.then_inc(S["o_taken"], 1)
                chain.settle()
                dve.wait_ge(S["o_taken"], b + 2)
                apart(dve, core)
                chain.step(dve.tensor_copy(core.x_res[:, b], upd[:, :, :]))
                row_stats(dve, chain, core, six, two, upd)
                chain.settle()
                apart(dve, core)
                chain.step(dve.tensor_copy(core.x_stat[:, b], two[:, :, :]))
                assert chain.n == STEPS, (chain.n, STEPS)

            def graph(b, s, first=False, last=False):
                for t in range(T):
                    dve.wait_ge(S["low_ready"], T * b + t + 1)
                    dve.scalar_tensor_tensor(z[s][:, t, :], z[s][:, t, :], s_col[s][:, t:t + 1], zlow[:, t, :], ALU.add,
                                             ALU.max).then_inc(S["leaky"], 1)
                if not first:
                    out(b - 1, 1 - s)
                if not last:
                    masked(b + 1, 1 - s)

            masked(0, 0)
            all_graphs(dve, graph)
            out(B - 1, 1)


E_ = 8
TOP = 2


def prep_stage(core, k, kind):
    nc = core.nc
    renorm, router = "renorm" in kind, "router" in kind
    tag = f"prep{k}"
    R = B * T
    with ExitStack() as ctx:
        m = Mem(nc, ctx, tag)
        names = Rows.NAMES + ["saved", "xt_done", "xT_ready", "logit_done", "logit_taken", "chain", "gate_chain",
                              "low_ready", "exp_ready", "tri_zero", "tri_set"]
        S = {n: m.sem(n) for n in names}
        rows_ = Rows(m, core, S, core.x_res if renorm else core.mid, shifted=renorm)
        xT = [m.sb(f"xT{s}", [P, N]) for s in range(2)]
        six, two = m.sb("six", [P, T, 6]), m.sb("two", [P, T, 2])
        tp = [m.ps(f"tp{s}") for s in range(2)]
        lg = [m.ps(f"lg{s}") for s in range(2)]
        if router:
            logits = m.sb("logits", [P, R, E_])
            prob = m.sb("prob", [P, R, E_])
            above, ties = m.sb("above", [P, R, E_, E_], BF16), m.sb("ties", [P, R, E_, E_], BF16)
            order = m.sb("order", [P, E_, E_], BF16)
            rank = m.sb("rank", [P, R, E_])
            row = [m.sb(f"row{i}", [P, R]) for i in range(5)]
            w_router = core.param(k, "er" if renorm else "hr")
        block = ctx.enter_context(nc.Block())

        @block.gpsimd
        def _(pool):
            rows_.scales(pool, core.x_stat, LN_EPS if renorm else 1e-6)
            if router:
                pool.memset(order[:, :, :], 1.0).then_inc(S["tri_zero"], 1)
                pool.wait_ge(S["tri_zero"], 1)
                pool.affine_select(out=order[:, :, :], in_=order[:, :, :], compare_op=ALU.is_gt, fill=0.0, base=0,
                                   pattern=[[1, E_], [-1, E_]], channel_multiplier=0).then_inc(S["tri_set"], 1)
            pairs(pool, lambda b, s: rows_.normalise(pool, b, s))

        @block.tensor
        def _(pe):
            if not router:
                return
            pe.wait_ge(core.params_in[k], 16)

            def graph(b, s):
                pe.wait_ge(S["xn_ready"], b + 1)
                turn(pe, core, tp[s], rows_.xn[s]).then_inc(S["xt_done"], 1)
                pe.wait_ge(S["xT_ready"], b + 1)
                pe.wait_ge(S["logit_taken"], b + 1)
                for t in range(T):
                    last = pe.matmul(lg[s][:, t * E_:(t + 1) * E_], xT[s][:, t * P:(t + 1) * P], w_router,
                                     start=True, stop=True)
                last.then_inc(S["logit_done"], 1)

            pairs(pe, graph)

        @block.scalar
        def _(act):
            act.sem_inc(S["saved"], 2)
            if router:
                act.wait_ge(core.params_in[k], 16)

            def graph(b, s):
                if renorm:
                    act.wait_ge(S["xn_ready"], b + 1)
                    act.copy(core.mid[:, b], rows_.xn[s][:, :, :]).then_inc(S["saved"], 1)
                if router:
                    act.wait_ge(S["xt_done"], b + 1)
                    if renorm:
                        ins = act.copy(xT[s][:, :], tp[s][:, :])
                    else:
                        ins = act.activation(xT[s][:, :], tp[s][:, :], ACT.Identity, scale=core.param(k, "ln2w"))
                    ins.then_inc(S["xT_ready"], 1)

            pairs(act, graph)
            if router:
                act.wait_ge(S["low_ready"], 1)
                act.activation(logits[:, :, :], logits[:, :, :], ACT.Exp).then_inc(S["exp_ready"], 1)

        @block.vector
        def _(dve):
            dve.sem_inc(S["xn_free"], 2)
            dve.sem_inc(S["logit_taken"], 2)
            if router:
                dve.wait_ge(core.params_in[k], 16)
                dve.wait_ge(S["tri_set"], 1)

            def graph(b, s):
                chain = Chain(dve, S["chain"], b * STEPS)
                if renorm:
                    dve.wait_ge(S["xn_ready"], b + 1)
                    row_stats(dve, chain, core, six, two, rows_.xn[s])
                    chain.settle()
                    apart(dve, core)
                    chain.step(dve.tensor_copy(core.stat2[:, b], two[:, :, :]))
                    dve.wait_ge(S["saved"], b + 1 + 2)
                if router:
                    dve.wait_ge(S["logit_done"], b + 1)
                    apart(dve, core)
                    out = logits[:, bass.ds(b * T, T), :]
                    got = lg[s][:, 0:T * E_].rearrange("p (t e) -> p t e", t=T)
                    if renorm:
                        ins = dve.tensor_tensor(out, got, core.param(k, "ebr").unsqueeze(1).broadcast_to([P, T, E_]), ALU.add)
                    else:
                        ins = dve.tensor_copy(out, got)
                    ins.then_inc(S["logit_taken"], 1)
                chain.settle() if chain.n else None
                dve.sem_inc(S["xn_free"], 1)

            STEPS = 2 * T + 1 if renorm else 0
            pairs(dve, graph)
            if not router:
                return
            g = Chain(dve, S["gate_chain"])
            dve.wait_ge(S["logit_taken"], B + 2)
            top, total, inv, kept, inv2 = (r[:, :] for r in row)
            wide = lambda ap: ap.unsqueeze(2).broadcast_to([P, R, E_])
            g.step(dve.tensor_reduce(top, logits[:, :, :], AX.X, ALU.max))
            g.settle()
            dve.tensor_tensor(logits[:, :, :], logits[:, :, :], wide(top), ALU.subtract).then_inc(S["low_ready"], 1)
            dve.wait_ge(S["exp_ready"], 1)
            g.step(dve.tensor_reduce(total, logits[:, :, :], AX.X, ALU.add))
            g.settle()
            g.step(dve.reciprocal(inv, total))
            g.settle()
            g.step(dve.tensor_tensor(prob[:, :, :], logits[:, :, :], wide(inv), ALU.mult))
            g.settle()
            other = prob[:, :, :].unsqueeze(2).broadcast_to([P, R, E_, E_])
            own = prob[:, :, :].unsqueeze(3).broadcast_to([P, R, E_, E_])
            g.step(dve.tensor_tensor(above[:, :, :, :], other, own, ALU.is_gt))
            g.step(dve.tensor_tensor(ties[:, :, :, :], other, own, ALU.is_ge))
            g.settle()
            g.step(dve.tensor_tensor(ties[:, :, :, :], ties[:, :, :, :],
                                     order[:, :, :].unsqueeze(1).broadcast_to([P, R, E_, E_]), ALU.mult))
            g.settle()
            g.step(dve.tensor_tensor(above[:, :, :, :], above[:, :, :, :], ties[:, :, :, :], ALU.max))
            g.settle()
            g.step(dve.tensor_reduce(rank[:, :, :], above[:, :, :, :], AX.X, ALU.add))
            g.settle()
            g.step(dve.scalar_tensor_tensor(prob[:, :, :], rank[:, :, :], float(TOP), prob[:, :, :], ALU.is_lt, ALU.mult))
            g.settle()
            g.step(dve.tensor_reduce(kept, prob[:, :, :], AX.X, ALU.add))
            g.settle()
            if not renorm:
                g.step(dve.tensor_scalar(kept, kept, 1e-9, None, ALU.add))
                g.settle()
            g.step(dve.reciprocal(inv2, kept))
            g.settle()
            g.step(dve.tensor_tensor(core.gate[:, :, :, :].rearrange("p b t e -> p (b t) e"), prob[:, :, :], wide(inv2), ALU.mult))
            g.settle()


def moe_stage(core, k, swiglu, store=False):
    nc = core.nc
    if swiglu:
        FULL = 341
        WID = [P, P, FULL - 2 * P]
    else:
        FULL = 512
        WID = [P] * 4
    HT = len(WID)
    with ExitStack() as ctx:
        m = Mem(nc, ctx, f"moe{k}")
        names = Rows.NAMES + ["xT_ready", "hid_done", "hid_read", "out_done", "combined", "gate_ready", "b1_done",
                              "w1_ready", "b1_ready", "gT_done", "gT_ready", "bias_done", "chain", "x_chain", "silu_ready",
                              "acc_init", "stored"]
        S = {n: m.sem(n) for n in names}
        rows_ = Rows(m, core, S, core.mid, shifted=not swiglu)
        xT = [m.sb(f"xT{s}", [P, N]) for s in range(2)]
        hid = [m.sb(f"hid{s}", [P, HT, N]) for s in range(2)]
        gates = [m.sb(f"gate{s}", [P, T, E_]) for s in range(2)]
        acc = [m.sb(f"acc{s}", [P, T, D]) for s in range(2)]
        upd = m.sb("upd", [P, T, D])
        six, two = m.sb("six", [P, T, 6]), m.sb("two", [P, T, 2])
        tp, gb = m.ps("tp"), m.ps("gb")
        hid_ps = [m.ps(f"hid_ps{i}") for i in range(4)]
        out_ps = [m.ps(f"out_ps{s}") for s in range(2)]
        par = lambda name: core.param(k, name)
        if swiglu:
            silu = [m.sb(f"silu{i}", [P, N]) for i in range(2)]
        else:
            b1 = m.sb("b1", [P, E_ * HT])
            gT = m.sb("gT", [E_, N])
        PAIRS = 2 if swiglu else 4
        block = ctx.enter_context(nc.Block())

        @block.sync
        def _(sp):
            core.load_params(sp, k + 1)
            if store:
                with sp.Fori(0, B) as b:
                    sp.wait_ge(S["x_chain"], b + 1)
                    sp.dma_start(core.dram["out"][b].rearrange("(t p) d -> p t d", p=P), core.x_res[:, b])\
                        .then_inc(S["stored"], 16)
                sp.wait_ge(S["stored"], 16 * B)

        @block.gpsimd
        def _(pool):
            rows_.normalise_all(pool, core.x_stat if swiglu else core.stat2, 1e-6 if swiglu else LN_EPS)

        @block.tensor
        def _(pe):
            pe.sem_inc(S["xn_free"], 2)
            pe.wait_ge(core.params_in[k], 16)
            if not swiglu:
                for e in range(E_):
                    for n in range(HT):
                        last = pe.matmul(gb[:, e * HT + n:e * HT + n + 1], par("ew1")[:, e * FULL + n * P:e * FULL + (n + 1) * P],
                                         par("ebt")[:, e:e + 1], start=True, stop=True)
                last.then_inc(S["b1_done"], 1)

            def front(b, s):
                pe.wait_ge(S["xn_ready"], b + 1)
                turn(pe, core, tp, rows_.xn[s]).then_inc(S["xn_free"], 1)

            def hidden(b, s, e):
                if e == 0:
                    pe.wait_ge(S["xT_ready"], b + 1)
                for n, wid in enumerate(WID):
                    i = e * HT + n
                    pe.wait_ge(S["hid_read"], E_ * HT * b + i + 1)
                    col = e * FULL + n * P
                    if swiglu:
                        pe.matmul(hid_ps[2 * (i % 2)][0:wid, :], par("hw1")[:, col:col + wid], xT[s][:, :], start=True, stop=True)\
                            .then_inc(S["hid_done"], 1)
                        pe.matmul(hid_ps[2 * (i % 2) + 1][0:wid, :], par("hw3")[:, col:col + wid], xT[s][:, :], start=True, stop=True)\
                            .then_inc(S["hid_done"], 1)
                    else:
                        pe.matmul(hid_ps[i % 4][:, :], par("ew1")[:, col:col + wid], xT[s][:, :], start=True, stop=True)\
                            .then_inc(S["hid_done"], 1)

            def output(b, e):
                pe.wait_ge(S["combined"], E_ * b + e + 1)
                pe.wait_ge(S["hid_read"], HT * (E_ * b + e + 1) + PAIRS)
                w2 = par("hw2" if swiglu else "ew2")
                for t in range(T):
                    for n, wid in enumerate(WID):
                        last = pe.matmul(out_ps[e % 2][:, t * D:(t + 1) * D], hid[e % 2][0:wid, n, t * P:(t + 1) * P],
                                         w2[0:wid, (e * HT + n) * D:(e * HT + n + 1) * D], start=(n == 0), stop=(n == HT - 1))
                last.then_inc(S["out_done"], 1)

            def graph(b, s, last=False):
                for e in range(E_):
                    if e == 0 and not swiglu:
                        pe.wait_ge(S["gate_ready"], b + 1)
                        for t in range(T):
                            ins = pe.transpose(tp[0:E_, t * P:(t + 1) * P], gates[s][:, t, :], core.ident[:, :])
                        ins.then_inc(S["gT_done"], 1)
                    if e < E_ - 1:
                        hidden(b, s, e + 1)
                    elif not last:
                        hidden(b + 1, 1 - s, 0)
                    if e == 0 and not swiglu:
                        pe.wait_ge(S["gT_ready"], b + 1)
                        for t in range(T):
                            ins = pe.matmul(gb[:, t * D:(t + 1) * D], gT[:, t * P:(t + 1) * P], par("eb2")[0:E_, :],
                                            start=True, stop=True)
                        ins.then_inc(S["bias_done"], 1)
                    if e == 3 and not last:
                        front(b + 1, 1 - s)
                    output(b, e)

            front(0, 0)
            if not swiglu:
                pe.wait_ge(S["w1_ready"], E_)
            hidden(0, 0, 0)
            pairs(pe, graph, 0, B - 2)
            graph(B - 2, 0)
            graph(B - 1, 1, last=True)

        @block.scalar
        def _(act):
            act.wait_ge(core.params_in[k], 16)
            if not swiglu:
                act.sem_inc(S["hid_read"], PAIRS)
                act.wait_ge(S["b1_ready"], 1)

            def front(b, s):
                act.wait_ge(S["xn_free"], b + 1 + 2)
                if swiglu:
                    ins = act.activation(xT[s][:, :], tp[:, :], ACT.Identity, scale=par("ln2w"))
                else:
                    ins = act.copy(xT[s][:, :], tp[:, :])
                ins.then_inc(S["xT_ready"], 1)

            def hidden(b, e):
                for n, wid in enumerate(WID):
                    i = e * HT + n
                    if swiglu:
                        act.wait_ge(S["hid_done"], 2 * (E_ * HT * b + i) + 1)
                        act.activation(silu[i % 2][0:wid, :], hid_ps[2 * (i % 2)][0:wid, :], ACT.Silu).then_inc(S["silu_ready"], 1)
                    else:
                        act.wait_ge(S["hid_done"], E_ * HT * b + i + 1)
                        act.activation(hid[e % 2][:, n, :], hid_ps[i % 4][:, :], ACT.Gelu, bias=b1[:, i:i + 1])\
                            .then_inc(S["hid_read"], 1)

            def graph(b, s, last=False):
                for e in range(E_):
                    if e == 0 and not swiglu:
                        act.wait_ge(S["gT_done"], b + 1)
                        act.copy(gT[:, :], tp[0:E_, :]).then_inc(S["gT_ready"], 1)
                    if e < E_ - 1:
                        hidden(b, e + 1)
                    elif not last:
                        hidden(b + 1, 0)
                    if e == 3 and not last:
                        front(b + 1, 1 - s)

            front(0, 0)
            hidden(0, 0)
            pairs(act, graph, 0, B - 2)
            graph(B - 2, 0)
            graph(B - 1, 1, last=True)

        @block.vector
        def _(dve):
            dve.sem_inc(S["combined"], 2)
            dve.wait_ge(core.params_in[k], 16)
            if swiglu:
                dve.sem_inc(S["hid_read"], PAIRS)
            else:
                dve.wait_ge(S["b1_done"], 1)
                dve.tensor_tensor(b1[:, :], gb[:, 0:E_ * HT], par("eb1"), ALU.add).then_inc(S["b1_ready"], 1)
                for e in range(E_):
                    w1 = par("ew1")[:, e * FULL:(e + 1) * FULL]
                    dve.tensor_scalar(w1, w1, par("eg")[:, e:e + 1], None, ALU.mult).then_inc(S["w1_ready"], 1)

            def product(b, e):
                for n, wid in enumerate(WID):
                    i = e * HT + n
                    dve.wait_ge(S["silu_ready"], E_ * HT * b + i + 1)
                    dve.wait_ge(S["hid_done"], 2 * (E_ * HT * b + i) + 2)
                    dve.tensor_tensor(hid[e % 2][0:wid, n, :], hid_ps[2 * (i % 2) + 1][0:wid, :], silu[i % 2][0:wid, :],
                                      ALU.mult).then_inc(S["hid_read"], 1)

            def take_gate(b, s):
                dve.tensor_copy(gates[s][:, :, :], core.gate[:, b]).then_inc(S["gate_ready"], 1)

            def graph(b, s, last=False):
                chain = Chain(dve, S["chain"], b * STEPS)
                gate = gates[s]
                dve.wait_ge(S["gate_ready"], b + 1)
                if not swiglu:
                    dve.wait_ge(S["bias_done"], b + 1)
                    dve.tensor_copy(flat(acc[s][:, :, :]), gb[:, :]).then_inc(S["acc_init"], 1)
                    dve.wait_ge(S["acc_init"], b + 1)
                for e in range(E_):
                    if swiglu:
                        if e < E_ - 1:
                            product(b, e + 1)
                        elif not last:
                            product(b + 1, 0)
                    dve.wait_ge(S["out_done"], E_ * b + e + 1)
                    for t in range(T):
                        before = core.mid[:, b, t, :] if e == 0 and swiglu else acc[s][:, t, :]
                        ins = dve.scalar_tensor_tensor(acc[s][:, t, :], out_ps[e % 2][:, t * D:(t + 1) * D], gate[:, t, e:e + 1],
                                                       before, ALU.mult, ALU.add)
                        if t < T - 1:
                            chain.step(ins)
                    ins.then_inc(S["combined"], 1)
                    if e == 3 and not last:
                        take_gate(b + 1, 1 - s)
                    chain.settle()
                    dve.wait_ge(S["combined"], E_ * b + e + 1 + 2)
                if store:
                    dve.tensor_tensor(core.x_res[:, b], acc[s][:, :, :], core.x_res[:, b], ALU.add).then_inc(S["x_chain"], 1)
                    dve.wait_ge(S["x_chain"], b + 1)
                else:
                    write_x(dve, chain, core, b, acc[s][:, :, :], core.x_res[:, b], upd, six, two)
                assert chain.n == STEPS, (chain.n, STEPS)

            STEPS = E_ * (T - 1) + (0 if store else WRITE_STEPS)
            take_gate(0, 0)
            if swiglu:
                product(0, 0)
            pairs(dve, graph, 0, B - 2)
            graph(B - 2, 0)
            graph(B - 1, 1, last=True)


def program(core):
    load_stage(core)
    mha_stage(core, 0, "mha0", 8, 16, 2, 0.25, core.x_res)
    lstm_stage(core, 1)
    mha_stage(core, 2, "mha1", 8, 16, 2, 0.25, core.mid, sym=True, from_xn=True)
    ffn1_stage(core, 3)
    mod_stage(core, 4)
    gat_stage(core, 5, 2)
    prep_stage(core, 6, "renorm+router")
    moe_stage(core, 6, False)
    gat_stage(core, 7, 3)
    prep_stage(core, 8, "renorm")
    mha_stage(core, 8, "mha3", 4, 32, 1, 32 ** -0.5, core.mid, rope=True)
    prep_stage(core, 9, "router")
    moe_stage(core, 9, True, store=True)


def columns(a):
    out = np.zeros((P, a.shape[1]), np.float32)
    out[:a.shape[0]] = a
    return out


def rows(v):
    return np.broadcast_to(v.reshape(1, -1), (P, v.size))


def head_columns(w, heads, dim, groups):
    out = np.zeros((P, groups, 4, 32), np.float32)
    out[..., :dim] = w.T.reshape(P, groups, 4, dim)
    return out.reshape(P, groups * P)


def head_bias(v, dim, groups):
    out = np.zeros((4, 32, groups), np.float32)
    out[:, :dim] = v.reshape(groups, 4, dim).transpose(1, 2, 0)
    return out.reshape(P, groups)


def hidden_rows(w):
    return w.reshape(-1, P, w.shape[1]).transpose(1, 0, 2).reshape(P, -1)


def half_turned(w):
    return w.reshape(P, 4, 2, 16)[:, :, ::-1].reshape(P, P)


def rope_tables():
    inv_freq = 1.0 / 10000.0 ** (np.arange(0, 32, 2, dtype=np.float32) / 32)
    freqs = np.outer(np.arange(N, dtype=np.float32), inv_freq)
    cos, sin = np.cos(freqs).T.astype(np.float32), np.sin(freqs).T.astype(np.float32)
    return np.tile(np.concatenate([cos, cos]), (4, 1)), np.tile(np.concatenate([-sin, sin]), (4, 1))


def pack(a):
    w = {}
    qkv, bqkv = a["L1_gnn_Wqkv"], a["L1_gnn_bqkv"]
    for tag, ws, bs, wo, bo in (
        ("0", [a["L0_gnn_W" + c] for c in "qkv"], [a["L0_gnn_b" + c] for c in "qkv"], a["L0_gnn_Wo"], a["L0_gnn_bo"]),
        ("1", [qkv[i * D:(i + 1) * D] for i in range(3)], [bqkv[i * D:(i + 1) * D] for i in range(3)], a["L1_gnn_Wo"], a["L1_gnn_bo"]),
    ):
        w["wq" + tag], w["wk" + tag] = (head_columns(x, 8, 16, 2) for x in ws[:2])
        w["bq" + tag], w["bk" + tag] = (head_bias(x, 16, 2) for x in bs[:2])
        w["wv" + tag], w["bv" + tag], w["wo" + tag], w["bo" + tag] = ws[2].T, rows(bs[2]), wo.T, rows(bo)
    w["w_ih"], w["w_hh"] = a["L0_ffn_W_ih"].T, a["L0_ffn_W_hh"].T
    w["b_ih"], w["b_hh"] = a["L0_ffn_b_ih"].reshape(4, P).T, a["L0_ffn_b_hh"].reshape(4, P).T
    w["w_lin"] = np.repeat(a["L0_ffn_W_lin"].T, P, axis=1)
    w["b_lin"] = rows(a["L0_ffn_b_lin"])
    w["fw"], w["bw"] = a["L0_ffn_fw_att"].T, a["L0_ffn_bw_att"].T
    w["f1w1"] = a["L1_gnn_W1"].T
    w["f1w2"] = hidden_rows(a["L1_gnn_W2"].T)
    w["f1b1"] = a["L1_gnn_b1"].reshape(4, P).T
    w["f1b2"], w["g1"], w["be1"], w["g2"], w["be2"] = (rows(a["L1_gnn_" + n]) for n in ("b2", "ln1_g", "ln1_b", "ln2_g", "ln2_b"))
    w["mw1"], w["mw2"], w["mb1"] = a["L1_ffn_w1"], hidden_rows(a["L1_ffn_w2"]), a["L1_ffn_b1"].reshape(4, P).T
    w["mb2"], w["mwr"], w["mbr"] = rows(a["L1_ffn_b2"]), a["L1_ffn_wr"], rows(a["L1_ffn_br"])
    w["gw2"], w["gwt2"], w["ga2"] = a["L2_gnn_W"], a["L2_gnn_W"].T, a["L2_gnn_a"].reshape(2, P).T
    w["gw3"], w["gwt3"], w["ga3"] = a["L3_gnn_W"].T, a["L3_gnn_W"], a["L3_gnn_a"].reshape(2, P).T
    w["ew1"] = a["L2_ffn_W1"].transpose(1, 0, 2).reshape(D, -1)
    w["ew2"] = hidden_rows(a["L2_ffn_W2"].reshape(-1, D))
    w["eb1"] = a["L2_ffn_b1"].reshape(-1, P).T
    w["eb2"] = columns(a["L2_ffn_b2"])
    w["eg"], w["ebt"], w["er"], w["ebr"] = a["L2_ffn_ln_g"].T, a["L2_ffn_ln_b"].T, a["L2_ffn_Wr"], rows(a["L2_ffn_br"])
    w["wq3"], w["wqr3"] = a["L3_ffn_wq"].T, half_turned(a["L3_ffn_wq"].T)
    both = lambda v: np.repeat(v.T.reshape(P, 2, 32), 2, axis=1).reshape(P, P)
    w["wk3"], w["wkr3"], w["wv3"] = both(a["L3_ffn_wk"]), half_turned(both(a["L3_ffn_wk"])), both(a["L3_ffn_wv"])
    w["wo3"], w["ln1w"], w["ln2w"] = a["L3_ffn_wo"].T, a["L3_ffn_ln1_w"].reshape(P, 1), a["L3_ffn_ln2_w"].reshape(P, 1)
    w["cos"], w["sin"] = rope_tables()
    w["hw1"] = a["L3_ffn_w1"].transpose(2, 0, 1).reshape(D, -1)
    w["hw3"] = a["L3_ffn_w3"].transpose(2, 0, 1).reshape(D, -1)
    padded = np.zeros((8, 3 * P, D), np.float32)
    padded[:, :341] = a["L3_ffn_w2"].transpose(0, 2, 1)
    w["hw2"] = hidden_rows(padded.reshape(-1, D))
    w["hr"] = a["L3_ffn_router_w"].T
    out = np.zeros((P, COLUMNS), np.float32)
    for name, (at, n) in PLACE.items():
        out[:, at:at + n] = w[name]
    return out


def kernel(**inputs):
    import concourse.bacc as _bacc
    from concourse.bass_utils import run_bass_kernel_spmd as _run

    a = {name: np.asarray(v) for name, v in inputs.items()}
    sent = {"x": np.ascontiguousarray(a["x"]), "adj": np.ascontiguousarray(a["adj"]), "weights": pack(a)}
    nc = _bacc.Bacc("TRN2", target_bir_lowering=False, num_devices=1)
    dram = {n: nc.dram_tensor(n, v.shape, mybir.dt.from_np(v.dtype), kind="ExternalInput").ap() for n, v in sent.items()}
    dram["out"] = nc.dram_tensor("out", (B, N, D), F32, kind="ExternalOutput").ap()
    with ExitStack() as ctx:
        program(Core(nc, ctx, dram))
    r = _run(nc, [sent], core_ids=[0])
    return r.results[0]["out"]
```
